# Optimizing a Trainium2 kernel written in Bass

```python
import numpy as np
import jax
import jax.numpy as jnp

def _softmax(x, axis=-1):
    return jax.nn.softmax(x, axis=axis)

def _gelu(x):
    return jax.nn.gelu(x, approximate=True)

def _silu(x):
    return jax.nn.silu(x)

def _sigmoid(x):
    return jax.nn.sigmoid(x)

def _layernorm(x, axis=-1, eps=1e-05):
    m = jnp.mean(x, axis=axis, keepdims=True)
    v = jnp.var(x, axis=axis, keepdims=True)
    return (x - m) / jnp.sqrt(v + eps)

def _scatter_add(tgt, idx, src, axis=0):
    return tgt.at[idx].add(src)

def _segment_sum(src, seg, n):
    return jax.ops.segment_sum(src, seg, n)
kernel_name = 'mk_metaformer_d2_conv_nhwc384_r4_db607d'

def setup_inputs(seed: int=0):
    np.random.seed(seed)
    _w = jnp.asarray

    def _rec_inputs():
        import jax
        import jax.numpy as jnp
        _gk = jax.random.key(seed)
        x = -0.0002221 + 1 * jax.random.normal(jax.random.fold_in(_gk, 1), (16, 16, 16, 96), jnp.float32)
        return x
    x = _rec_inputs()

    def _L0_conv_setup():
        import jax, jax.numpy as jnp
        import numpy as np
        import math
        WS = (8, 8)
        SHIFT = (4, 4)
        HEADS = 12
        C_DIM = 96

        def _rel_position_bias(cpb_w1, cpb_b1, cpb_w2):
            ws0, ws1 = WS
            ch = jnp.arange(-(ws0 - 1), ws0, dtype=jnp.float32)
            cw = jnp.arange(-(ws1 - 1), ws1, dtype=jnp.float32)
            table = jnp.stack(jnp.meshgrid(ch, cw, indexing='ij'), axis=-1)
            table = table / jnp.array([ws0 - 1, ws1 - 1], jnp.float32) * 8.0
            table = jnp.sign(table) * jnp.log2(jnp.abs(table) + 1.0) / 3.0
            h = jax.nn.relu(table @ cpb_w1.T + cpb_b1)
            bias_table = (h @ cpb_w2.T).reshape(-1, HEADS)
            coords = np.stack(np.meshgrid(np.arange(ws0), np.arange(ws1), indexing='ij'))
            coords = coords.reshape(2, -1)
            rel = (coords[:, :, None] - coords[:, None, :]).transpose(1, 2, 0)
            rel[..., 0] += ws0 - 1
            rel[..., 1] += ws1 - 1
            rel[..., 0] *= 2 * ws1 - 1
            idx = jnp.asarray(rel.sum(-1))
            bias = bias_table[idx]
            bias = jnp.transpose(bias, (2, 0, 1))
            return 16.0 * jax.nn.sigmoid(bias)

        def _shift_attn_mask(pad_H, pad_W):
            ws0, ws1 = WS
            s0, s1 = SHIFT
            m = np.zeros((pad_H, pad_W), dtype=np.float32)
            cnt = 0
            h_slices = ((0, pad_H - ws0), (pad_H - ws0, pad_H - s0), (pad_H - s0, pad_H))
            w_slices = ((0, pad_W - ws1), (pad_W - ws1, pad_W - s1), (pad_W - s1, pad_W))
            for h0, h1 in h_slices:
                for w0, w1 in w_slices:
                    m[h0:h1, w0:w1] = cnt
                    cnt += 1
            m = m.reshape(pad_H // ws0, ws0, pad_W // ws1, ws1)
            m = m.transpose(0, 2, 1, 3).reshape(-1, ws0 * ws1)
            diff = m[:, None, :] - m[:, :, None]
            mask = np.where(diff != 0, -100.0, 0.0).astype(np.float32)
            return jnp.asarray(mask)
        key = jax.random.key(seed)
        ks = jax.random.split(key, 7)
        C = C_DIM
        x = jax.random.normal(ks[0], (16, 16, 16, C), jnp.float32)
        qkv_w = jax.random.normal(ks[1], (3 * C, C), jnp.float32) * 0.02
        qkv_b = jax.random.normal(ks[2], (3 * C,), jnp.float32) * 0.02
        proj_w = jax.random.normal(ks[3], (C, C), jnp.float32) * 0.02
        proj_b = jax.random.normal(ks[4], (C,), jnp.float32) * 0.02
        logit_scale = jnp.full((HEADS, 1, 1), math.log(10.0), jnp.float32)
        cpb_w1 = jax.random.normal(ks[5], (128, 2), jnp.float32) * 0.02
        cpb_b1 = jnp.zeros((128,), jnp.float32)
        cpb_w2 = jax.random.normal(ks[6], (HEADS, 128), jnp.float32) * 0.02
        return {'x': x, 'qkv_w': qkv_w, 'qkv_b': qkv_b, 'proj_w': proj_w, 'proj_b': proj_b, 'logit_scale': logit_scale, 'cpb_w1': cpb_w1, 'cpb_b1': cpb_b1, 'cpb_w2': cpb_w2}
    _L0_conv_all = _L0_conv_setup()
    _L0_conv_in = {k: v for k, v in _L0_conv_all.items() if k in ('qkv_w', 'qkv_b', 'proj_w', 'proj_b', 'logit_scale', 'cpb_w1', 'cpb_b1', 'cpb_w2')}
    del _L0_conv_all

    def _L0_ffn_setup():
        import jax, jax.numpy as jnp
        import numpy as np
        NUM_GROUPS = 5
        EPS = 1e-05
        QB = 128.0

        def _binarize_weights_groupwise(W):
            n_out = W.shape[0]
            gs = n_out // NUM_GROUPS
            Wb = jnp.zeros_like(W)
            for g in range(NUM_GROUPS):
                wg = W[g * gs:(g + 1) * gs]
                z = wg - wg.mean()
                ste = z + jax.lax.stop_gradient(jnp.sign(z) - z)
                Wb = Wb.at[g * gs:(g + 1) * gs].set(ste)
            return Wb

        def _quantize_activations_groupwise(x):
            n = x.shape[0]
            gs = n // NUM_GROUPS
            xq = jnp.zeros_like(x)
            for g in range(NUM_GROUPS):
                ag = x[g * gs:(g + 1) * gs]
                gamma = jnp.max(jnp.abs(ag))
                xq = xq.at[g * gs:(g + 1) * gs].set(jnp.clip(ag * QB / (gamma + EPS), -QB + EPS, QB - EPS))
            return xq

        def _bitlinear(x, W, b):
            Wb = _binarize_weights_groupwise(W)
            y = jnp.einsum('btc,oc->bto', x, Wb) + b
            return _quantize_activations_groupwise(y)
        key = jax.random.key(seed)
        k1, k2, k3, k4, k5 = jax.random.split(key, 5)
        B, T, C = (10, 512, 96)
        H = 4 * C
        lim1 = 1.0 / np.sqrt(C)
        lim2 = 1.0 / np.sqrt(H)
        x = jax.random.normal(k1, (B, T, C), dtype=jnp.float32)
        W1 = jax.random.uniform(k2, (H, C), minval=-lim1, maxval=lim1, dtype=jnp.float32)
        b1 = jax.random.uniform(k3, (H,), minval=-lim1, maxval=lim1, dtype=jnp.float32)
        W2 = jax.random.uniform(k4, (C, H), minval=-lim2, maxval=lim2, dtype=jnp.float32)
        b2 = jax.random.uniform(k5, (C,), minval=-lim2, maxval=lim2, dtype=jnp.float32)
        return {'x': x, 'W1': W1, 'b1': b1, 'W2': W2, 'b2': b2}
    _L0_ffn_all = _L0_ffn_setup()
    _L0_ffn_in = {k: v for k, v in _L0_ffn_all.items() if k in ('W1', 'b1', 'W2', 'b2')}
    del _L0_ffn_all

    def _L1_conv_setup():
        import jax, jax.numpy as jnp
        import numpy as np
        from jax import lax
        B, H, W = (8, 32, 32)
        NC = 96
        GROUPS = 6
        HEADS = 12
        HC = NC // HEADS
        GC = NC // GROUPS
        KK = 3
        LN_EPS = 0.001

        def _bilinear_sample_zero(img, warp):
            N, Hh, Ww, C = img.shape
            img = jnp.pad(img, ((0, 0), (1, 1), (1, 1), (0, 0)))
            Hp, Wp = (Hh + 2, Ww + 2)
            wxy = warp + 1.0
            xq = wxy[..., 0]
            yq = wxy[..., 1]
            y0 = jnp.clip(jnp.floor(yq), 0.0, Hp - 2)
            x0 = jnp.clip(jnp.floor(xq), 0.0, Wp - 2)
            ay = jnp.clip(yq - y0, 0.0, 1.0)[..., None]
            ax = jnp.clip(xq - x0, 0.0, 1.0)[..., None]
            y0i = y0.astype(jnp.int32)
            x0i = x0.astype(jnp.int32)
            flat = img.reshape(N * Hp * Wp, C)
            boff = (jnp.arange(N, dtype=jnp.int32) * (Hp * Wp))[:, None]

            def gather(yi, xi):
                return flat[boff + yi * Wp + xi]
            tl = gather(y0i, x0i)
            tr = gather(y0i, x0i + 1)
            bl = gather(y0i + 1, x0i)
            br = gather(y0i + 1, x0i + 1)
            top = tl + ax * (tr - tl)
            bot = bl + ax * (br - bl)
            return top + ay * (bot - top)

        def _forward(x, w_q, b_q, w_off0, b_off0, ln_g, ln_b, w_offp, w_k, b_k, w_v, b_v, w_o, b_o):
            Bq, Hh, Ww, C = x.shape
            n_sample = Hh * Ww
            q = x @ w_q + b_q
            t = lax.conv_general_dilated(q, w_off0, (1, 1), 'SAME', dimension_numbers=('NHWC', 'HWIO', 'NHWC'), feature_group_count=GROUPS) + b_off0
            mu = jnp.mean(t, axis=-1, keepdims=True)
            var = jnp.mean(jnp.square(t - mu), axis=-1, keepdims=True)
            t = (t - mu) / jnp.sqrt(var + LN_EPS) * ln_g + ln_b
            t = jax.nn.gelu(t, approximate=False)
            t = t.reshape(Bq, Hh, Ww, GROUPS, GC).transpose(0, 3, 1, 2, 4)
            t = t.reshape(Bq * GROUPS, Hh, Ww, GC)
            offset = t @ w_offp
            offset_range = jnp.array([Hh / 2.0, Ww / 2.0], dtype=x.dtype)
            offset = jnp.tanh(offset) * offset_range
            ry, rx = jnp.meshgrid(jnp.arange(Hh, dtype=x.dtype), jnp.arange(Ww, dtype=x.dtype), indexing='xy')
            ref = jnp.stack((ry, rx), -1).reshape(1, Hh, Ww, 2)
            pos = offset + ref
            xg = x.reshape(Bq, Hh, Ww, GROUPS, GC).transpose(0, 3, 1, 2, 4)
            xg = xg.reshape(Bq * GROUPS, Hh, Ww, GC)
            warp = jnp.stack([pos[..., 1], pos[..., 0]], axis=-1).reshape(Bq * GROUPS, n_sample, 2)
            xs = _bilinear_sample_zero(xg, warp)
            xs = xs.reshape(Bq, GROUPS, n_sample, GC).transpose(0, 2, 1, 3).reshape(Bq, n_sample, C)
            k = xs @ w_k + b_k
            v = xs @ w_v + b_v
            qh = q.reshape(Bq, n_sample, HEADS, HC)
            kh = k.reshape(Bq, n_sample, HEADS, HC)
            vh = v.reshape(Bq, n_sample, HEADS, HC)
            scale = jnp.asarray(HC, x.dtype) ** (-0.5)
            attn = jnp.einsum('bmhc,bnhc->bhmn', qh, kh) * scale
            attn = jax.nn.softmax(attn, axis=-1)
            out = jnp.einsum('bhmn,bnhc->bmhc', attn, vh).reshape(Bq, Hh, Ww, C)
            y = out @ w_o + b_o
            return y
        key = jax.random.key(seed)
        ks = jax.random.split(key, 8)
        f = jnp.float32
        s = 0.02
        return {'x': jax.random.normal(ks[0], (B, H, W, NC), f), 'w_q': jax.random.normal(ks[1], (NC, NC), f) * s, 'b_q': jnp.zeros((NC,), f), 'w_off0': jax.random.normal(ks[2], (KK, KK, GC, NC), f) * s, 'b_off0': jnp.zeros((NC,), f), 'ln_g': jnp.ones((NC,), f), 'ln_b': jnp.zeros((NC,), f), 'w_offp': jax.random.normal(ks[3], (GC, 2), f) * s, 'w_k': jax.random.normal(ks[4], (NC, NC), f) * s, 'b_k': jnp.zeros((NC,), f), 'w_v': jax.random.normal(ks[5], (NC, NC), f) * s, 'b_v': jnp.zeros((NC,), f), 'w_o': jax.random.normal(ks[6], (NC, NC), f) * s, 'b_o': jnp.zeros((NC,), f)}
    _L1_conv_all = _L1_conv_setup()
    _L1_conv_in = {k: v for k, v in _L1_conv_all.items() if k in ('w_q', 'b_q', 'w_off0', 'b_off0', 'ln_g', 'ln_b', 'w_offp', 'w_k', 'b_k', 'w_v', 'b_v', 'w_o', 'b_o')}
    del _L1_conv_all

    def _L1_ffn_setup():
        import jax, jax.numpy as jnp
        import numpy as np
        NUM_EXPERTS = 4
        TOP_K = 2
        DIM = 96
        HID = 4 * DIM
        key = jax.random.key(seed)
        ks = jax.random.split(key, 5)
        B, S = (16, 512)
        scale_in = 1.0 / np.sqrt(DIM)
        scale_hid = 1.0 / np.sqrt(HID)
        return {'x': jax.random.normal(ks[0], (B, S, DIM), dtype=jnp.float32), 'gate_w': jax.random.normal(ks[1], (DIM, NUM_EXPERTS), dtype=jnp.float32) * scale_in, 'gate_b': jnp.zeros((NUM_EXPERTS,), dtype=jnp.float32), 'w1': jax.random.normal(ks[2], (NUM_EXPERTS, DIM, HID), dtype=jnp.float32) * scale_in, 'b1': jnp.zeros((NUM_EXPERTS, HID), dtype=jnp.float32), 'w2': jax.random.normal(ks[3], (NUM_EXPERTS, HID, DIM), dtype=jnp.float32) * scale_hid, 'b2': jnp.zeros((NUM_EXPERTS, DIM), dtype=jnp.float32)}
    _L1_ffn_all = _L1_ffn_setup()
    _L1_ffn_in = {k: v for k, v in _L1_ffn_all.items() if k in ('gate_w', 'gate_b', 'w1', 'b1', 'w2', 'b2')}
    del _L1_ffn_all
    return {'x': x, 'L0_conv_qkv_w': _L0_conv_in['qkv_w'], 'L0_conv_qkv_b': _L0_conv_in['qkv_b'], 'L0_conv_proj_w': _L0_conv_in['proj_w'], 'L0_conv_proj_b': _L0_conv_in['proj_b'], 'L0_conv_logit_scale': _L0_conv_in['logit_scale'], 'L0_conv_cpb_w1': _L0_conv_in['cpb_w1'], 'L0_conv_cpb_b1': _L0_conv_in['cpb_b1'], 'L0_conv_cpb_w2': _L0_conv_in['cpb_w2'], 'L0_ffn_W1': _L0_ffn_in['W1'], 'L0_ffn_b1': _L0_ffn_in['b1'], 'L0_ffn_W2': _L0_ffn_in['W2'], 'L0_ffn_b2': _L0_ffn_in['b2'], 'L1_conv_w_q': _L1_conv_in['w_q'], 'L1_conv_b_q': _L1_conv_in['b_q'], 'L1_conv_w_off0': _L1_conv_in['w_off0'], 'L1_conv_b_off0': _L1_conv_in['b_off0'], 'L1_conv_ln_g': _L1_conv_in['ln_g'], 'L1_conv_ln_b': _L1_conv_in['ln_b'], 'L1_conv_w_offp': _L1_conv_in['w_offp'], 'L1_conv_w_k': _L1_conv_in['w_k'], 'L1_conv_b_k': _L1_conv_in['b_k'], 'L1_conv_w_v': _L1_conv_in['w_v'], 'L1_conv_b_v': _L1_conv_in['b_v'], 'L1_conv_w_o': _L1_conv_in['w_o'], 'L1_conv_b_o': _L1_conv_in['b_o'], 'L1_ffn_gate_w': _L1_ffn_in['gate_w'], 'L1_ffn_gate_b': _L1_ffn_in['gate_b'], 'L1_ffn_w1': _L1_ffn_in['w1'], 'L1_ffn_b1': _L1_ffn_in['b1'], 'L1_ffn_w2': _L1_ffn_in['w2'], 'L1_ffn_b2': _L1_ffn_in['b2']}

def reference(x, L0_conv_qkv_w, L0_conv_qkv_b, L0_conv_proj_w, L0_conv_proj_b, L0_conv_logit_scale, L0_conv_cpb_w1, L0_conv_cpb_b1, L0_conv_cpb_w2, L0_ffn_W1, L0_ffn_b1, L0_ffn_W2, L0_ffn_b2, L1_conv_w_q, L1_conv_b_q, L1_conv_w_off0, L1_conv_b_off0, L1_conv_ln_g, L1_conv_ln_b, L1_conv_w_offp, L1_conv_w_k, L1_conv_b_k, L1_conv_w_v, L1_conv_b_v, L1_conv_w_o, L1_conv_b_o, L1_ffn_gate_w, L1_ffn_gate_b, L1_ffn_w1, L1_ffn_b1, L1_ffn_w2, L1_ffn_b2):
    import jax
    import jax.numpy as jnp

    def _L0_conv_ref(x, qkv_w, qkv_b, proj_w, proj_b, logit_scale, cpb_w1, cpb_b1, cpb_w2):
        import jax, jax.numpy as jnp
        import numpy as np
        import math
        WS = (8, 8)
        SHIFT = (4, 4)
        HEADS = 12
        C_DIM = 96

        def _rel_position_bias(cpb_w1, cpb_b1, cpb_w2):
            ws0, ws1 = WS
            ch = jnp.arange(-(ws0 - 1), ws0, dtype=jnp.float32)
            cw = jnp.arange(-(ws1 - 1), ws1, dtype=jnp.float32)
            table = jnp.stack(jnp.meshgrid(ch, cw, indexing='ij'), axis=-1)
            table = table / jnp.array([ws0 - 1, ws1 - 1], jnp.float32) * 8.0
            table = jnp.sign(table) * jnp.log2(jnp.abs(table) + 1.0) / 3.0
            h = jax.nn.relu(table @ cpb_w1.T + cpb_b1)
            bias_table = (h @ cpb_w2.T).reshape(-1, HEADS)
            coords = np.stack(np.meshgrid(np.arange(ws0), np.arange(ws1), indexing='ij'))
            coords = coords.reshape(2, -1)
            rel = (coords[:, :, None] - coords[:, None, :]).transpose(1, 2, 0)
            rel[..., 0] += ws0 - 1
            rel[..., 1] += ws1 - 1
            rel[..., 0] *= 2 * ws1 - 1
            idx = jnp.asarray(rel.sum(-1))
            bias = bias_table[idx]
            bias = jnp.transpose(bias, (2, 0, 1))
            return 16.0 * jax.nn.sigmoid(bias)

        def _shift_attn_mask(pad_H, pad_W):
            ws0, ws1 = WS
            s0, s1 = SHIFT
            m = np.zeros((pad_H, pad_W), dtype=np.float32)
            cnt = 0
            h_slices = ((0, pad_H - ws0), (pad_H - ws0, pad_H - s0), (pad_H - s0, pad_H))
            w_slices = ((0, pad_W - ws1), (pad_W - ws1, pad_W - s1), (pad_W - s1, pad_W))
            for h0, h1 in h_slices:
                for w0, w1 in w_slices:
                    m[h0:h1, w0:w1] = cnt
                    cnt += 1
            m = m.reshape(pad_H // ws0, ws0, pad_W // ws1, ws1)
            m = m.transpose(0, 2, 1, 3).reshape(-1, ws0 * ws1)
            diff = m[:, None, :] - m[:, :, None]
            mask = np.where(diff != 0, -100.0, 0.0).astype(np.float32)
            return jnp.asarray(mask)
        B, H, W, C = x.shape
        ws0, ws1 = WS
        s0, s1 = SHIFT
        L = ws0 * ws1
        hd = C // HEADS
        bias = _rel_position_bias(cpb_w1, cpb_b1, cpb_w2)
        xr = jnp.roll(x, (-s0, -s1), axis=(1, 2))
        nWh, nWw = (H // ws0, W // ws1)
        nW = nWh * nWw
        xw = xr.reshape(B, nWh, ws0, nWw, ws1, C).transpose(0, 1, 3, 2, 4, 5)
        xw = xw.reshape(B * nW, L, C)
        qb = qkv_b.at[C:2 * C].set(0.0)
        qkv = xw @ qkv_w.T + qb
        qkv = qkv.reshape(B * nW, L, 3, HEADS, hd).transpose(2, 0, 3, 1, 4)
        q, k, v = (qkv[0], qkv[1], qkv[2])
        qn = q / jnp.maximum(jnp.linalg.norm(q, axis=-1, keepdims=True), 1e-12)
        kn = k / jnp.maximum(jnp.linalg.norm(k, axis=-1, keepdims=True), 1e-12)
        scale = jnp.exp(jnp.minimum(logit_scale, math.log(100.0)))
        attn = jnp.einsum('whid,whjd->whij', qn, kn) * scale + bias
        mask = _shift_attn_mask(H, W)
        attn = attn.reshape(B, nW, HEADS, L, L) + mask[None, :, None]
        attn = jax.nn.softmax(attn.reshape(B * nW, HEADS, L, L), axis=-1)
        out = jnp.einsum('whij,whjd->whid', attn, v)
        out = out.transpose(0, 2, 1, 3).reshape(B * nW, L, C)
        out = out @ proj_w.T + proj_b
        out = out.reshape(B, nWh, nWw, ws0, ws1, C).transpose(0, 1, 3, 2, 4, 5)
        out = out.reshape(B, H, W, C)
        out = jnp.roll(out, (s0, s1), axis=(1, 2))
        return out

    def _L0_ffn_ref(x, W1, b1, W2, b2):
        import jax, jax.numpy as jnp
        import numpy as np
        NUM_GROUPS = 5
        EPS = 1e-05
        QB = 128.0

        def _binarize_weights_groupwise(W):
            n_out = W.shape[0]
            gs = n_out // NUM_GROUPS
            Wb = jnp.zeros_like(W)
            for g in range(NUM_GROUPS):
                wg = W[g * gs:(g + 1) * gs]
                z = wg - wg.mean()
                ste = z + jax.lax.stop_gradient(jnp.sign(z) - z)
                Wb = Wb.at[g * gs:(g + 1) * gs].set(ste)
            return Wb

        def _quantize_activations_groupwise(x):
            n = x.shape[0]
            gs = n // NUM_GROUPS
            xq = jnp.zeros_like(x)
            for g in range(NUM_GROUPS):
                ag = x[g * gs:(g + 1) * gs]
                gamma = jnp.max(jnp.abs(ag))
                xq = xq.at[g * gs:(g + 1) * gs].set(jnp.clip(ag * QB / (gamma + EPS), -QB + EPS, QB - EPS))
            return xq

        def _bitlinear(x, W, b):
            Wb = _binarize_weights_groupwise(W)
            y = jnp.einsum('btc,oc->bto', x, Wb) + b
            return _quantize_activations_groupwise(y)
        h = _bitlinear(x, W1, b1)
        h = jax.nn.gelu(h, approximate=False)
        out = _bitlinear(h, W2, b2)
        return out

    def _L1_conv_ref(x, w_q, b_q, w_off0, b_off0, ln_g, ln_b, w_offp, w_k, b_k, w_v, b_v, w_o, b_o):
        import jax, jax.numpy as jnp
        import numpy as np
        from jax import lax
        B, H, W = (8, 32, 32)
        NC = 96
        GROUPS = 6
        HEADS = 12
        HC = NC // HEADS
        GC = NC // GROUPS
        KK = 3
        LN_EPS = 0.001

        def _bilinear_sample_zero(img, warp):
            N, Hh, Ww, C = img.shape
            img = jnp.pad(img, ((0, 0), (1, 1), (1, 1), (0, 0)))
            Hp, Wp = (Hh + 2, Ww + 2)
            wxy = warp + 1.0
            xq = wxy[..., 0]
            yq = wxy[..., 1]
            y0 = jnp.clip(jnp.floor(yq), 0.0, Hp - 2)
            x0 = jnp.clip(jnp.floor(xq), 0.0, Wp - 2)
            ay = jnp.clip(yq - y0, 0.0, 1.0)[..., None]
            ax = jnp.clip(xq - x0, 0.0, 1.0)[..., None]
            y0i = y0.astype(jnp.int32)
            x0i = x0.astype(jnp.int32)
            flat = img.reshape(N * Hp * Wp, C)
            boff = (jnp.arange(N, dtype=jnp.int32) * (Hp * Wp))[:, None]

            def gather(yi, xi):
                return flat[boff + yi * Wp + xi]
            tl = gather(y0i, x0i)
            tr = gather(y0i, x0i + 1)
            bl = gather(y0i + 1, x0i)
            br = gather(y0i + 1, x0i + 1)
            top = tl + ax * (tr - tl)
            bot = bl + ax * (br - bl)
            return top + ay * (bot - top)

        def _forward(x, w_q, b_q, w_off0, b_off0, ln_g, ln_b, w_offp, w_k, b_k, w_v, b_v, w_o, b_o):
            Bq, Hh, Ww, C = x.shape
            n_sample = Hh * Ww
            q = x @ w_q + b_q
            t = lax.conv_general_dilated(q, w_off0, (1, 1), 'SAME', dimension_numbers=('NHWC', 'HWIO', 'NHWC'), feature_group_count=GROUPS) + b_off0
            mu = jnp.mean(t, axis=-1, keepdims=True)
            var = jnp.mean(jnp.square(t - mu), axis=-1, keepdims=True)
            t = (t - mu) / jnp.sqrt(var + LN_EPS) * ln_g + ln_b
            t = jax.nn.gelu(t, approximate=False)
            t = t.reshape(Bq, Hh, Ww, GROUPS, GC).transpose(0, 3, 1, 2, 4)
            t = t.reshape(Bq * GROUPS, Hh, Ww, GC)
            offset = t @ w_offp
            offset_range = jnp.array([Hh / 2.0, Ww / 2.0], dtype=x.dtype)
            offset = jnp.tanh(offset) * offset_range
            ry, rx = jnp.meshgrid(jnp.arange(Hh, dtype=x.dtype), jnp.arange(Ww, dtype=x.dtype), indexing='xy')
            ref = jnp.stack((ry, rx), -1).reshape(1, Hh, Ww, 2)
            pos = offset + ref
            xg = x.reshape(Bq, Hh, Ww, GROUPS, GC).transpose(0, 3, 1, 2, 4)
            xg = xg.reshape(Bq * GROUPS, Hh, Ww, GC)
            warp = jnp.stack([pos[..., 1], pos[..., 0]], axis=-1).reshape(Bq * GROUPS, n_sample, 2)
            xs = _bilinear_sample_zero(xg, warp)
            xs = xs.reshape(Bq, GROUPS, n_sample, GC).transpose(0, 2, 1, 3).reshape(Bq, n_sample, C)
            k = xs @ w_k + b_k
            v = xs @ w_v + b_v
            qh = q.reshape(Bq, n_sample, HEADS, HC)
            kh = k.reshape(Bq, n_sample, HEADS, HC)
            vh = v.reshape(Bq, n_sample, HEADS, HC)
            scale = jnp.asarray(HC, x.dtype) ** (-0.5)
            attn = jnp.einsum('bmhc,bnhc->bhmn', qh, kh) * scale
            attn = jax.nn.softmax(attn, axis=-1)
            out = jnp.einsum('bhmn,bnhc->bmhc', attn, vh).reshape(Bq, Hh, Ww, C)
            y = out @ w_o + b_o
            return y
        return _forward(x, w_q, b_q, w_off0, b_off0, ln_g, ln_b, w_offp, w_k, b_k, w_v, b_v, w_o, b_o)

    def _L1_ffn_ref(x, gate_w, gate_b, w1, b1, w2, b2):
        import jax, jax.numpy as jnp
        import numpy as np
        NUM_EXPERTS = 4
        TOP_K = 2
        DIM = 96
        HID = 4 * DIM
        scores = jnp.einsum('bsd,de->bse', x, gate_w) + gate_b
        probs = jax.nn.softmax(scores, axis=-1)
        topk_vals, topk_idx = jax.lax.top_k(probs, TOP_K)
        mask = jnp.sum(jax.nn.one_hot(topk_idx, NUM_EXPERTS, dtype=probs.dtype), axis=-2)
        masked = probs * mask
        masked = masked / (jnp.sum(masked, axis=-1, keepdims=True) + 1e-09)
        h = jax.nn.gelu(jnp.einsum('bsd,edh->ebsh', x, w1) + b1[:, None, None, :], approximate=False)
        y = jnp.einsum('ebsh,ehd->ebsd', h, w2) + b2[:, None, None, :]
        out = jnp.einsum('bse,ebsd->bsd', masked, y)
        return out

    def _gn(v, G=32, eps=1e-05):
        B_, H_, W_, C_ = v.shape
        g = v.reshape(B_, H_, W_, G, C_ // G)
        m = jnp.mean(g, axis=(1, 2, 4), keepdims=True)
        s = jnp.var(g, axis=(1, 2, 4), keepdims=True)
        return ((g - m) / jnp.sqrt(s + eps)).reshape(v.shape)

    def _ln_c(v, eps=1e-06):
        m = jnp.mean(v, axis=-1, keepdims=True)
        s = jnp.var(v, axis=-1, keepdims=True)
        return (v - m) / jnp.sqrt(s + eps)

    def _ln_t(v, eps=1e-05):
        m = jnp.mean(v, axis=-1, keepdims=True)
        s = jnp.var(v, axis=-1, keepdims=True)
        return (v - m) / jnp.sqrt(s + eps)

    def _to_tokens(v):
        B_, H_, W_, C_ = v.shape
        return v.reshape(B_, H_ * W_, C_)

    def _from_tokens(t, like):
        return t.reshape(like.shape)
    x = x + _L0_conv_ref(_ln_c(x), L0_conv_qkv_w, L0_conv_qkv_b, L0_conv_proj_w, L0_conv_proj_b, L0_conv_logit_scale, L0_conv_cpb_w1, L0_conv_cpb_b1, L0_conv_cpb_w2)
    t = _to_tokens(x)
    t = t + _L0_ffn_ref(_ln_t(t), L0_ffn_W1, L0_ffn_b1, L0_ffn_W2, L0_ffn_b2)
    x = _from_tokens(t, x)
    x = x + _L1_conv_ref(_ln_c(x), L1_conv_w_q, L1_conv_b_q, L1_conv_w_off0, L1_conv_b_off0, L1_conv_ln_g, L1_conv_ln_b, L1_conv_w_offp, L1_conv_w_k, L1_conv_b_k, L1_conv_w_v, L1_conv_b_v, L1_conv_w_o, L1_conv_b_o)
    t = _to_tokens(x)
    t = t + _L1_ffn_ref(_ln_t(t), L1_ffn_gate_w, L1_ffn_gate_b, L1_ffn_w1, L1_ffn_b1, L1_ffn_w2, L1_ffn_b2)
    x = _from_tokens(t, x)
    return x

_drawn_inputs = setup_inputs


def setup_inputs(seed=0):
    import zlib

    import numpy as np

    out = dict(_drawn_inputs(seed))
    spreads = {'L0_conv_logit_scale': (2.3025851249694824, 0.6),
     'L0_conv_cpb_b1': (0.0, 2.0),
     'L1_conv_b_q': (0.0, 2.0),
     'L1_conv_b_off0': (0.0, 2.0),
     'L1_conv_ln_g': (1.0, 0.6),
     'L1_conv_ln_b': (0.0, 2.0),
     'L1_conv_b_k': (0.0, 2.0),
     'L1_conv_b_v': (0.0, 0.8),
     'L1_conv_b_o': (0.0, 0.8),
     'L1_ffn_gate_b': (0.0, 0.8),
     'L1_ffn_b1': (0.0, 0.8),
     'L1_ffn_b2': (0.0, 2.0)}
    factors = {'L0_conv_qkv_b': 7.642,
     'L0_conv_proj_b': 2.79,
     'L0_conv_cpb_w1': 200.0,
     'L0_conv_cpb_w2': 200.0,
     'L0_ffn_b1': 8.0,
     'L0_ffn_b2': 200.0,
     'L1_conv_w_q': 8.0,
     'L1_conv_w_off0': 22.446,
     'L1_conv_w_offp': 8.0,
     'L1_conv_w_k': 8.0,
     'L1_conv_w_v': 8.0,
     'L1_conv_w_o': 8.0,
     'L1_ffn_gate_w': 3.353,
     'L1_ffn_w1': 3.583,
     'L1_ffn_w2': 3.061}
    for name, (base, spread) in spreads.items():
        noise = np.random.default_rng([zlib.crc32(name.encode()), seed]).standard_normal(out[name].shape)
        drawn = base * np.exp(spread * noise) if base else spread * noise
        out[name] = jnp.asarray(drawn.astype(out[name].dtype))
    for name, factor in factors.items():
        out[name] = (out[name] * factor).astype(out[name].dtype)
    return out
```

```python
from contextlib import ExitStack

import concourse.bass as bass
from concourse import mybir

F32 = mybir.dt.float32
BF16 = mybir.dt.bfloat16
ALU = mybir.AluOpType
ACT = mybir.ActivationFunctionType
AX = mybir.AxisListType
RMAX = bass.bass_isa.ReduceOp.max

P = 128
IMAGES = 16
SIDE = 16
TOK = SIDE * SIDE
TILES = TOK // P
C = 96
HEADS = 12
HD = C // HEADS
PAIRS = HEADS // 2
SLOT = 64
SPLIT = 6 * HD
MASKROWS = 5
MAXCOL = SPLIT + MASKROWS
FULL = MAXCOL + 3
WIN = 64
HID = 4 * C
MT = HID // P
GROUPS = 5
GIMG = IMAGES // GROUPS
QIMG = GROUPS * GIMG
EPSQ = 1e-5
QB = 128.0
LIM = QB - EPSQ
DG = 6
GC = C // DG
EXPERTS = 4
REL = 15 * 15
SHIFT = 4


def build_program(nc, A, out):
    ctx = ExitStack()
    with ctx:
        def sb(name, shape, dt=F32):
            return ctx.enter_context(nc.sbuf_tensor(name, shape, dt))

        ident = sb("ident", [P, P])
        identb = sb("identb", [P, P], BF16)
        perm_in = sb("perm_in", [P, P])
        perm_out = sb("perm_out", [P, P])
        flip = sb("flip", [WIN, P])
        mask_q = sb("mask_q", [P, TILES, MASKROWS])
        mask_k = sb("mask_k", [P, TILES, MASKROWS])
        table = sb("table", [2, REL])
        cpb_w1 = sb("cpb_w1", [2, P])
        cpb_b1 = sb("cpb_b1", [P, 1])
        cpb_w2 = sb("cpb_w2", [P, HEADS])
        lscale = sb("lscale", [P, HEADS])
        wqkv = sb("wqkv", [C + 1, 3 * C])
        wproj = sb("wproj", [C + 1, C])
        w1 = sb("w1", [C, HID])
        w1s = sb("w1s", [C, HID])
        b1 = sb("b1", [P, MT])
        w2 = sb("w2", [P, MT, C])
        w2s = sb("w2s", [P, MT, C])
        b2 = sb("b2", [C, 1])
        wq = sb("wq", [C + 1, C])
        wconv = sb("wconv", [C, 9, C])
        boff = sb("boff", [1, C])
        lng = sb("lng", [P, C])
        lnb = sb("lnb", [P, C])
        woffp = sb("woffp", [C, 2, C])
        posc = sb("posc", [C, 2, TOK])
        wkv = sb("wkv", [C + 1, 2 * C])
        wo = sb("wo", [C + 1, C])
        wg = sb("wg", [C + 1, EXPERTS])
        we1 = sb("we1", [C + 1, EXPERTS, HID])
        we2 = sb("we2", [P, EXPERTS, MT, C])
        be2 = sb("be2", [1, EXPERTS * C])
        tri = sb("tri", [P, EXPERTS, EXPERTS])
        loads = [(ident, "ident"), (perm_in, "perm_in"), (perm_out, "perm_out"), (flip, "flip"),
                 (mask_q, "mask_q"), (mask_k, "mask_k"), (table, "table"), (cpb_w1, "cpb_w1"),
                 (cpb_b1, "cpb_b1"), (cpb_w2, "cpb_w2"), (lscale, "lscale"), (wqkv, "wqkv"),
                 (wproj, "wproj"), (w1, "w1"), (b1, "b1"), (w2, "w2"), (b2, "b2"), (wq, "wq"),
                 (wconv, "wconv"), (boff, "boff"), (lng, "lng"), (lnb, "lnb"), (woffp, "woffp"),
                 (posc, "posc"), (wkv, "wkv"), (wo, "wo"), (wg, "wg"), (we1, "we1"), (we2, "we2"),
                 (be2, "be2"), (tri, "tri")]
        onesm = sb("onesm", [P, P])
        neghalf = sb("neghalf", [P, 2 * TILES * HEADS])
        zero1 = sb("zero1", [P, 1])
        hid_t = sb("hid_t", [P, REL])
        bt_sb = sb("bt_sb", [HEADS, REL])
        ebraw = sb("ebraw", [WIN, HEADS, WIN])
        ebz = sb("ebz", [P, HEADS, WIN])
        expbias = sb("expbias", [P, 2, PAIRS, WIN])
        wsum = sb("wsum", [P, GROUPS])
        wmean = sb("wmean", [P, 2, GROUPS])
        y1all = sb("y1all", [P, IMAGES, MT, TOK])
        y2all = sb("y2all", [C, IMAGES, TOK])
        gm1 = sb("gm1", [P, IMAGES])
        gm2 = sb("gm2", [P, IMAGES])
        gg = sb("gg", [P, 2, GROUPS])
        ggall = sb("ggall", [P, 2, GROUPS])
        gs = sb("gs", [P, 2, GROUPS])
        qs1 = sb("qs1", [P, IMAGES])
        qs2 = sb("qs2", [P, IMAGES])
        xin = sb("xin", [P, TILES, C])
        xres = sb("xres", [P, TILES, C])
        stats = sb("stats", [P, TILES, 6])
        mv = sb("mv", [P, TILES, 2])
        veps = sb("veps", [P, TILES])
        rstd = sb("rstd", [P, TILES])
        xn = sb("xn", [P, TILES, C])
        xnt = sb("xnt", [C + 1, TOK])
        sq = sb("sq", [P, TILES, 2 * HEADS, HD])
        ss = sb("ss", [P, TILES, 2 * HEADS])
        rn = sb("rn", [P, TILES, 2 * HEADS])
        qk = sb("qk", [P, TILES, 2, HEADS, HD])
        res = sb("res", [P, TILES, 2, HEADS, HD])
        stack = sb("stack", [P, TILES, 2, HEADS, SLOT], BF16)
        stackt = sb("stackt", [P, 2, PAIRS, TOK], BF16)
        va = sb("va", [P, TILES, HEADS, 32])
        nm = sb("nm", [P, TILES, 2, PAIRS])
        nmr = sb("nmr", [P, TILES, 2, PAIRS])
        prob = sb("prob", [P, 2, 2, 2, TOK])
        ot = sb("ot", [P, 3, TOK])
        rec = sb("rec", [P, TILES, HEADS])
        on = sb("on", [P, TILES, C])
        ont = sb("ont", [C + 1, TOK])
        hb = sb("hb", [P, 2, MT, TOK])
        ycl = sb("ycl", [C, TOK])
        qpad = sb("qpad", [C, 3, SIDE + 2, SIDE])
        tn = sb("tn", [P, TILES, C])
        tnt = sb("tnt", [C, TOK])
        th = sb("th", [C, 2, TOK])
        hat = sb("hat", [C, 2, TOK])
        hatx = sb("hatx", [P, TILES, DG, SIDE])
        rows = sb("rows", [C, DG, SIDE, GC])
        samp = sb("samp", [P, 2, 2 * SIDE, GC])
        xs = sb("xs", [P, TILES, C])
        sc = sb("sc", [P, TILES, EXPERTS])
        scm = sb("scm", [P, TILES])
        scs = sb("scs", [P, TILES])
        gt = sb("gt", [P, TILES, EXPERTS, EXPERTS])
        eq = sb("eq", [P, TILES, EXPERTS, EXPERTS])
        acc = sb("acc", [P, TILES, C])

        ps = ctx.enter_context(nc.psum_tensor("ps", [P, 8, 512], F32))

        def bank_bf(b):
            return ps[:, b, 0:384].bitcast(BF16).rearrange("p (a c) -> p a c", c=P)

        x1_dram = nc.dram_tensor("x1_scratch", [IMAGES * TOK, C], F32).ap()
        xn_dram = nc.dram_tensor("xn_scratch", [TOK, C], F32).ap()
        bt_dram = nc.dram_tensor("bt_scratch", [HEADS, REL], F32).ap()

        class Signal:

            def __init__(self, name, n):
                self.sem = ctx.enter_context(nc.semaphore(name))
                self.n = n

            def at(self, i, k):
                return i * self.n + k

        made = {}

        def signals(prefix, **counts):
            for k, n in counts.items():
                made[prefix + k] = Signal(prefix + k, n)
            return {k: made[prefix + k] for k in counts}

        weights_in = ctx.enter_context(nc.semaphore("weights_in"))
        bt_dma = ctx.enter_context(nc.semaphore("bt_dma"))
        setup_dve = ctx.enter_context(nc.semaphore("setup_dve"))
        setup_pool = ctx.enter_context(nc.semaphore("setup_pool"))
        setup_pe = ctx.enter_context(nc.semaphore("setup_pe"))
        setup_act = ctx.enter_context(nc.semaphore("setup_act"))
        gam = [ctx.enter_context(nc.semaphore(f"gamma{n}")) for n in range(2)]
        gam_all = [ctx.enter_context(nc.semaphore(f"gamma_all{n}")) for n in range(2)]
        gam_ready = [ctx.enter_context(nc.semaphore(f"gamma_ready{n}")) for n in range(2)]
        dve_own = ctx.enter_context(nc.semaphore("dve_own"))
        pool_own = ctx.enter_context(nc.semaphore("pool_own"))
        act_own = ctx.enter_context(nc.semaphore("act_own"))

        SA = signals("a_", x_in=48, var=2, rstd=2, xn=2, xt=2, xnt=2, qkv=2, sq=2, v=2, ss=2, rn=2,
                     qk=2, stack=1, qt=2, kt=2, qt_sb=2, kt_sb=2, s=2, nm=2, q2t=2, q2t_sb=2,
                     st=2, exp=2, prob=2, pv=2, ot=2, otr=2, on=2, ontp=2, ont=2, proj=2,
                     x1=2, x1_out=48, var2=2, rstd2=2, xn2=2, x2t=2, x2t_sb=2, y1=1, y1_sb=1,
                     gm=1)
        SB = signals("b_", cl=1, h=1, y2=1, y2_sb=1, gm=1)
        SC = signals("c_", x_in=16, ycl=1, yt=2, var=2, rstd=2, xn=2, xn_out=16, rows_in=16 * DG,
                     xt=2, xnt=2, q=2, qc=1, qpad=1, q_sb=2, conv=2, cvar=2, crstd=2, cn=1,
                     cg=1, tt=2, tnt=2, offs=1, tanh=1, hat=1, hxt=1, hatx=1, t3=2, mul=6, xs=2,
                     xst=2, xst_sb=2, kv=2, k_sb=2, v=2, stack=1, qt=2, kt=2, qt_sb=2, kt_sb=2,
                     s=6, nm=6, parts=1, q2t=2, q2t_sb=2, st=6, exp=6, pv=6, ot=3, otr=2, on=2,
                     ontp=2, ont=2, proj=2, x3=2, var3=2, rstd3=2, xn3=2, x3t=2, x3t_sb=2, gate=2,
                     gsub=1, gexp=1, h1=4, h=4, y=2, acc=2, out=32)

        owner = {}
        for k in ("x_in", "x1_out"):
            owner["a_" + k] = "sp"
        for k in ("x_in", "xn_out", "rows_in", "out"):
            owner["c_" + k] = "sp"
        for k in ("var", "xn", "ss", "qk", "nm", "on", "x1", "var2", "xn2", "gm"):
            owner["a_" + k] = "dve"
        for k in ("cl", "gm"):
            owner["b_" + k] = "dve"
        for k in ("ycl", "var", "xn", "cvar", "cn", "hat", "mul", "xs", "nm", "parts", "on", "x3",
                  "var3", "xn3", "gsub", "acc"):
            owner["c_" + k] = "dve"
        for k in ("rstd", "rn", "stack", "prob", "rstd2"):
            owner["a_" + k] = "pool"
        for k in ("rstd", "crstd", "stack", "rstd3"):
            owner["c_" + k] = "pool"
        for k in ("xnt", "sq", "v", "qt_sb", "kt_sb", "q2t_sb", "exp", "ot", "ont", "x2t_sb", "y1_sb"):
            owner["a_" + k] = "act"
        for k in ("h", "y2_sb"):
            owner["b_" + k] = "act"
        for k in ("xnt", "qpad", "q_sb", "cg", "tnt", "tanh", "hatx", "xst_sb", "k_sb", "v", "qt_sb",
                  "kt_sb", "q2t_sb", "exp", "ot", "ont", "x3t_sb", "gexp", "h"):
            owner["c_" + k] = "act"

        def prime(eng, who):
            for k, s in made.items():
                if owner.get(k, "pe") == who:
                    eng.sem_inc(s.sem, s.n)

        class Own:

            def __init__(self, eng, sem):
                self.eng, self.sem, self.n = eng, sem, 0
                eng.sem_clear(sem)

            def mark(self, ins):
                ins.then_inc(self.sem, 1)
                self.n += 1
                return self.n

            def wait(self, n):
                self.eng.wait_ge(self.sem, n)

            def link(self, ins):
                self.wait(self.mark(ins))

        def plain(eng):
            eng.wait_ge(weights_in, 16 * len(loads))

        block = ctx.enter_context(nc.Block())
        ASETUP = 8

        @block.sync
        def _(sp):
            prime(sp, "sp")
            for t, name in loads:
                sp.dma_start(t[:], A[name]).then_inc(weights_in, 16)
            sp.wait_ge(setup_act, 2)
            sp.dma_start(bt_dram, bt_sb[:, :]).then_inc(bt_dma, 16)
            sp.wait_ge(bt_dma, 16)
            for rj in range(8):
                for cj in range(8):
                    src = bt_dram.rearrange("h (r c) -> h r c", c=15)[:, rj:rj + 8, cj:cj + 8]
                    sp.dma_start(ebraw[rj * 8 + cj:rj * 8 + cj + 1, :, :], src).then_inc(bt_dma, 16)
            with sp.Fori(1, IMAGES + 1) as i:
                W = lambda s, k: sp.wait_ge(SA[s].sem, SA[s].at(i, k))
                base = (i - 1) * TOK
                plain(sp)
                W("x1", 0)
                cut = TOK - SHIFT * SIDE - P
                x = A["x"]
                sp.dma_start(xin[:, 0, :], x[bass.ds(base + SHIFT * SIDE, P), :]).then_inc(SA["x_in"].sem, 16)
                sp.dma_start(xin[0:cut, 1, :], x[bass.ds(base + SHIFT * SIDE + P, cut), :]).then_inc(SA["x_in"].sem, 16)
                sp.dma_start(xin[cut:P, 1, :], x[bass.ds(base, P - cut), :]).then_inc(SA["x_in"].sem, 16)
                plain(sp)
                W("x1", 2)
                o = x1_dram
                sp.dma_start(o[bass.ds(base + SHIFT * SIDE, P), :], xres[:, 0, :]).then_inc(SA["x1_out"].sem, 16)
                sp.dma_start(o[bass.ds(base + SHIFT * SIDE + P, cut), :], xres[0:cut, 1, :]).then_inc(SA["x1_out"].sem, 16)
                sp.dma_start(o[bass.ds(base, P - cut), :], xres[cut:P, 1, :]).then_inc(SA["x1_out"].sem, 16)
            sp.wait_ge(SA["x1_out"].sem, (IMAGES + 1) * 48)
            sp.wait_ge(gam_ready[1], 1)
            with sp.Fori(1, IMAGES + 1) as i:
                W = lambda s, k: sp.wait_ge(SC[s].sem, SC[s].at(i, k))
                base = (i - 1) * TOK
                plain(sp)
                W("acc", 0)
                sp.dma_start(xin[:, :, :], x1_dram[bass.ds(base, TOK), :].rearrange("(t p) c -> p t c", p=P)).then_inc(SC["x_in"].sem, 16)
                W("xn", 2)
                sp.dma_start(xn_dram.rearrange("(t p) c -> p t c", p=P), xn[:, :, :]).then_inc(SC["xn_out"].sem, 16)
                W("xn_out", 16)
                for g in range(DG):
                    src = xn_dram.rearrange("(r c) (g k) -> r c g k", c=SIDE, g=DG)[:, :, g, :]
                    sp.dma_start(rows[GC * g:GC * g + SIDE, g, :, :], src).then_inc(SC["rows_in"].sem, 16)
                for t in range(TILES):
                    plain(sp)
                    W("acc", t + 1)
                    sp.dma_start(out[bass.ds(base + t * P, P), :], acc[:, t, :]).then_inc(SC["out"].sem, 16)
            sp.wait_ge(SC["out"].sem, (IMAGES + 1) * 32)

        def split_stack(W, own, ready, i):
            def blk(qk_, b, n=1, step=1):
                v = stack[:, :, qk_, :, :] if qk_ is not None else stack[:, :, :, :, :]
                return v, b
            pool = nc.gpsimd
            src = qk[:, :, :, :, :].rearrange("p t a h c -> p (t a h) c")
            st = stack[:, :, :, :, :].rearrange("p t a h c -> p (t a h) c")
            rs = res[:, :, :, :, :].rearrange("p t a h c -> p (t a h) c")
            own.link(pool.tensor_copy(st[:, :, 0:HD], src))
            own.link(pool.tensor_tensor(rs, src, st[:, :, 0:HD], ALU.subtract))
            own.link(pool.tensor_copy(st[:, :, HD:2 * HD], rs))
            for t in range(TILES):
                q, k = stack[:, t, 0], stack[:, t, 1]
                ops = [(q, 2, None), (k, 5, None), (q, 3, 0), (q, 5, 0), (q, 4, 1), (k, 2, 0), (k, 4, 0), (k, 3, 1)]
                for n, (d, b, frm) in enumerate(ops):
                    dst = d[:, :, HD * b:HD * b + HD]
                    if frm is None:
                        a = 0 if d is q else 1
                        own.mark(pool.tensor_tensor(dst, res[:, t, a], d[:, :, HD:2 * HD], ALU.subtract))
                    else:
                        last = pool.tensor_copy(dst, d[:, :, HD * frm:HD * frm + HD])
                        if not (t == TILES - 1 and n == len(ops) - 1):
                            own.mark(last)
            own.wait(own.n)
            last.then_inc(ready, 1)

        @block.gpsimd
        def _(pool):
            g = nc.gpsimd
            prime(pool, "pool")
            n = 0

            def setup(ins):
                ins.then_inc(setup_pool, 1)

            setup(g.memset(onesm[:], 1.0))
            setup(g.memset(neghalf[:], -0.5))
            setup(g.memset(zero1[:], 0.0))
            setup(g.memset(stack[:], 0.0))
            setup(g.memset(va[:], 0.0))
            setup(g.memset(rows[:], 0.0))
            setup(g.memset(qpad[:], 0.0))
            setup(g.memset(y2all[:], 0.0))
            pool.wait_ge(weights_in, 16 * len(loads))
            pool.wait_ge(setup_pool, 8)
            for t in range(TILES):
                for a, m in ((0, mask_q), (1, mask_k)):
                    setup(g.tensor_copy(stack[:, t, a, :, SPLIT:MAXCOL],
                                        m[:, t:t + 1, :].to_broadcast([P, HEADS, MASKROWS])))
            g.memset(stack[:, :, 1, :, MAXCOL:FULL].rearrange("p t h c -> p t h c"), 1.0).then_inc(setup_pool, 1)
            setup(g.memset(va[:, :, :, HD:HD + 1], 1.0))
            pool.wait_ge(setup_pool, 14)

            with pool.Fori(1, IMAGES + 1) as i:
                own = Own(pool, pool_own)
                W = lambda s, k: pool.wait_ge(SA[s].sem, SA[s].at(i, k))
                for t in range(TILES):
                    W("var", t + 1)
                    g.tensor_tensor(rstd[:, t:t + 1], veps[:, t:t + 1], neghalf[:, 0:1], ALU.pow).then_inc(SA["rstd"].sem, 1)
                for t in range(TILES):
                    W("ss", t + 1)
                    g.tensor_tensor(rn[:, t, :], ss[:, t, :], neghalf[:, 0:2 * HEADS], ALU.pow).then_inc(SA["rn"].sem, 1)
                plain(pool)
                W("qk", 2)
                split_stack(W, own, SA["stack"].sem, i)
                for t in range(TILES):
                    W("exp", t + 1)
                    pv = prob[:, t].rearrange("p a b c -> p (a b c)")[:, 0:HEADS * WIN]
                    g.tensor_tensor(pv, pv, expbias[:].rearrange("p a b c -> p (a b c)"), ALU.mult).then_inc(SA["prob"].sem, 1)
                for t in range(TILES):
                    W("var2", t + 1)
                    g.tensor_tensor(rstd[:, t:t + 1], veps[:, t:t + 1], neghalf[:, 0:1], ALU.pow).then_inc(SA["rstd2"].sem, 1)

            pool.wait_ge(gam[0], 1)
            g.partition_all_reduce(ggall[:, 0], gg[:, 0], P, RMAX).then_inc(gam_all[0], 1)
            pool.wait_ge(gam[1], 1)
            g.partition_all_reduce(ggall[:, 1], gg[:, 1], P, RMAX).then_inc(gam_all[1], 1)
            g.memset(stack[:, :, :, :, SPLIT:MAXCOL], 0.0).then_inc(setup_pool, 1)
            pool.wait_ge(setup_pool, 15)
            with pool.Fori(1, IMAGES + 1) as i:
                own = Own(pool, pool_own)
                W = lambda s, k: pool.wait_ge(SC[s].sem, SC[s].at(i, k))
                for var, rs in (("var", "rstd"), ("cvar", "crstd")):
                    for t in range(TILES):
                        W(var, t + 1)
                        g.tensor_tensor(rstd[:, t:t + 1], veps[:, t:t + 1], neghalf[:, 0:1], ALU.pow).then_inc(SC[rs].sem, 1)
                plain(pool)
                W("q_sb", 2)
                W("k_sb", 2)
                split_stack(W, own, SC["stack"].sem, i)
                for t in range(TILES):
                    W("var3", t + 1)
                    g.tensor_tensor(rstd[:, t:t + 1], veps[:, t:t + 1], neghalf[:, 0:1], ALU.pow).then_inc(SC["rstd3"].sem, 1)

        @block.vector
        def _(dve):
            v = nc.vector
            prime(dve, "dve")
            dve.wait_ge(weights_in, 16 * len(loads))
            dve.wait_ge(setup_pool, 8)
            n = [0]

            def setup(ins):
                ins.then_inc(setup_dve, 1)
                n[0] += 1
                dve.wait_ge(setup_dve, n[0])

            setup(v.tensor_copy(identb[:], ident[:]))
            setup(v.memset(xnt[C:C + 1, :], 1.0))
            setup(v.memset(ont[C:C + 1, :], 1.0))
            setup(v.memset(gm2[:], 0.0))
            setup(v.tensor_reduce(wsum[0:C, :], w1[:, 0:GROUPS * (HID // GROUPS)].rearrange("p (g n) -> p g n", g=GROUPS), AX.X, ALU.add))
            dve.wait_ge(setup_pe, 1)
            setup(v.tensor_scalar(wmean[0:C, 0, :], ps[0:C, 0, 0:GROUPS], 1.0 / (HID // GROUPS * C), None, ALU.mult))
            gw = C // GROUPS
            w2g = w2[:, :, 0:GROUPS * gw].rearrange("p m (g n) -> p g m n", g=GROUPS)
            setup(v.tensor_reduce(wsum[:, :], w2g, AX.XY, ALU.add))
            dve.wait_ge(setup_pe, 2)
            setup(v.tensor_scalar(wmean[:, 1, :], ps[:, 0, 0:GROUPS], 1.0 / (gw * HID), None, ALU.mult))
            v.memset(w1s[:], 0.0).then_inc(setup_dve, 1)
            v.memset(w2s[:], 0.0).then_inc(setup_dve, 1)
            n[0] += 2
            dve.wait_ge(setup_dve, n[0])
            g1 = HID // GROUPS
            for g in range(GROUPS):
                v.tensor_scalar(w1s[:, g1 * g:g1 * (g + 1)], w1[:, g1 * g:g1 * (g + 1)], wmean[0:C, 0, g:g + 1], None, ALU.subtract).then_inc(setup_dve, 1)
                v.tensor_scalar(w2s[:, :, gw * g:gw * (g + 1)], w2[:, :, gw * g:gw * (g + 1)], wmean[:, 1, g:g + 1], None, ALU.subtract).then_inc(setup_dve, 1)
            n[0] += 10
            dve.wait_ge(setup_act, 4)
            setup(v.tensor_scalar(ebz[:], ebz[:], 8.0, 8.0, ALU.mult, ALU.add))
            import math
            setup(v.tensor_scalar(lscale[:], lscale[:], math.log(100.0), None, ALU.min))

            def norm(own, W, src, eps, S, var, rs, dst_sig, t, i, dst, late=None):
                own.link(v.bn_stats(stats[:, t, :], src))
                own.link(v.bn_aggr(mv[:, t, :], stats[:, t, :]))
                v.tensor_scalar(veps[:, t:t + 1], mv[:, t, 1:2], eps, None, ALU.add).then_inc(S[var].sem, 1)

            def norm_apply(W, src, S, rs, sig, t, dst):
                W(rs, t + 1)
                v.tensor_scalar(dst, src, mv[:, t, 0:1], rstd[:, t:t + 1], ALU.subtract, ALU.mult).then_inc(S[sig].sem, 1)

            dve.wait_ge(setup_act, ASETUP)
            with dve.Fori(1, IMAGES + 1) as i:
                own = Own(dve, dve_own)
                W = lambda s, k: dve.wait_ge(SA[s].sem, SA[s].at(i, k))
                W("x_in", 48)
                for t in range(TILES):
                    norm(own, W, xin[:, t, :], 1e-6, SA, "var", "rstd", "xn", t, i, xn)
                for t in range(TILES):
                    norm_apply(W, xin[:, t, :], SA, "rstd", "xn", t, xn[:, t, :])
                for t in range(TILES):
                    W("sq", t + 1)
                    own.link(v.tensor_reduce(ss[:, t, :], sq[:, t], AX.X, ALU.add))
                    v.tensor_scalar(ss[:, t, :], ss[:, t, :], 1e-24, None, ALU.max).then_inc(SA["ss"].sem, 1)
                for t in range(TILES):
                    W("rn", t + 1)
                    W("v", t + 1)
                    own.link(v.tensor_tensor(rn[:, t, 0:HEADS], rn[:, t, 0:HEADS], lscale[:], ALU.mult))
                    v.tensor_tensor(qk[:, t].rearrange("p a h c -> p (a h) c"),
                                    ps[:, 2 + t, 0:2 * C].rearrange("p (h c) -> p h c", c=HD),
                                    rn[:, t, :].to_broadcast([P, 2 * HEADS, HD]), ALU.mult).then_inc(SA["qk"].sem, 1)
                for t in range(TILES):
                    W("s", t + 1)
                    own.link(v.tensor_reduce(nm[:, t], ps[:, 4 + 2 * t:6 + 2 * t, 0:PAIRS * WIN].rearrange("p a (b n) -> p a b n", n=WIN),
                                             AX.X, ALU.max, negate=True))
                    sv = stack[:, t, 0].rearrange("p (b a) c -> p a b c", a=2)
                    own.link(v.tensor_copy(sv[:, :, :, MAXCOL], nm[:, t]))
                    own.link(v.tensor_tensor(nmr[:, t], nm[:, t], sv[:, :, :, MAXCOL], ALU.subtract))
                    own.link(v.tensor_copy(sv[:, :, :, MAXCOL + 1], nmr[:, t]))
                    v.tensor_tensor(sv[:, :, :, MAXCOL + 2], nmr[:, t], sv[:, :, :, MAXCOL + 1], ALU.subtract).then_inc(SA["nm"].sem, 1)
                for t in range(TILES):
                    W("otr", t + 1)
                    o = ps[:, 4 + 2 * t, 0:384].rearrange("p (h c) -> p h c", c=32)
                    own.link(v.reciprocal(rec[:, t, :], o[:, :, HD]))
                    v.tensor_tensor(on[:, t].rearrange("p (h c) -> p h c", c=HD), o[:, :, 0:HD],
                                    rec[:, t, :].to_broadcast([P, HEADS, HD]), ALU.mult).then_inc(SA["on"].sem, 1)
                W("x1_out", 0)
                for t in range(TILES):
                    W("proj", t + 1)
                    v.tensor_tensor(xres[:, t, :], xin[:, t, :], ps[:, t, 0:C], ALU.add).then_inc(SA["x1"].sem, 1)
                for t in range(TILES):
                    W("x1", t + 1)
                    norm(own, W, xres[:, t, :], 1e-5, SA, "var2", "rstd2", "xn2", t, i, xn)
                for t in range(TILES):
                    norm_apply(W, xres[:, t, :], SA, "rstd2", "xn2", t, xn[:, t, :])
                W("y1_sb", 1)
                v.tensor_reduce(gm1[:, bass.ds(i - 1, 1)], y1all[:, bass.ds(i - 1, 1)].rearrange("p a m n -> p (a m n)"),
                                AX.X, ALU.max, apply_absolute_value=True).then_inc(SA["gm"].sem, 1)

            def gammas(n, gm, done, qs):
                dve.wait_ge(done, 1)
                v.tensor_reduce(gg[:, n], gm[:, 0:QIMG].rearrange("p (g n) -> p g n", n=GIMG), AX.X, ALU.max).then_inc(gam[n], 1)
                own = Own(dve, dve_own)
                dve.wait_ge(gam_all[n], 1)
                own.link(v.tensor_scalar(gs[:, n], ggall[:, n], EPSQ, None, ALU.add))
                own.link(v.reciprocal(gs[:, n], gs[:, n]))
                own.link(v.tensor_scalar(gs[:, n], gs[:, n], QB, None, ALU.mult))
                own.link(v.memset(qs[:], 0.0))
                v.tensor_copy(qs[:, 0:QIMG].rearrange("p (g n) -> p g n", n=GIMG),
                              gs[:, n].to_broadcast([P, GROUPS, GIMG])).then_inc(gam_ready[n], 1)
                dve.wait_ge(gam_ready[n], 1)

            dve.wait_ge(SA["gm"].sem, IMAGES + 1)
            gammas(0, gm1, SA["gm"].sem, qs1)
            with dve.Fori(1, QIMG + 1) as i:
                own = Own(dve, dve_own)
                W = lambda s, k: dve.wait_ge(SB[s].sem, SB[s].at(i, k))
                y = y1all[:, bass.ds(i - 1, 1)].rearrange("p a m n -> p (a m n)")
                W("h", 0)
                h0 = hb[:, 0].rearrange("p m n -> p (m n)")
                own.link(v.tensor_scalar(h0, y, qs1[:, bass.ds(i - 1, 1)], LIM, ALU.mult, ALU.min))
                v.tensor_scalar(h0, h0, -LIM, None, ALU.max).then_inc(SB["cl"].sem, 1)
                W("y2_sb", 1)
                v.tensor_reduce(gm2[0:C, bass.ds(i - 1, 1)], y2all[:, bass.ds(i - 1, 1), :].rearrange("p a n -> p (a n)"),
                                AX.X, ALU.max, apply_absolute_value=True).then_inc(SB["gm"].sem, 1)
            dve.wait_ge(SB["gm"].sem, QIMG + 1)
            gammas(1, gm2, SB["gm"].sem, qs2)

            with dve.Fori(1, IMAGES + 1) as i:
                own = Own(dve, dve_own)
                W = lambda s, k: dve.wait_ge(SC[s].sem, SC[s].at(i, k))
                own.link(v.tensor_scalar(ycl[:], y2all[:, bass.ds(i - 1, 1), :].rearrange("p a n -> p (a n)"),
                                         qs2[0:C, bass.ds(i - 1, 1)], LIM, ALU.mult, ALU.min))
                v.tensor_scalar(ycl[:], ycl[:], -LIM, None, ALU.max).then_inc(SC["ycl"].sem, 1)
                W("x_in", 16)
                for t in range(TILES):
                    W("yt", t + 1)
                    own.link(v.tensor_tensor(xin[:, t, :], xin[:, t, :], ps[:, t, 0:C], ALU.add))
                for t in range(TILES):
                    norm(own, W, xin[:, t, :], 1e-6, SC, "var", "rstd", "xn", t, i, xn)
                for t in range(TILES):
                    norm_apply(W, xin[:, t, :], SC, "rstd", "xn", t, xn[:, t, :])
                for t in range(TILES):
                    W("conv", t + 1)
                    norm(own, W, ps[:, 2 + t, 0:C], 1e-3, SC, "cvar", "crstd", "cn", t, i, tn)
                for t in range(TILES):
                    W("crstd", t + 1)
                    own.link(v.tensor_scalar(tn[:, t, :], ps[:, 2 + t, 0:C], mv[:, t, 0:1], rstd[:, t:t + 1], ALU.subtract, ALU.mult))
                own.link(v.tensor_tensor(tn[:], tn[:], lng[:, :].rearrange("p (a c) -> p a c", a=1).to_broadcast([P, TILES, C]), ALU.mult))
                v.tensor_tensor(tn[:], tn[:], lnb[:, :].rearrange("p (a c) -> p a c", a=1).to_broadcast([P, TILES, C]), ALU.add).then_inc(SC["cn"].sem, 1)
                W("tanh", 1)
                thf, htf = th[:].rearrange("p a n -> p (a n)"), hat[:].rearrange("p a n -> p (a n)")
                own.link(v.scalar_tensor_tensor(thf, thf, SIDE / 2.0, posc[:].rearrange("p a n -> p (a n)"), ALU.mult, ALU.add))
                own.link(v.scalar_tensor_tensor(htf, thf, -1.0, thf, ALU.mult, ALU.min))
                v.tensor_scalar(htf, htf, 1.0, 0.0, ALU.add, ALU.max).then_inc(SC["hat"].sem, 1)
                W("hatx", 1)
                for t in range(TILES):
                    W("t3", t + 1)
                    for b in range(3):
                        hx = hatx[:, t, 2 * b:2 * b + 2, :].rearrange("p g c -> p (g c)")
                        v.tensor_tensor(samp[:, (3 * t + b) % 2], ps[:, 5 - 4 * t + b, :].rearrange("p (a c) -> p a c", c=GC),
                                        hx.to_broadcast([P, 2 * SIDE, GC]), ALU.mult).then_inc(SC["mul"].sem, 1)
                        W("mul", 3 * t + b + 1)
                        ins = v.tensor_reduce(xs[:, t, 2 * GC * b:2 * GC * (b + 1)].rearrange("p (g k) -> p g k", g=2),
                                              samp[:, (3 * t + b) % 2].rearrange("p (g c) k -> p g k c", g=2), AX.X, ALU.add)
                        if b == 2:
                            ins.then_inc(SC["xs"].sem, 1)
                        else:
                            own.link(ins)
                for u in range(6):
                    t, pq = u // 3, u % 3
                    W("s", u + 1)
                    bk = 4 + 2 * (u % 2)
                    v.tensor_reduce(nm[:, t, :, 2 * pq:2 * pq + 2], ps[:, bk:bk + 2, :].rearrange("p a (b n) -> p a b n", n=TOK),
                                    AX.X, ALU.max, negate=True).then_inc(SC["nm"].sem, 1)
                W("nm", 6)
                for t in range(TILES):
                    sv = stack[:, t, 0].rearrange("p (b a) c -> p a b c", a=2)
                    own.link(v.tensor_copy(sv[:, :, :, MAXCOL], nm[:, t]))
                    own.link(v.tensor_tensor(nmr[:, t], nm[:, t], sv[:, :, :, MAXCOL], ALU.subtract))
                    own.link(v.tensor_copy(sv[:, :, :, MAXCOL + 1], nmr[:, t]))
                    ins = v.tensor_tensor(sv[:, :, :, MAXCOL + 2], nmr[:, t], sv[:, :, :, MAXCOL + 1], ALU.subtract)
                    if t:
                        ins.then_inc(SC["parts"].sem, 1)
                    else:
                        own.link(ins)
                for t in range(TILES):
                    W("otr", t + 1)
                    o = ps[:, t, 0:384].rearrange("p (h c) -> p h c", c=32)
                    own.link(v.reciprocal(rec[:, t, :], o[:, :, HD]))
                    v.tensor_tensor(on[:, t].rearrange("p (h c) -> p h c", c=HD), o[:, :, 0:HD],
                                    rec[:, t, :].to_broadcast([P, HEADS, HD]), ALU.mult).then_inc(SC["on"].sem, 1)
                for t in range(TILES):
                    W("proj", t + 1)
                    v.tensor_tensor(xres[:, t, :], xin[:, t, :], ps[:, t, 0:C], ALU.add).then_inc(SC["x3"].sem, 1)
                for t in range(TILES):
                    W("x3", t + 1)
                    norm(own, W, xres[:, t, :], 1e-5, SC, "var3", "rstd3", "xn3", t, i, xn)
                for t in range(TILES):
                    norm_apply(W, xres[:, t, :], SC, "rstd3", "xn3", t, xn[:, t, :])
                W("gate", 2)
                own.link(v.tensor_copy(sc[:], ps[:, 0:2, 0:EXPERTS]))
                own.link(v.tensor_reduce(scm[:], sc[:], AX.X, ALU.max))
                v.tensor_tensor(sc[:], sc[:], scm[:].to_broadcast([P, TILES, EXPERTS]), ALU.subtract).then_inc(SC["gsub"].sem, 1)
                W("gexp", 1)
                own.link(v.tensor_reduce(scs[:], sc[:], AX.X, ALU.add))
                own.link(v.reciprocal(scs[:], scs[:]))
                own.link(v.tensor_tensor(sc[:], sc[:], scs[:].to_broadcast([P, TILES, EXPERTS]), ALU.mult))
                for t in range(TILES):
                    other = sc[:, t:t + 1, :].to_broadcast([P, EXPERTS, EXPERTS])
                    mine = sc[:, t, :].to_broadcast([P, EXPERTS, EXPERTS])
                    own.mark(v.tensor_tensor(gt[:, t], other, mine, ALU.is_gt))
                    own.link(v.tensor_tensor(eq[:, t], other, mine, ALU.is_equal))
                    own.link(v.tensor_tensor(eq[:, t], eq[:, t], tri[:], ALU.mult))
                own.link(v.tensor_tensor(gt[:], gt[:], eq[:], ALU.add))
                own.link(v.tensor_reduce(eq[:, :, :, 0], gt[:], AX.X, ALU.add))
                own.link(v.tensor_scalar(eq[:, :, :, 0], eq[:, :, :, 0], 1.5, None, ALU.is_lt))
                own.link(v.tensor_tensor(sc[:], sc[:], eq[:, :, :, 0], ALU.mult))
                own.link(v.tensor_reduce(scs[:], sc[:], AX.X, ALU.add))
                own.link(v.tensor_scalar(scs[:], scs[:], 1e-9, None, ALU.add))
                own.link(v.reciprocal(scs[:], scs[:]))
                own.link(v.tensor_tensor(sc[:], sc[:], scs[:].to_broadcast([P, TILES, EXPERTS]), ALU.mult))
                W("out", 0)
                for t in range(TILES):
                    W("y", t + 1)
                    src = xres
                    for e in range(EXPERTS):
                        ins = v.scalar_tensor_tensor(acc[:, t, :], ps[:, 2 + t, C * e:C * e + C], sc[:, t, e:e + 1],
                                                     src[:, t, :], ALU.mult, ALU.add)
                        src = acc
                        if e == EXPERTS - 1:
                            ins.then_inc(SC["acc"].sem, 1)
                        else:
                            own.link(ins)

        @block.scalar
        def _(act):
            a = nc.scalar
            prime(act, "act")
            n = [0]

            def setup(ins):
                ins.then_inc(setup_act, 1)
                n[0] += 1
                act.wait_ge(setup_act, n[0])

            act.wait_ge(setup_pe, 3)
            setup(a.activation(hid_t[:], ps[:, 1, 0:REL], ACT.Relu, bias=cpb_b1[:, 0:1]))
            act.wait_ge(setup_pe, 4)
            setup(a.copy(bt_sb[:], ps[0:HEADS, 2, 0:REL]))
            act.wait_ge(setup_pe, 5)
            setup(a.activation(ebz[:, 0:6], ps[:, 3, 0:384].rearrange("p (h n) -> p h n", n=WIN), ACT.Tanh, scale=0.5))
            setup(a.activation(ebz[:, 6:12], ps[:, 4, 0:384].rearrange("p (h n) -> p h n", n=WIN), ACT.Tanh, scale=0.5))
            act.wait_ge(setup_dve, 21)
            setup(a.activation(expbias[:], ebz[:].rearrange("p (b a) n -> p a b n", a=2), ACT.Exp))
            act.wait_ge(setup_dve, 22)
            setup(a.activation(lscale[:], lscale[:], ACT.Exp))
            setup(a.activation(w1s[:], w1s[:], ACT.Sign))
            setup(a.activation(w2s[:], w2s[:], ACT.Sign))

            act.wait_ge(setup_pool, 14)
            with act.Fori(1, IMAGES + 1) as i:
                W = lambda s, k: act.wait_ge(SA[s].sem, SA[s].at(i, k))
                for t in range(TILES):
                    W("xt", t + 1)
                    a.copy(xnt[0:C, P * t:P * t + P], ps[0:C, t, 0:P]).then_inc(SA["xnt"].sem, 1)
                for t in range(TILES):
                    W("qkv", t + 1)
                    a.activation(sq[:, t].rearrange("p h c -> p (h c)"), ps[:, 2 + t, 0:2 * C], ACT.Square).then_inc(SA["sq"].sem, 1)
                for t in range(TILES):
                    a.copy(va[:, t, :, 0:HD], ps[:, 2 + t, 2 * C:3 * C].rearrange("p (h c) -> p h c", c=HD)).then_inc(SA["v"].sem, 1)
                for t in range(TILES):
                    W("qt", t + 1)
                    a.copy(stackt[:, 0, :, P * t:P * t + P], bank_bf(2 + t)).then_inc(SA["qt_sb"].sem, 1)
                    W("kt", t + 1)
                    a.copy(stackt[:, 1, :, P * t:P * t + P], bank_bf(4 + 2 * t)).then_inc(SA["kt_sb"].sem, 1)
                for t in range(TILES):
                    W("q2t", t + 1)
                    a.copy(stackt[:, 0, :, P * t:P * t + P], bank_bf(2 + t)).then_inc(SA["q2t_sb"].sem, 1)
                for t in range(TILES):
                    W("st", t + 1)
                    pv = prob[:, t].rearrange("p a b c -> p (a b c)")[:, 0:HEADS * WIN]
                    a.activation(pv.rearrange("p (a n) -> p a n", a=2), ps[:, 4 + 2 * t:6 + 2 * t, 0:PAIRS * WIN], ACT.Exp).then_inc(SA["exp"].sem, 1)
                for t in range(TILES):
                    W("pv", t + 1)
                    o = ot[:, :, P * t:P * t + P].rearrange("p s (w n) -> p s w n", w=2)
                    own = a.copy(o[:, :, 0, :], ps[:, t, 0:3 * WIN].rearrange("p (s n) -> p s n", n=WIN))
                    a.copy(o[:, :, 1, :], ps[:, 2 + t, 0:3 * WIN].rearrange("p (s n) -> p s n", n=WIN)).then_inc(SA["ot"].sem, 1)
                for t in range(TILES):
                    W("ontp", t + 1)
                    a.copy(ont[0:C, P * t:P * t + P], ps[0:C, 5 + 2 * t, 0:P]).then_inc(SA["ont"].sem, 1)
                for t in range(TILES):
                    W("x2t", t + 1)
                    a.copy(xnt[0:C, P * t:P * t + P], ps[0:C, 2 + t, 0:P]).then_inc(SA["x2t_sb"].sem, 1)
                W("y1", 1)
                for m in range(MT):
                    ins = a.activation(y1all[:, bass.ds(i - 1, 1), m, :].rearrange("p a n -> p (a n)"),
                                       ps[:, 4 + m // 2, TOK * (m % 2):TOK * (m % 2) + TOK], ACT.Identity, bias=b1[:, m:m + 1])
                ins.then_inc(SA["y1_sb"].sem, 1)

            with act.Fori(1, QIMG + 1) as i:
                W = lambda s, k: act.wait_ge(SB[s].sem, SB[s].at(i, k))
                W("cl", 1)
                W("y2", 0)
                a.activation(hb[:, 1].rearrange("p m n -> p (m n)"), hb[:, 0].rearrange("p m n -> p (m n)"), ACT.Gelu).then_inc(SB["h"].sem, 1)
                W("y2", 1)
                k = SHIFT * SIDE
                a.activation(y2all[:, bass.ds(i - 1, 1), k:TOK].rearrange("p a n -> p (a n)"), ps[0:C, 0, 0:TOK - k], ACT.Identity, bias=b2[:, 0:1])
                a.activation(y2all[:, bass.ds(i - 1, 1), 0:k].rearrange("p a n -> p (a n)"), ps[0:C, 0, TOK - k:TOK], ACT.Identity,
                             bias=b2[:, 0:1]).then_inc(SB["y2_sb"].sem, 1)

            with act.Fori(1, IMAGES + 1) as i:
                W = lambda s, k: act.wait_ge(SC[s].sem, SC[s].at(i, k))
                for t in range(TILES):
                    W("xt", t + 1)
                    a.copy(xnt[0:C, P * t:P * t + P], ps[0:C, 2 + t, 0:P]).then_inc(SC["xnt"].sem, 1)
                W("qc", 1)
                qc = ps[0:C, 4, 0:TOK].rearrange("p (r c) -> p r c", c=SIDE)
                a.copy(qpad[:, 0, 1:1 + SIDE, 1:SIDE], qc[:, :, 0:SIDE - 1])
                a.copy(qpad[:, 1, 1:1 + SIDE, :], qc)
                a.copy(qpad[:, 2, 1:1 + SIDE, 0:SIDE - 1], qc[:, :, 1:SIDE]).then_inc(SC["qpad"].sem, 1)
                for t in range(TILES):
                    W("q", t + 1)
                    a.copy(qk[:, t, 0], ps[:, t, 0:C].rearrange("p (h c) -> p h c", c=HD)).then_inc(SC["q_sb"].sem, 1)
                W("cn", 1)
                a.activation(tn[:], tn[:], ACT.Gelu).then_inc(SC["cg"].sem, 1)
                for t in range(TILES):
                    W("tt", t + 1)
                    a.copy(tnt[:, P * t:P * t + P], ps[0:C, t, 0:P]).then_inc(SC["tnt"].sem, 1)
                W("offs", 1)
                a.activation(th[:].rearrange("p a n -> p (a n)"), ps[0:C, 4, :], ACT.Tanh).then_inc(SC["tanh"].sem, 1)
                W("hxt", 1)
                a.copy(hatx[:].rearrange("p t g c -> p (t g c)"), ps[:, 4, 0:2 * C]).then_inc(SC["hatx"].sem, 1)
                W("xst", 2)
                for t in range(TILES):
                    a.copy(xnt[0:C, P * t:P * t + P], ps[0:C, 4, P * t:P * t + P]).then_inc(SC["xst_sb"].sem, 1)
                for t in range(TILES):
                    W("kv", t + 1)
                    a.copy(qk[:, t, 1], ps[:, t, 0:C].rearrange("p (h c) -> p h c", c=HD)).then_inc(SC["k_sb"].sem, 1)
                for t in range(TILES):
                    a.copy(va[:, t, :, 0:HD], ps[:, t, C:2 * C].rearrange("p (h c) -> p h c", c=HD)).then_inc(SC["v"].sem, 1)
                for t in range(TILES):
                    W("qt", t + 1)
                    a.copy(stackt[:, 0, :, P * t:P * t + P], bank_bf(2 + t)).then_inc(SC["qt_sb"].sem, 1)
                    W("kt", t + 1)
                    a.copy(stackt[:, 1, :, P * t:P * t + P], bank_bf(t)).then_inc(SC["kt_sb"].sem, 1)
                for t in range(TILES):
                    W("q2t", t + 1)
                    a.copy(stackt[:, 0, :, P * t:P * t + P], bank_bf(t)).then_inc(SC["q2t_sb"].sem, 1)
                for u in range(6):
                    W("st", u + 1)
                    if u >= 2:
                        W("pv", u - 1)
                    bk = 4 + 2 * (u % 2)
                    a.activation(prob[:, u % 2].rearrange("p a b n -> p a (b n)"), ps[:, bk:bk + 2, :], ACT.Exp, scale=float(HD) ** -0.5).then_inc(SC["exp"].sem, 1)
                for s in range(3):
                    W("pv", 2 * s + 2)
                    if s == 0:
                        W("pv", 4)
                    a.copy(ot[:, s, :], ps[:, 2 + s // 2, TOK * (s % 2):TOK * (s % 2) + TOK]).then_inc(SC["ot"].sem, 1)
                for t in range(TILES):
                    W("ontp", t + 1)
                    a.copy(ont[0:C, P * t:P * t + P], ps[0:C, 2 + t, 0:P]).then_inc(SC["ont"].sem, 1)
                for t in range(TILES):
                    W("x3t", t + 1)
                    a.copy(xnt[0:C, P * t:P * t + P], ps[0:C, 2 + t, 0:P]).then_inc(SC["x3t_sb"].sem, 1)
                W("gsub", 1)
                a.activation(sc[:], sc[:], ACT.Exp).then_inc(SC["gexp"].sem, 1)
                for e in range(EXPERTS):
                    W("h1", e + 1)
                    bk = 4 + 2 * (e % 2)
                    a.activation(hb[:, e % 2].rearrange("p m n -> p (m n)"), ps[:, bk:bk + 2, :].rearrange("p a n -> p (a n)")[:, 0:MT * TOK],
                                 ACT.Gelu).then_inc(SC["h"].sem, 1)

        @block.tensor
        def _(pe):
            m = nc.tensor
            prime(pe, "pe")

            def mm(o, l, r, start=True, stop=True):
                return m.matmul(o, l, r, start=start, stop=stop)

            def turn(bank, st, t, a):
                for b in range(PAIRS):
                    ins = m.transpose(bank_bf(bank)[:, b, :], st[:, t, a].rearrange("p h c -> p (h c)")[:, P * b:P * b + P], identb[:])
                return ins

            pe.wait_ge(weights_in, 16 * len(loads))
            pe.wait_ge(setup_pool, 8)
            pe.wait_ge(setup_dve, 5)
            mm(ps[0:C, 0, 0:GROUPS], onesm[0:C, 0:C], wsum[0:C, :]).then_inc(setup_pe, 1)
            pe.wait_ge(setup_dve, 7)
            mm(ps[:, 0, 0:GROUPS], onesm[:, :], wsum[:, :]).then_inc(setup_pe, 1)
            mm(ps[:, 1, 0:REL], cpb_w1[:], table[:]).then_inc(setup_pe, 1)
            pe.wait_ge(setup_act, 1)
            mm(ps[0:HEADS, 2, 0:REL], cpb_w2[:], hid_t[:]).then_inc(setup_pe, 1)
            pe.wait_ge(bt_dma, 16 * 65)
            for b in range(2):
                ins = mm(ps[:, 3 + b, 0:384], flip[:], ebraw[:, 6 * b:6 * b + 6, :].rearrange("p h n -> p (h n)"))
            ins.then_inc(setup_pe, 1)
            pe.wait_ge(setup_act, ASETUP)
            pe.wait_ge(setup_dve, 22)
            pe.wait_ge(setup_pool, 14)

            with pe.Fori(1, IMAGES + 1) as i:
                W = lambda s, k: pe.wait_ge(SA[s].sem, SA[s].at(i, k))
                for t in range(TILES):
                    W("xn", t + 1)
                    mm(ps[0:C, t, 0:P], xn[:, t, :], perm_in[:]).then_inc(SA["xt"].sem, 1)
                for t in range(TILES):
                    W("xnt", t + 1)
                    mm(ps[:, 2 + t, 0:3 * C], xnt[:, P * t:P * t + P], wqkv[:]).then_inc(SA["qkv"].sem, 1)
                W("stack", 1)
                W("v", 2)
                W("y1_sb", 0)
                for t in range(TILES):
                    turn(2 + t, stack, t, 0).then_inc(SA["qt"].sem, 1)
                    turn(4 + 2 * t, stack, t, 1).then_inc(SA["kt"].sem, 1)

                def window(t, w):
                    return slice(P * t + WIN * w, P * t + WIN * w + WIN)

                for t in range(TILES):
                    plain(pe)
                    W("qt_sb", t + 1)
                    W("kt_sb", t + 1)
                    for h in range(HEADS):
                        b, a = h // 2, h % 2
                        r = slice(SLOT * a, SLOT * a + MAXCOL)
                        for w in range(2):
                            ins = mm(ps[WIN * w:WIN * w + WIN, 4 + 2 * t + a, WIN * b:WIN * b + WIN],
                                     stackt[r, 0, b, window(t, w)], stackt[r, 1, b, window(t, w)])
                    ins.then_inc(SA["s"].sem, 1)
                for t in range(TILES):
                    W("nm", t + 1)
                    turn(2 + t, stack, t, 0).then_inc(SA["q2t"].sem, 1)
                for t in range(TILES):
                    plain(pe)
                    W("q2t_sb", t + 1)
                    for h in range(HEADS):
                        b, a = h // 2, h % 2
                        r = slice(SLOT * a, SLOT * a + FULL)
                        for w in range(2):
                            ins = mm(ps[WIN * w:WIN * w + WIN, 4 + 2 * t + a, WIN * b:WIN * b + WIN],
                                     stackt[r, 1, b, window(t, w)], stackt[r, 0, b, window(t, w)])
                    ins.then_inc(SA["st"].sem, 1)
                for t in range(TILES):
                    plain(pe)
                    W("prob", t + 1)
                    pv = prob[:, t].rearrange("p a b c -> p (a b c)")
                    for h in range(HEADS):
                        for w in range(2):
                            k = slice(WIN * w, WIN * w + WIN)
                            at = (h % 2) * PAIRS * WIN + (h // 2) * WIN
                            ins = mm(ps[32 * (h % 4):32 * (h % 4) + 32, t if w == 0 else 2 + t, WIN * (h // 4):WIN * (h // 4) + WIN],
                                     va[k, t, h, :], pv[k, at:at + WIN])
                    ins.then_inc(SA["pv"].sem, 1)
                for t in range(TILES):
                    W("ot", t + 1)
                    for s in range(3):
                        ins = m.transpose(ps[:, 4 + 2 * t, P * s:P * s + P], ot[:, s, P * t:P * t + P], ident[:])
                    ins.then_inc(SA["otr"].sem, 1)
                for t in range(TILES):
                    W("on", t + 1)
                    mm(ps[0:C, 5 + 2 * t, 0:P], on[:, t, :], perm_out[:]).then_inc(SA["ontp"].sem, 1)
                for t in range(TILES):
                    W("ont", t + 1)
                    mm(ps[:, t, 0:C], ont[:, P * t:P * t + P], wproj[:]).then_inc(SA["proj"].sem, 1)
                for t in range(TILES):
                    W("xn2", t + 1)
                    m.transpose(ps[0:C, 2 + t, 0:P], xn[:, t, :], ident[:]).then_inc(SA["x2t"].sem, 1)
                W("x2t_sb", 2)
                for k in range(MT):
                    ins = mm(ps[:, 4 + k // 2, TOK * (k % 2):TOK * (k % 2) + TOK], w1s[:, P * k:P * k + P], xnt[0:C, :])
                ins.then_inc(SA["y1"].sem, 1)

            with pe.Fori(1, QIMG + 1) as i:
                W = lambda s, k: pe.wait_ge(SB[s].sem, SB[s].at(i, k))
                W("h", 1)
                W("y2_sb", 0)
                for k in range(MT):
                    ins = mm(ps[0:C, 0, 0:TOK], w2s[:, k, :], hb[:, 1, k, :], k == 0, k == MT - 1)
                ins.then_inc(SB["y2"].sem, 1)

            pe.wait_ge(SB["y2_sb"].sem, QIMG + 1)
            pe.wait_ge(SA["y1_sb"].sem, IMAGES + 1)
            with pe.Fori(1, IMAGES + 1) as i:
                W = lambda s, k: pe.wait_ge(SC[s].sem, SC[s].at(i, k))
                W("ycl", 1)
                for t in range(TILES):
                    m.transpose(ps[:, t, 0:C], ycl[:, P * t:P * t + P], ident[0:C, 0:C]).then_inc(SC["yt"].sem, 1)
                W("acc", 0)
                for t in range(TILES):
                    W("xn", t + 1)
                    m.transpose(ps[0:C, 2 + t, 0:P], xn[:, t, :], ident[:]).then_inc(SC["xt"].sem, 1)
                W("xnt", 2)
                mm(ps[0:C, 4, 0:TOK], wq[:], xnt[:]).then_inc(SC["qc"].sem, 1)
                for t in range(TILES):
                    mm(ps[:, t, 0:C], xnt[:, P * t:P * t + P], wq[:]).then_inc(SC["q"].sem, 1)
                W("qpad", 1)
                for t in range(TILES):
                    o = ps[:, 2 + t, 0:C]
                    for k in range(9):
                        r0 = 8 * t + k // 3
                        mm(o, qpad[:, k % 3, r0:r0 + 8, :].rearrange("p r c -> p (r c)"), wconv[:, k, :], k == 0, False)
                    mm(o, onesm[0:1, :], boff[:], False, True).then_inc(SC["conv"].sem, 1)
                W("cg", 1)
                W("q_sb", 2)
                for t in range(TILES):
                    m.transpose(ps[0:C, t, 0:P], tn[:, t, :], ident[:]).then_inc(SC["tt"].sem, 1)
                W("tnt", 2)
                for k in range(2):
                    ins = mm(ps[0:C, 4, TOK * k:TOK * k + TOK], woffp[:, k, :], tnt[:])
                ins.then_inc(SC["offs"].sem, 1)
                W("hat", 1)
                for t in range(TILES):
                    ins = m.transpose(ps[:, 4, C * t:C * t + C], hat[:, 1, P * t:P * t + P], ident[0:C, 0:C])
                ins.then_inc(SC["hxt"].sem, 1)
                W("rows_in", 16 * DG)
                for t in range(TILES):
                    for b in range(3):
                        ins = mm(ps[:, 5 - 4 * t + b, :], hat[:, 0, P * t:P * t + P],
                                 rows[:, 2 * b:2 * b + 2].rearrange("p g c k -> p (g c k)"))
                    ins.then_inc(SC["t3"].sem, 1)
                W("hatx", 1)
                W("xs", 2)
                for t in range(TILES):
                    m.transpose(ps[0:C, 4, P * t:P * t + P], xs[:, t, :], ident[:]).then_inc(SC["xst"].sem, 1)
                W("xst_sb", 2)
                for t in range(TILES):
                    mm(ps[:, t, 0:2 * C], xnt[:, P * t:P * t + P], wkv[:]).then_inc(SC["kv"].sem, 1)
                W("stack", 1)
                W("v", 2)
                for t in range(TILES):
                    turn(2 + t, stack, t, 0).then_inc(SC["qt"].sem, 1)
                    turn(t, stack, t, 1).then_inc(SC["kt"].sem, 1)
                W("qt_sb", 2)
                W("kt_sb", 2)
                for u in range(6):
                    t, pq = u // 3, u % 3
                    if u >= 2:
                        W("nm", u - 1)
                    for h in range(4):
                        b, a = 2 * pq + h // 2, h % 2
                        r = slice(SLOT * a, SLOT * a + SPLIT)
                        ins = mm(ps[:, 4 + 2 * (u % 2) + a, TOK * (h // 2):TOK * (h // 2) + TOK],
                                 stackt[r, 0, b, P * t:P * t + P], stackt[r, 1, b, :])
                    ins.then_inc(SC["s"].sem, 1)
                W("parts", 1)
                for t in range(TILES):
                    turn(t, stack, t, 0).then_inc(SC["q2t"].sem, 1)
                W("q2t_sb", 2)

                def values(u):
                    pq, k = u // 2, u % 2
                    W("exp", u + 1)
                    for h in range(4):
                        ins = mm(ps[32 * h:32 * h + 32, 2 + pq // 2, TOK * (pq % 2):TOK * (pq % 2) + TOK],
                                 va[:, k, 4 * pq + h, :], prob[:, u % 2, h % 2, h // 2, :], k == 0, k == 1)
                    ins.then_inc(SC["pv"].sem, 1)

                for u in range(6):
                    pq, k = u // 2, u % 2
                    if u >= 2:
                        W("exp", u - 1)
                    for h in range(4):
                        b, a = 2 * pq + h // 2, h % 2
                        r = slice(SLOT * a, SLOT * a + FULL)
                        ins = mm(ps[:, 4 + 2 * (u % 2) + a, TOK * (h // 2):TOK * (h // 2) + TOK],
                                 stackt[r, 1, b, P * k:P * k + P], stackt[r, 0, b, :])
                    ins.then_inc(SC["st"].sem, 1)
                    if u >= 1:
                        values(u - 1)
                values(5)
                W("ot", 3)
                for t in range(TILES):
                    for s in range(3):
                        ins = m.transpose(ps[:, t, P * s:P * s + P], ot[:, s, P * t:P * t + P], ident[:])
                    ins.then_inc(SC["otr"].sem, 1)
                for t in range(TILES):
                    W("on", t + 1)
                    m.transpose(ps[0:C, 2 + t, 0:P], on[:, t, :], ident[:]).then_inc(SC["ontp"].sem, 1)
                for t in range(TILES):
                    W("ont", t + 1)
                    mm(ps[:, t, 0:C], ont[:, P * t:P * t + P], wo[:]).then_inc(SC["proj"].sem, 1)
                for t in range(TILES):
                    W("xn3", t + 1)
                    m.transpose(ps[0:C, 2 + t, 0:P], xn[:, t, :], ident[:]).then_inc(SC["x3t"].sem, 1)
                W("x3t_sb", 2)
                for t in range(TILES):
                    mm(ps[:, t, 0:EXPERTS], xnt[:, P * t:P * t + P], wg[:]).then_inc(SC["gate"].sem, 1)
                for t in range(TILES):
                    mm(ps[:, 2 + t, 0:EXPERTS * C], onesm[0:1, :], be2[:], True, False)

                def up(e):
                    if e >= 2:
                        W("h", e - 1)
                    bk = 4 + 2 * (e % 2)
                    for k in range(MT):
                        ins = mm(ps[:, bk + k // 2, TOK * (k % 2):TOK * (k % 2) + TOK], we1[:, e, P * k:P * k + P], xnt[:])
                    ins.then_inc(SC["h1"].sem, 1)

                up(0)
                for e in range(EXPERTS):
                    if e + 1 < EXPERTS:
                        up(e + 1)
                    W("h", e + 1)
                    for t in range(TILES):
                        for k in range(MT):
                            ins = mm(ps[:, 2 + t, C * e:C * e + C], hb[:, e % 2, k, P * t:P * t + P], we2[:, e, k, :],
                                     False, k == MT - 1 and e == EXPERTS - 1)
                        if e == EXPERTS - 1:
                            ins.then_inc(SC["y"].sem, 1)


def _constants():
    import numpy as np

    c = {}
    c["ident"] = np.eye(P, dtype=np.float32)
    perm = np.zeros((P, P), np.float32)
    for w in range(2):
        for r in range(8):
            for q in range(8):
                perm[r * SIDE + (SHIFT + 8 * w + q) % SIDE, w * WIN + r * 8 + q] = 1
    c["perm_in"] = perm
    c["perm_out"] = np.ascontiguousarray(perm.T)
    flip = np.zeros((WIN, P), np.float32)
    for j in range(WIN):
        flip[WIN - 1 - j, j] = flip[WIN - 1 - j, WIN + j] = 1
    c["flip"] = flip
    mq = np.zeros((P, TILES, MASKROWS), np.float32)
    mk = np.zeros((P, TILES, MASKROWS), np.float32)
    for t in range(TILES):
        for w in range(2):
            for r in range(8):
                for q in range(8):
                    p = w * WIN + r * 8 + q
                    cl = 2 * (t == 1 and r >= 4) + (w == 1 and q >= 4)
                    mq[p, t, 0], mk[p, t, 0] = 1, -100
                    mq[p, t, 1 + cl], mk[p, t, 1 + cl] = 1, 100
    c["mask_q"], c["mask_k"] = mq, mk
    d = np.arange(-7, 8, dtype=np.float32)
    tb = np.stack(np.meshgrid(d, d, indexing="ij"), axis=-1) / np.float32(7) * np.float32(8)
    tb = np.sign(tb) * np.log2(np.abs(tb) + np.float32(1)) / np.float32(3)
    c["table"] = np.ascontiguousarray(tb.reshape(REL, 2).T.astype(np.float32))
    q = np.arange(TOK)
    r = np.arange(SIDE)
    y = (q % SIDE)[None, :] - r[:, None]
    x = (q // SIDE)[None, :] - r[:, None]
    c["posc"] = np.ascontiguousarray(np.tile(np.stack([y, x], 1), (DG, 1, 1)).astype(np.float32))
    c["tri"] = np.ascontiguousarray(np.broadcast_to(np.tril(np.ones((EXPERTS, EXPERTS), np.float32), -1), (P, EXPERTS, EXPERTS)))
    return c


def _layout(a):
    import numpy as np

    row = lambda v: np.asarray(v).reshape(1, -1)
    cat = lambda *v: np.ascontiguousarray(np.concatenate(v, 0))
    T = lambda v: np.ascontiguousarray(np.asarray(v).T)
    L = {"x": np.ascontiguousarray(a["x"]).reshape(IMAGES * TOK, C)}
    L["cpb_w1"] = T(a["L0_conv_cpb_w1"])
    L["cpb_b1"] = np.ascontiguousarray(a["L0_conv_cpb_b1"]).reshape(P, 1)
    L["cpb_w2"] = T(a["L0_conv_cpb_w2"])
    L["lscale"] = np.ascontiguousarray(np.broadcast_to(row(a["L0_conv_logit_scale"]), (P, HEADS)))
    qb = np.array(a["L0_conv_qkv_b"]).reshape(1, -1)
    qb[:, C:2 * C] = 0
    L["wqkv"] = cat(T(a["L0_conv_qkv_w"]), qb)
    L["wproj"] = cat(T(a["L0_conv_proj_w"]), row(a["L0_conv_proj_b"]))
    L["w1"] = T(a["L0_ffn_W1"])
    L["b1"] = T(np.asarray(a["L0_ffn_b1"]).reshape(MT, P))
    L["w2"] = np.ascontiguousarray(np.asarray(a["L0_ffn_W2"]).T.reshape(MT, P, C).transpose(1, 0, 2))
    L["b2"] = np.ascontiguousarray(a["L0_ffn_b2"]).reshape(C, 1)
    L["wq"] = cat(a["L1_conv_w_q"], row(a["L1_conv_b_q"]))
    w0 = np.asarray(a["L1_conv_w_off0"]).reshape(9, GC, C)
    wc = np.zeros((C, 9, C), w0.dtype)
    wp = np.asarray(a["L1_conv_w_offp"])
    wf = np.zeros((C, 2, C), wp.dtype)
    for g in range(DG):
        s = slice(GC * g, GC * g + GC)
        wc[s, :, s] = w0[:, :, s].transpose(1, 0, 2)
        wf[s, 0, s] = np.broadcast_to(wp[:, 0:1], (GC, SIDE))
        wf[s, 1, s] = np.broadcast_to(wp[:, 1:2], (GC, SIDE))
    L["wconv"], L["woffp"] = wc, wf
    L["boff"] = np.ascontiguousarray(row(a["L1_conv_b_off0"]))
    L["lng"] = np.ascontiguousarray(np.broadcast_to(row(a["L1_conv_ln_g"]), (P, C)))
    L["lnb"] = np.ascontiguousarray(np.broadcast_to(row(a["L1_conv_ln_b"]), (P, C)))
    L["wkv"] = cat(np.concatenate([a["L1_conv_w_k"], a["L1_conv_w_v"]], 1),
                   np.concatenate([row(a["L1_conv_b_k"]), row(a["L1_conv_b_v"])], 1))
    L["wo"] = cat(a["L1_conv_w_o"], row(a["L1_conv_b_o"]))
    L["wg"] = cat(a["L1_ffn_gate_w"], row(a["L1_ffn_gate_b"]))
    w1 = np.asarray(a["L1_ffn_w1"]).transpose(1, 0, 2)
    L["we1"] = cat(w1, np.asarray(a["L1_ffn_b1"]).reshape(1, EXPERTS, HID))
    L["we2"] = np.ascontiguousarray(np.asarray(a["L1_ffn_w2"]).reshape(EXPERTS, MT, P, C).transpose(2, 0, 1, 3))
    L["be2"] = np.ascontiguousarray(row(a["L1_ffn_b2"]))
    return L


def kernel(**inputs):
    import numpy as _np
    import concourse.bacc as _bacc
    from concourse import mybir as _mybir
    from concourse.bass_utils import run_bass_kernel_spmd as _run

    nc = _bacc.Bacc("TRN2", target_bir_lowering=False, num_devices=1)
    given = {**_layout(inputs), **_constants()}
    arrays, aps = {}, {}
    for name, a in given.items():
        a = _np.ascontiguousarray(a)
        arrays[f"in_{name}"] = a
        aps[name] = nc.dram_tensor(f"in_{name}", a.shape, _mybir.dt.from_np(a.dtype), kind="ExternalInput").ap()
    out = nc.dram_tensor("out_0", (IMAGES * TOK, C), _mybir.dt.float32, kind="ExternalOutput").ap()
    build_program(nc, aps, out)
    r = _run(nc, [arrays], core_ids=[0])
    return _np.asarray(r.results[0]["out_0"]).reshape(IMAGES, SIDE, SIDE, C)
```

```python
from contextlib import ExitStack

import concourse.bass as bass
from concourse import mybir

F32 = mybir.dt.float32
BF16 = mybir.dt.bfloat16
ALU = mybir.AluOpType
ACT = mybir.ActivationFunctionType
AX = mybir.AxisListType
RMAX = bass.bass_isa.ReduceOp.max

P = 128
IMAGES = 16
SIDE = 16
TOK = SIDE * SIDE
TILES = TOK // P
C = 96
HEADS = 12
HD = C // HEADS
PAIRS = HEADS // 2
SLOT = 64
SPLIT = 6 * HD
MASKROWS = 5
MAXCOL = SPLIT + MASKROWS
FULL = MAXCOL + 3
WIN = 64
HID = 4 * C
MT = HID // P
GROUPS = 5
GIMG = IMAGES // GROUPS
QIMG = GROUPS * GIMG
EPSQ = 1e-5
QB = 128.0
LIM = QB - EPSQ
DG = 6
GC = C // DG
EXPERTS = 4
REL = 15 * 15
SHIFT = 4
ORDER_A = "bfbfbfbfbfbfbbbb"
ORDER_C = "bf" * 9 + "bf" * 9


def build_program(nc, A, out):
    ctx = ExitStack()
    with ctx:
        def sb(name, shape, dt=F32):
            return ctx.enter_context(nc.sbuf_tensor(name, shape, dt))

        ident = sb("ident", [P, P])
        identb = sb("identb", [P, P], BF16)
        perm_in = sb("perm_in", [P, P])
        perm_out = sb("perm_out", [P, P])
        flip = sb("flip", [WIN, P])
        mask_q = sb("mask_q", [P, TILES, MASKROWS])
        mask_k = sb("mask_k", [P, TILES, MASKROWS])
        table = sb("table", [2, REL])
        cpb_w1 = sb("cpb_w1", [2, P])
        cpb_b1 = sb("cpb_b1", [P, 1])
        cpb_w2 = sb("cpb_w2", [P, HEADS])
        lscale = sb("lscale", [P, HEADS])
        wqkv = sb("wqkv", [C + 1, 3 * C])
        wproj = sb("wproj", [C + 1, C])
        w1 = sb("w1", [C, HID])
        w1s = sb("w1s", [C, HID])
        b1 = sb("b1", [P, MT])
        w2 = sb("w2", [P, MT, C])
        w2s = sb("w2s", [P, MT, C])
        b2 = sb("b2", [C, 1])
        wq = sb("wq", [C + 1, C])
        wconv = sb("wconv", [C, 9, C])
        lng = sb("lng", [P, C])
        lnb = sb("lnb", [P, C])
        woffp = sb("woffp", [C, 2, C])
        posc = sb("posc", [C, 2, TOK])
        wkv = sb("wkv", [C + 1, 2 * C])
        wo = sb("wo", [C + 1, C])
        wg = sb("wg", [C + 1, EXPERTS])
        we1 = sb("we1", [C + 1, EXPERTS, HID])
        we2 = sb("we2", [P, EXPERTS, MT, C])
        be2 = sb("be2", [1, EXPERTS * C + C])
        bres = sb("bres", [1, EXPERTS * C + C])
        bpart = sb("bpart", [1, 3, EXPERTS * C + C], BF16)
        bias3 = sb("bias3", [3, EXPERTS * C + C], BF16)
        onesb = sb("onesb", [3, P], BF16)
        tri = sb("tri", [P, EXPERTS, EXPERTS])
        loads = [(ident, "ident"), (perm_in, "perm_in"), (perm_out, "perm_out"), (flip, "flip"),
                 (mask_q, "mask_q"), (mask_k, "mask_k"), (table, "table"), (cpb_w1, "cpb_w1"),
                 (cpb_b1, "cpb_b1"), (cpb_w2, "cpb_w2"), (lscale, "lscale"), (wqkv, "wqkv"),
                 (wproj, "wproj"), (w1, "w1"), (b1, "b1"), (w2, "w2"), (b2, "b2"), (wq, "wq"),
                 (wconv, "wconv"), (lng, "lng"), (lnb, "lnb"), (woffp, "woffp"),
                 (posc, "posc"), (wkv, "wkv"), (wo, "wo"), (wg, "wg"), (we1, "we1"), (we2, "we2"),
                 (be2, "be2"), (tri, "tri")]
        onesm = sb("onesm", [P, P])
        neghalf = sb("neghalf", [P, 2 * TILES * HEADS])
        hid_t = sb("hid_t", [P, REL])
        bt_sb = sb("bt_sb", [HEADS, REL])
        ebraw = sb("ebraw", [WIN, HEADS, WIN])
        ebz = sb("ebz", [P, HEADS, WIN])
        expbias = sb("expbias", [P, 2, PAIRS, WIN])
        wsum = sb("wsum", [P, GROUPS])
        wmean = sb("wmean", [P, 2, GROUPS])
        y1all = sb("y1all", [P, IMAGES, MT, TOK])
        y2all = sb("y2all", [C, IMAGES, TOK])
        gm1 = sb("gm1", [P, IMAGES])
        gm2 = sb("gm2", [P, IMAGES])
        gg = sb("gg", [P, 2, GROUPS])
        ggall = sb("ggall", [P, 2, GROUPS])
        gs = sb("gs", [P, 2, GROUPS])
        qs1 = sb("qs1", [P, IMAGES])
        qs2 = sb("qs2", [P, IMAGES])
        xraw = sb("xraw", [P, TILES, C])
        xin = sb("xin", [P, TILES, C])
        xkeep = sb("xkeep", [P, TILES, C])
        xres = sb("xres", [P, TILES, C])
        norms = {h: dict(stats=sb(h + "stats", [P, TILES, 6]), mv=sb(h + "mv", [P, TILES, 2]),
                         veps=sb(h + "veps", [P, TILES]), rstd=sb(h + "rstd", [P, TILES])) for h in "fb"}
        f_xn = sb("f_xn", [P, TILES, C])
        b_xn = sb("b_xn", [P, TILES, C])
        f_xnt = sb("f_xnt", [C + 1, TOK])
        b_xnt = sb("b_xnt", [C + 1, TOK])
        sq = sb("sq", [P, TILES, 2, HEADS, HD])
        ss = sb("ss", [P, TILES, 2 * HEADS])
        rn = sb("rn", [P, TILES, 2, HEADS])
        qk = sb("qk", [P, 2, TILES, HEADS, HD])
        res = sb("res", [P, 2, TILES, HEADS, HD])
        stack = sb("stack", [P, 2, TILES, HEADS, SLOT], BF16)
        stackt = sb("stackt", [P, 2, PAIRS, TOK], BF16)
        f_v = sb("f_v", [P, TILES, HEADS, HD])
        va = sb("va", [P, TILES, HEADS, 32])
        nm = sb("nm", [P, TILES, 2, PAIRS])
        nmr = sb("nmr", [P, TILES, 2, PAIRS])
        prob = sb("prob", [P, 2, 2, 2, TOK])
        ot = sb("ot", [P, 3, TOK])
        rec = sb("rec", [P, TILES, HEADS])
        on = sb("on", [P, TILES, C])
        ont = sb("ont", [C + 1, TOK])
        hb = sb("hb", [P, 3, MT, TOK])
        ycl = sb("ycl", [C, TOK])
        qpad = sb("qpad", [C, 3, SIDE + 2, SIDE])
        tn = sb("tn", [P, TILES, C])
        tnt = sb("tnt", [C, TOK])
        th = sb("th", [C, 2, TOK])
        hat = sb("hat", [C, 2, TOK])
        hatx = sb("hatx", [P, TILES, DG, SIDE])
        rows = sb("rows", [C, DG, SIDE, GC])
        samp = sb("samp", [P, 2, 2 * SIDE, GC])
        xs = sb("xs", [P, TILES, C])
        sc = sb("sc", [P, TILES, EXPERTS])
        scm = sb("scm", [P, TILES])
        scs = sb("scs", [P, TILES])
        gt = sb("gt", [P, TILES, EXPERTS, EXPERTS])
        eq = sb("eq", [P, TILES, EXPERTS, EXPERTS])
        acc = sb("acc", [P, TILES, C])

        ps = ctx.enter_context(nc.psum_tensor("ps", [P, 8, 512], F32))

        def bank_bf(b):
            return ps[:, b, 0:384].bitcast(BF16).rearrange("p (a c) -> p a c", c=P)

        def tiles(b, n):
            return ps[:, b, 0:TILES * n].rearrange("p (t c) -> p t c", c=n)

        x1_dram = nc.dram_tensor("x1_scratch", [IMAGES * TOK, C], F32).ap()
        xn_dram = nc.dram_tensor("xn_scratch", [TOK, C], F32).ap()
        bt_dram = nc.dram_tensor("bt_scratch", [HEADS, REL], F32).ap()

        class Signal:

            def __init__(self, name, n):
                self.sem = ctx.enter_context(nc.semaphore(name))
                self.n = n

            def at(self, i, k):
                return i * self.n + k

        made = {}

        def signals(prefix, owner, **counts):
            for k, n in counts.items():
                made[prefix + k] = (Signal(prefix + k, n), owner)

        def plain_sem(name):
            return ctx.enter_context(nc.semaphore(name))

        weights_in = plain_sem("weights_in")
        bt_dma = plain_sem("bt_dma")
        bias_dma = plain_sem("bias_dma")
        setup_dve = plain_sem("setup_dve")
        setup_pool = plain_sem("setup_pool")
        setup_pe = plain_sem("setup_pe")
        setup_act = plain_sem("setup_act")
        gam = [plain_sem(f"gamma{n}") for n in range(2)]
        gam_all = [plain_sem(f"gamma_all{n}") for n in range(2)]
        gam_ready = [plain_sem(f"gamma_ready{n}") for n in range(2)]
        own_sems = {k: plain_sem(k) for k in ("dve_f", "dve_b", "pool_f", "pool_b")}

        signals("a_", "sp", x_in=48, x1_out=48)
        signals("a_", "dve", var=1, xn=1, ss=1, qk=2, nm=2, on=2, x1=1, var2=1, xn2=1, gm=1)
        signals("a_", "pool", rstd=1, rn=1, keep=1, va=1, split=1, prob=2, rstd2=1)
        signals("a_", "act", xnt=1, sq=2, v=2, copies=1, qt_sb=2, kt_sb=2, q2t_sb=2, exp=2, ot=1, ont=1,
                x2t_sb=1, y1_sb=1)
        signals("a_", "pe", xt=1, qkv=2, qt=2, kt=2, s=2, q2t=2, st=2, pv=1, otr=2, ontp=1, proj=1,
                x2t=1, y1=1)
        signals("b_", "dve", cl=3, gm=3)
        signals("b_", "act", h=3, y2_sb=3)
        signals("b_", "pe", y2=3)
        signals("c_", "sp", x_in=16, xn_out=16, rows_in=16 * DG, out=16)
        signals("c_", "dve", ycl=1, xadd=1, var=1, xn=1, cvar=1, cn=1, hat=1, mul=6, xs=1, nm=6, parts=1,
                on=2, x3=1, var3=1, xn3=1, gsub=1, acc=1)
        signals("c_", "pool", rstd=1, crstd=1, keep=1, split=1, rstd3=1)
        signals("c_", "act", xnt=1, qpad=1, q_sb=1, cg=1, tnt=1, tanh=1, hatx=1, xst_sb=1, k_sb=1, v=1,
                copies=1, qt_sb=2, kt_sb=2, q2t_sb=2, exp=6, ot=3, ont=1, x3t_sb=1, gexp=1, h=4)
        signals("c_", "pe", yt=1, xt=1, qc=1, q=1, conv=1, tt=1, offs=1, hxt=1, t3=6, xst=1, kv=1,
                qt=2, kt=2, s=6, q2t=2, st=6, pv=6, otr=2, ontp=1, proj=1, x3t=1, gate=1, h1=4, y=1)

        def S(name):
            return made[name][0].sem

        def waits(eng, prefix, i):
            def w(name, k):
                sig = made[prefix + name][0]
                eng.wait_ge(sig.sem, sig.at(i, k))
            return w

        def prime(eng, who):
            for s, owner in made.values():
                if owner == who:
                    eng.sem_inc(s.sem, s.n)

        settled = {k: plain_sem("settled_" + k) for k in ("sp", "pool", "pe")}

        def settle(eng, who):
            eng.sem_inc(settled[who], 1)

        def weave(order, back, front):
            for c in order:
                next(back if c == "b" else front)
            for rest in (back, front):
                assert next(rest, "end") == "end", "stages left over"

        def run(stages, n):
            for k in range(n):
                next(stages)
            assert next(stages, "end") == "end"

        def run_pass(eng, order, front, back):
            run(front(1), order.count("f"))
            with eng.Fori(1, IMAGES) as i:
                weave(order, back(i), front(i + 1))
            run(back(IMAGES), order.count("b"))

        class Own:

            def __init__(self, eng, sem):
                self.eng, self.sem, self.n = eng, own_sems[sem], 0
                eng.sem_clear(self.sem)

            def mark(self, ins):
                ins.then_inc(self.sem, 1)
                self.n += 1
                return self.n

            def wait(self, n):
                self.eng.wait_ge(self.sem, n)

            def link(self, ins):
                self.wait(self.mark(ins))

        block = ctx.enter_context(nc.Block())
        ASETUP = 8
        DSETUP = 27

        @block.sync
        def _(sp):
            prime(sp, "sp")
            for t, name in loads:
                sp.dma_start(t[:], A[name]).then_inc(weights_in, 16)
            sp.wait_ge(setup_act, 2)
            sp.dma_start(bt_dram, bt_sb[:, :]).then_inc(bt_dma, 16)
            sp.wait_ge(bt_dma, 16)
            for rj in range(8):
                for cj in range(8):
                    src = bt_dram.rearrange("h (r c) -> h r c", c=15)[:, rj:rj + 8, cj:cj + 8]
                    sp.dma_start(ebraw[rj * 8 + cj:rj * 8 + cj + 1, :, :], src).then_inc(bt_dma, 16)
            sp.wait_ge(setup_dve, DSETUP)
            for k in range(3):
                sp.dma_start(bias3[k:k + 1, :], bpart[:, k, :]).then_inc(bias_dma, 16)
            cut = TOK - SHIFT * SIDE - P

            def shifted(i):
                base = (i - 1) * TOK
                return ((bass.ds(base + SHIFT * SIDE, P), 0, slice(0, P)),
                        (bass.ds(base + SHIFT * SIDE + P, cut), 1, slice(0, cut)),
                        (bass.ds(base, P - cut), 1, slice(cut, P)))

            def front_a(i):
                w = waits(sp, "a_", i)
                w("keep", 0)
                settle(sp, "sp")
                for rows_, t, part in shifted(i):
                    sp.dma_start(xin[part, t, :], A["x"][rows_, :]).then_inc(S("a_x_in"), 16)
                for _ in range(ORDER_A.count("f")):
                    yield

            def back_a(i):
                w = waits(sp, "a_", i)
                for _ in range(8):
                    yield
                w("x1", 1)
                settle(sp, "sp")
                for rows_, t, part in shifted(i):
                    sp.dma_start(x1_dram[rows_, :], xres[part, t, :]).then_inc(S("a_x1_out"), 16)
                for _ in range(2):
                    yield

            run_pass(sp, ORDER_A, front_a, back_a)
            sp.wait_ge(S("a_x1_out"), (IMAGES + 1) * 48)
            sp.wait_ge(gam_ready[1], 1)

            def front_c(i):
                w = waits(sp, "c_", i)
                base = (i - 1) * TOK
                w("xadd", 0)
                settle(sp, "sp")
                sp.dma_start(xraw[:, :, :], x1_dram[bass.ds(base, TOK), :].rearrange("(t p) c -> p t c", p=P)).then_inc(S("c_x_in"), 16)
                yield
                w("xn", 1)
                sp.dma_start(xn_dram.rearrange("(t p) c -> p t c", p=P), f_xn[:, :, :]).then_inc(S("c_xn_out"), 16)
                w("xn_out", 16)
                for g in range(DG):
                    src = xn_dram.rearrange("(r c) (g k) -> r c g k", c=SIDE, g=DG)[:, :, g, :]
                    sp.dma_start(rows[GC * g:GC * g + SIDE, g, :, :], src).then_inc(S("c_rows_in"), 16)
                for _ in range(ORDER_C.count("f") - 1):
                    yield

            def back_c(i):
                w = waits(sp, "c_", i)
                base = (i - 1) * TOK
                for _ in range(ORDER_C.count("b") - 1):
                    yield
                w("acc", 1)
                settle(sp, "sp")
                sp.dma_start(out[bass.ds(base, TOK), :].rearrange("(t p) c -> p t c", p=P), acc[:, :, :]).then_inc(S("c_out"), 16)
                yield

            run_pass(sp, ORDER_C, front_c, back_c)
            sp.wait_ge(S("c_out"), (IMAGES + 1) * 16)

        @block.gpsimd
        def _(pool):
            g = nc.gpsimd
            prime(pool, "pool")

            def setup(ins):
                ins.then_inc(setup_pool, 1)

            setup(g.memset(onesm[:], 1.0))
            setup(g.memset(neghalf[:], -0.5))
            setup(g.memset(stack[:], 0.0))
            setup(g.memset(va[:], 0.0))
            setup(g.memset(rows[:], 0.0))
            setup(g.memset(qpad[:], 0.0))
            setup(g.memset(y2all[:], 0.0))
            setup(g.memset(onesb[:], 1.0))
            pool.wait_ge(weights_in, 16 * len(loads))
            pool.wait_ge(setup_pool, 8)
            for t in range(TILES):
                for a, m in ((0, mask_q), (1, mask_k)):
                    setup(g.tensor_copy(stack[:, a, t, :, SPLIT:MAXCOL],
                                        m[:, t:t + 1, :].to_broadcast([P, HEADS, MASKROWS])))
            setup(g.memset(stack[:, 1, :, :, MAXCOL:FULL].rearrange("p t h c -> p (t h) c"), 1.0))
            setup(g.memset(va[:, :, :, HD:HD + 1], 1.0))
            pool.wait_ge(setup_pool, 14)

            def power(half, ready):
                n = norms[half]
                g.tensor_tensor(n["rstd"][:], n["veps"][:], neghalf[:, 0:TILES], ALU.pow).then_inc(S(ready), 1)

            def split(own, ready):
                flat = lambda v: v.rearrange("p a t h c -> p (a t h) c")
                one = lambda v, a: v[:, a].rearrange("p t h c -> p (t h) c")
                st, rs = flat(stack[:]), flat(res[:])
                src = flat(qk[:])
                own.link(g.tensor_copy(st[:, :, 0:HD], src))
                own.link(g.tensor_tensor(rs, src, st[:, :, 0:HD], ALU.subtract))
                own.link(g.tensor_copy(st[:, :, HD:2 * HD], rs))
                q, k, rq, rk = one(stack, 0), one(stack, 1), one(res, 0), one(res, 1)
                own.mark(g.tensor_tensor(q[:, :, 2 * HD:3 * HD], rq, q[:, :, HD:2 * HD], ALU.subtract))
                own.mark(g.tensor_tensor(k[:, :, 5 * HD:6 * HD], rk, k[:, :, HD:2 * HD], ALU.subtract))
                own.mark(g.tensor_copy(q[:, :, 4 * HD:5 * HD], rq))
                own.wait(own.n)
                g.tensor_copy(k[:, :, 3 * HD:4 * HD], rk).then_inc(ready, 1)

            def front_a(i):
                w = waits(pool, "a_", i)
                own = Own(pool, "pool_f")
                w("var", 1)
                power("f", "a_rstd")
                yield
                yield
                w("ss", 1)
                g.tensor_tensor(rn[:].rearrange("p t a h -> p (t a h)"), ss[:].rearrange("p t h -> p (t h)"),
                                neghalf[:, 0:2 * TILES * HEADS], ALU.pow).then_inc(S("a_rn"), 1)
                yield
                yield
                w("qk", 2)
                w("q2t", 0)
                settle(pool, "pool")
                split(own, S("a_split"))
                yield
                yield

            def back_a(i):
                w = waits(pool, "a_", i)
                w("x1", 0)
                w("pv", 0)
                w("v", 2)
                settle(pool, "pool")
                g.tensor_copy(xkeep[:], xin[:]).then_inc(S("a_keep"), 1)
                g.tensor_copy(va[:, :, :, 0:HD], f_v[:]).then_inc(S("a_va"), 1)
                yield
                yield
                yield
                yield
                for t in range(TILES):
                    w("exp", t + 1)
                    pv = prob[:, t].rearrange("p a b c -> p (a b c)")[:, 0:HEADS * WIN]
                    g.tensor_tensor(pv, pv, expbias[:].rearrange("p a b c -> p (a b c)"), ALU.mult).then_inc(S("a_prob"), 1)
                yield
                yield
                yield
                yield
                w("var2", 1)
                power("b", "a_rstd2")
                yield
                yield

            run_pass(pool, ORDER_A, front_a, back_a)

            pool.wait_ge(gam[0], 1)
            g.partition_all_reduce(ggall[:, 0], gg[:, 0], P, RMAX).then_inc(gam_all[0], 1)
            pool.wait_ge(gam[1], 1)
            g.partition_all_reduce(ggall[:, 1], gg[:, 1], P, RMAX).then_inc(gam_all[1], 1)
            g.memset(stack[:, :, :, :, SPLIT:MAXCOL], 0.0).then_inc(setup_pool, 1)
            pool.wait_ge(setup_pool, 15)

            def front_c(i):
                w = waits(pool, "c_", i)
                own = Own(pool, "pool_f")
                w("var", 1)
                power("f", "c_rstd")
                yield
                yield
                yield
                w("cvar", 1)
                power("f", "c_crstd")
                yield
                yield
                yield
                yield
                for _ in range(6):
                    yield
                yield
                yield
                w("k_sb", 1)
                w("q_sb", 1)
                w("q2t", 0)
                settle(pool, "pool")
                split(own, S("c_split"))
                yield
                yield
                yield

            def back_c(i):
                w = waits(pool, "c_", i)
                w("x3", 0)
                settle(pool, "pool")
                g.tensor_copy(xkeep[:], xin[:]).then_inc(S("c_keep"), 1)
                for _ in range(12):
                    yield
                w("var3", 1)
                power("b", "c_rstd3")
                for _ in range(6):
                    yield

            run_pass(pool, ORDER_C, front_c, back_c)

        @block.vector
        def _(dve):
            import math
            v = nc.vector
            prime(dve, "dve")
            dve.wait_ge(weights_in, 16 * len(loads))
            dve.wait_ge(setup_pool, 8)
            n = [0]

            def setup(ins):
                ins.then_inc(setup_dve, 1)
                n[0] += 1
                dve.wait_ge(setup_dve, n[0])

            setup(v.tensor_copy(identb[:], ident[:]))
            setup(v.memset(f_xnt[C:C + 1, :], 1.0))
            setup(v.memset(b_xnt[C:C + 1, :], 1.0))
            setup(v.memset(ont[C:C + 1, :], 1.0))
            setup(v.memset(gm2[:], 0.0))
            setup(v.tensor_reduce(wsum[0:C, :], w1[:, 0:GROUPS * (HID // GROUPS)].rearrange("p (g n) -> p g n", g=GROUPS), AX.X, ALU.add))
            dve.wait_ge(setup_pe, 1)
            setup(v.tensor_scalar(wmean[0:C, 0, :], ps[0:C, 0, 0:GROUPS], 1.0 / (HID // GROUPS * C), None, ALU.mult))
            gw = C // GROUPS
            w2g = w2[:, :, 0:GROUPS * gw].rearrange("p m (g n) -> p g m n", g=GROUPS)
            setup(v.tensor_reduce(wsum[:, :], w2g, AX.XY, ALU.add))
            dve.wait_ge(setup_pe, 2)
            setup(v.tensor_scalar(wmean[:, 1, :], ps[:, 0, 0:GROUPS], 1.0 / (gw * HID), None, ALU.mult))
            setup(v.memset(w1s[:], 0.0))
            setup(v.memset(w2s[:], 0.0))
            g1 = HID // GROUPS
            for g in range(GROUPS):
                v.tensor_scalar(w1s[:, g1 * g:g1 * (g + 1)], w1[:, g1 * g:g1 * (g + 1)], wmean[0:C, 0, g:g + 1], None, ALU.subtract).then_inc(setup_dve, 1)
                v.tensor_scalar(w2s[:, :, gw * g:gw * (g + 1)], w2[:, :, gw * g:gw * (g + 1)], wmean[:, 1, g:g + 1], None, ALU.subtract).then_inc(setup_dve, 1)
            n[0] += 2 * GROUPS
            setup(v.tensor_copy(bpart[:, 0, :], be2[:]))
            setup(v.tensor_tensor(bres[:], be2[:], bpart[:, 0, :], ALU.subtract))
            setup(v.tensor_copy(bpart[:, 1, :], bres[:]))
            setup(v.tensor_tensor(bpart[:, 2, :], bres[:], bpart[:, 1, :], ALU.subtract))
            dve.wait_ge(setup_act, 4)
            setup(v.tensor_scalar(ebz[:], ebz[:], 8.0, 8.0, ALU.mult, ALU.add))
            setup(v.tensor_scalar(lscale[:], lscale[:], math.log(100.0), None, ALU.min))
            assert n[0] == DSETUP

            def norm(half, own, srcs, eps, ready):
                n = norms[half]
                for t in range(TILES):
                    own.mark(v.bn_stats(n["stats"][:, t, :], srcs[t]))
                own.wait(own.n)
                for t in range(TILES):
                    own.mark(v.bn_aggr(n["mv"][:, t, :], n["stats"][:, t, :]))
                own.wait(own.n)
                v.tensor_scalar(n["veps"][:], n["mv"][:, :, 1], eps, None, ALU.add).then_inc(S(ready), 1)

            def normed(half, dst, srcs):
                n = norms[half]
                for t in range(TILES):
                    ins = v.tensor_scalar(dst[:, t, :], srcs[t], n["mv"][:, t, 0:1], n["rstd"][:, t:t + 1], ALU.subtract, ALU.mult)
                return ins

            def both(v_):
                return [v_[:, t, :] for t in range(TILES)]

            def negmax_parts(own, t):
                sv = stack[:, 0, t].rearrange("p (b a) c -> p a b c", a=2)
                own.link(v.tensor_copy(sv[:, :, :, MAXCOL], nm[:, t]))
                own.link(v.tensor_tensor(nmr[:, t], nm[:, t], sv[:, :, :, MAXCOL], ALU.subtract))
                own.link(v.tensor_copy(sv[:, :, :, MAXCOL + 1], nmr[:, t]))
                return v.tensor_tensor(sv[:, :, :, MAXCOL + 2], nmr[:, t], sv[:, :, :, MAXCOL + 1], ALU.subtract)

            def divide(own, t, bank):
                o = ps[:, bank, 0:384].rearrange("p (h c) -> p h c", c=32)
                own.link(v.reciprocal(rec[:, t, :], o[:, :, HD]))
                return v.tensor_tensor(on[:, t].rearrange("p (h c) -> p h c", c=HD), o[:, :, 0:HD],
                                       rec[:, t, :].to_broadcast([P, HEADS, HD]), ALU.mult)

            dve.wait_ge(setup_act, ASETUP)

            def front_a(i):
                w = waits(dve, "a_", i)
                own = Own(dve, "dve_f")
                w("x_in", 48)
                norm("f", own, both(xin), 1e-6, "a_var")
                w("rstd", 1)
                normed("f", f_xn, both(xin)).then_inc(S("a_xn"), 1)
                yield
                yield
                w("sq", 2)
                own.link(v.tensor_reduce(ss[:], sq[:].rearrange("p t a h c -> p t (a h) c"), AX.X, ALU.add))
                v.tensor_scalar(ss[:], ss[:], 1e-24, None, ALU.max).then_inc(S("a_ss"), 1)
                yield
                w("rn", 1)
                for t in range(TILES):
                    own.link(v.tensor_tensor(rn[:, t, 0, :], rn[:, t, 0, :], lscale[:], ALU.mult))
                w("split", 0)
                w("copies", 0)
                for t in range(TILES):
                    w("v", t + 1)
                    v.tensor_tensor(qk[:, :, t], ps[:, t, 0:2 * C].rearrange("p (a h c) -> p a h c", a=2, c=HD),
                                    rn[:, t].to_broadcast([P, 2, HEADS, HD]), ALU.mult).then_inc(S("a_qk"), 1)
                yield
                yield
                yield

            def back_a(i):
                w = waits(dve, "a_", i)
                own = Own(dve, "dve_b")
                yield
                for t in range(TILES):
                    w("s", t + 1)
                    own.link(v.tensor_reduce(nm[:, t], ps[:, 4 + 2 * t:6 + 2 * t, 0:PAIRS * WIN].rearrange("p a (b n) -> p a b n", n=WIN),
                                             AX.X, ALU.max, negate=True))
                    negmax_parts(own, t).then_inc(S("a_nm"), 1)
                yield
                yield
                yield
                yield
                for t in range(TILES):
                    w("otr", t + 1)
                    divide(own, t, 4 + 2 * t).then_inc(S("a_on"), 1)
                yield
                yield
                w("x1_out", 0)
                w("keep", 1)
                w("proj", 1)
                v.tensor_tensor(xres[:], xkeep[:], tiles(7, C), ALU.add).then_inc(S("a_x1"), 1)
                yield
                w("x1", 1)
                norm("b", own, both(xres), 1e-5, "a_var2")
                w("rstd2", 1)
                normed("b", b_xn, both(xres)).then_inc(S("a_xn2"), 1)
                yield
                w("y1_sb", 1)
                v.tensor_reduce(gm1[:, bass.ds(i - 1, 1)], y1all[:, bass.ds(i - 1, 1)].rearrange("p a m n -> p (a m n)"),
                                AX.X, ALU.max, apply_absolute_value=True).then_inc(S("a_gm"), 1)
                yield

            run_pass(dve, ORDER_A, front_a, back_a)

            def gammas(n, gm, qs):
                v.tensor_reduce(gg[:, n], gm[:, 0:QIMG].rearrange("p (g n) -> p g n", n=GIMG), AX.X, ALU.max).then_inc(gam[n], 1)
                own = Own(dve, "dve_f")
                dve.wait_ge(gam_all[n], 1)
                own.link(v.tensor_scalar(gs[:, n], ggall[:, n], EPSQ, None, ALU.add))
                own.link(v.reciprocal(gs[:, n], gs[:, n]))
                own.link(v.tensor_scalar(gs[:, n], gs[:, n], QB, None, ALU.mult))
                own.link(v.memset(qs[:], 0.0))
                v.tensor_copy(qs[:, 0:QIMG].rearrange("p (g n) -> p g n", n=GIMG),
                              gs[:, n].to_broadcast([P, GROUPS, GIMG])).then_inc(gam_ready[n], 1)
                dve.wait_ge(gam_ready[n], 1)

            dve.wait_ge(S("a_gm"), IMAGES + 1)
            gammas(0, gm1, qs1)
            with dve.Fori(1, GROUPS + 1) as i:
                own = Own(dve, "dve_f")
                w = waits(dve, "b_", i)
                for u in range(GIMG):
                    img = bass.ds((i - 1) * GIMG + u, 1)
                    h0 = hb[:, u].rearrange("p m n -> p (m n)")
                    if u == 0:
                        w("y2", 0)
                    own.link(v.tensor_scalar(h0, y1all[:, img].rearrange("p a m n -> p (a m n)"), qs1[:, img], LIM, ALU.mult, ALU.min))
                    v.tensor_scalar(h0, h0, -LIM, None, ALU.max).then_inc(S("b_cl"), 1)
                for u in range(GIMG):
                    img = bass.ds((i - 1) * GIMG + u, 1)
                    w("y2_sb", u + 1)
                    v.tensor_reduce(gm2[0:C, img], y2all[:, img, :].rearrange("p a n -> p (a n)"),
                                    AX.X, ALU.max, apply_absolute_value=True).then_inc(S("b_gm"), 1)
            dve.wait_ge(S("b_gm"), (GROUPS + 1) * GIMG)
            gammas(1, gm2, qs2)

            def front_c(i):
                w = waits(dve, "c_", i)
                own = Own(dve, "dve_f")
                own.link(v.tensor_scalar(ycl[:], y2all[:, bass.ds(i - 1, 1), :].rearrange("p a n -> p (a n)"),
                                         qs2[0:C, bass.ds(i - 1, 1)], LIM, ALU.mult, ALU.min))
                v.tensor_scalar(ycl[:], ycl[:], -LIM, None, ALU.max).then_inc(S("c_ycl"), 1)
                w("x_in", 16)
                w("keep", 0)
                w("yt", 1)
                v.tensor_tensor(xin[:], xraw[:], tiles(0, C), ALU.add).then_inc(S("c_xadd"), 1)
                w("xadd", 1)
                norm("f", own, both(xin), 1e-6, "c_var")
                w("rstd", 1)
                normed("f", f_xn, both(xin)).then_inc(S("c_xn"), 1)
                yield
                yield
                yield
                w("conv", 1)
                norm("f", own, both(tiles(0, C)), 1e-3, "c_cvar")
                w("crstd", 1)
                own.link(normed("f", tn, both(tiles(0, C))))
                row = lambda x: x[:, :].rearrange("p (a c) -> p a c", a=1).to_broadcast([P, TILES, C])
                own.link(v.tensor_tensor(tn[:], tn[:], row(lng), ALU.mult))
                v.tensor_tensor(tn[:], tn[:], row(lnb), ALU.add).then_inc(S("c_cn"), 1)
                yield
                yield
                w("tanh", 1)
                flat = lambda x: x[:].rearrange("p a n -> p (a n)")
                own.link(v.scalar_tensor_tensor(flat(th), flat(th), SIDE / 2.0, flat(posc), ALU.mult, ALU.add))
                own.link(v.scalar_tensor_tensor(flat(hat), flat(th), -1.0, flat(th), ALU.mult, ALU.min))
                v.tensor_scalar(flat(hat), flat(hat), 1.0, 0.0, ALU.add, ALU.max).then_inc(S("c_hat"), 1)
                yield
                yield
                for k in range(6):
                    t, b = k // 3, k % 3
                    if k == 0:
                        w("hatx", 1)
                    w("t3", k + 1)
                    hx = hatx[:, t, 2 * b:2 * b + 2, :].rearrange("p g c -> p (g c)")
                    v.tensor_tensor(samp[:, k % 2], ps[:, k % 2, :].rearrange("p (a c) -> p a c", c=GC),
                                    hx.to_broadcast([P, 2 * SIDE, GC]), ALU.mult).then_inc(S("c_mul"), 1)
                    w("mul", k + 1)
                    ins = v.tensor_reduce(xs[:, t, 2 * GC * b:2 * GC * (b + 1)].rearrange("p (g k) -> p g k", g=2),
                                          samp[:, k % 2].rearrange("p (g c) k -> p g k c", g=2), AX.X, ALU.add)
                    if k == 5:
                        ins.then_inc(S("c_xs"), 1)
                    else:
                        own.link(ins)
                    yield
                yield
                yield
                yield
                yield
                yield

            def back_c(i):
                w = waits(dve, "c_", i)
                own = Own(dve, "dve_b")
                yield
                for u in range(6):
                    t, pq = u // 3, u % 3
                    w("s", u + 1)
                    bk = 4 + 2 * (u % 2)
                    v.tensor_reduce(nm[:, t, :, 2 * pq:2 * pq + 2], ps[:, bk:bk + 2, :].rearrange("p a (b n) -> p a b n", n=TOK),
                                    AX.X, ALU.max, negate=True).then_inc(S("c_nm"), 1)
                    if u % 2:
                        yield
                w("nm", 6)
                own.link(negmax_parts(own, 0))
                negmax_parts(own, 1).then_inc(S("c_parts"), 1)
                yield
                for u in range(3):
                    yield
                yield
                for t in range(TILES):
                    w("otr", t + 1)
                    divide(own, t, 4 + t).then_inc(S("c_on"), 1)
                yield
                yield
                w("keep", 1)
                w("proj", 1)
                w("acc", 0)
                v.tensor_tensor(xres[:], xkeep[:], tiles(7, C), ALU.add).then_inc(S("c_x3"), 1)
                yield
                w("x3", 1)
                norm("b", own, both(xres), 1e-5, "c_var3")
                w("rstd3", 1)
                normed("b", b_xn, both(xres)).then_inc(S("c_xn3"), 1)
                yield
                w("gate", 1)
                own.link(v.tensor_copy(sc[:], tiles(3, EXPERTS)))
                own.link(v.tensor_reduce(scm[:], sc[:], AX.X, ALU.max))
                v.tensor_tensor(sc[:], sc[:], scm[:].to_broadcast([P, TILES, EXPERTS]), ALU.subtract).then_inc(S("c_gsub"), 1)
                yield
                w("gexp", 1)
                own.link(v.tensor_reduce(scs[:], sc[:], AX.X, ALU.add))
                own.link(v.reciprocal(scs[:], scs[:]))
                own.link(v.tensor_tensor(sc[:], sc[:], scs[:].to_broadcast([P, TILES, EXPERTS]), ALU.mult))
                for t in range(TILES):
                    other = sc[:, t:t + 1, :].to_broadcast([P, EXPERTS, EXPERTS])
                    mine = sc[:, t, :].to_broadcast([P, EXPERTS, EXPERTS])
                    own.mark(v.tensor_tensor(gt[:, t], other, mine, ALU.is_gt))
                    own.mark(v.tensor_tensor(eq[:, t], other, mine, ALU.is_equal))
                own.wait(own.n)
                for t in range(TILES):
                    own.mark(v.tensor_tensor(eq[:, t], eq[:, t], tri[:], ALU.mult))
                own.wait(own.n)
                own.link(v.tensor_tensor(gt[:], gt[:], eq[:], ALU.add))
                own.link(v.tensor_reduce(eq[:, :, :, 0], gt[:], AX.X, ALU.add))
                own.link(v.tensor_scalar(eq[:, :, :, 0], eq[:, :, :, 0], 1.5, None, ALU.is_lt))
                own.link(v.tensor_tensor(sc[:], sc[:], eq[:, :, :, 0], ALU.mult))
                own.link(v.tensor_reduce(scs[:], sc[:], AX.X, ALU.add))
                own.link(v.tensor_scalar(scs[:], scs[:], 1e-9, None, ALU.add))
                own.link(v.reciprocal(scs[:], scs[:]))
                own.link(v.tensor_tensor(sc[:], sc[:], scs[:].to_broadcast([P, TILES, EXPERTS]), ALU.mult))
                yield
                yield
                yield
                w("out", 0)
                w("y", 1)
                for e in range(EXPERTS):
                    src = acc if e else xres
                    for t in range(TILES):
                        ins = v.scalar_tensor_tensor(acc[:, t, :], ps[:, 2 + t, C * e:C * e + C], sc[:, t, e:e + 1],
                                                     src[:, t, :], ALU.mult, ALU.add)
                        if e < EXPERTS - 1:
                            own.mark(ins)
                    if e < EXPERTS - 1:
                        own.wait(own.n)
                    else:
                        ins.then_inc(S("c_acc"), 1)
                yield

            run_pass(dve, ORDER_C, front_c, back_c)

        @block.scalar
        def _(act):
            a = nc.scalar
            prime(act, "act")
            n = [0]

            def setup(ins):
                ins.then_inc(setup_act, 1)
                n[0] += 1
                act.wait_ge(setup_act, n[0])

            act.wait_ge(setup_pe, 3)
            setup(a.activation(hid_t[:], ps[:, 1, 0:REL], ACT.Relu, bias=cpb_b1[:, 0:1]))
            act.wait_ge(setup_pe, 4)
            setup(a.copy(bt_sb[:], ps[0:HEADS, 2, 0:REL]))
            act.wait_ge(setup_pe, 5)
            setup(a.activation(ebz[:, 0:6], ps[:, 3, 0:384].rearrange("p (h n) -> p h n", n=WIN), ACT.Tanh, scale=0.5))
            setup(a.activation(ebz[:, 6:12], ps[:, 4, 0:384].rearrange("p (h n) -> p h n", n=WIN), ACT.Tanh, scale=0.5))
            act.wait_ge(setup_dve, DSETUP)
            setup(a.activation(expbias[:], ebz[:].rearrange("p (b a) n -> p a b n", a=2), ACT.Exp))
            setup(a.activation(lscale[:], lscale[:], ACT.Exp))
            setup(a.activation(w1s[:], w1s[:], ACT.Sign))
            setup(a.activation(w2s[:], w2s[:], ACT.Sign))

            act.wait_ge(setup_pool, 14)

            def copies(ready):
                for x, b in ((0, 3), (1, 2)):
                    d = stack[:, x].rearrange("p t h c -> p (t h) c")
                    s_ = qk[:, x].rearrange("p t h c -> p (t h) c")
                    a.copy(d[:, :, HD * b:HD * b + HD], s_)
                    ins = a.copy(d[:, :, HD * (b + 2):HD * (b + 2) + HD], s_)
                ins.then_inc(ready, 1)

            def turned(w, sig, k, x, t, bank):
                w(sig, k)
                return a.copy(stackt[:, x, :, P * t:P * t + P], bank_bf(bank))

            def front_a(i):
                w = waits(act, "a_", i)
                yield
                w("xt", 1)
                a.copy(f_xnt[0:C, :], ps[0:C, 0, 0:TOK]).then_inc(S("a_xnt"), 1)
                yield
                for t in range(TILES):
                    w("qkv", t + 1)
                    a.activation(sq[:, t].rearrange("p a h c -> p (a h c)"), ps[:, t, 0:2 * C], ACT.Square).then_inc(S("a_sq"), 1)
                w("va", 0)
                for t in range(TILES):
                    a.copy(f_v[:, t].rearrange("p h c -> p (h c)"), ps[:, t, 2 * C:3 * C]).then_inc(S("a_v"), 1)
                yield
                yield
                w("q2t", 0)
                w("qk", 2)
                copies(S("a_copies"))
                yield
                yield

            def back_a(i):
                w = waits(act, "a_", i)
                for t in range(TILES):
                    turned(w, "qt", t + 1, 0, t, 2 + t).then_inc(S("a_qt_sb"), 1)
                    turned(w, "kt", t + 1, 1, t, 4 + 2 * t).then_inc(S("a_kt_sb"), 1)
                yield
                yield
                for t in range(TILES):
                    turned(w, "q2t", t + 1, 0, t, 2 + t).then_inc(S("a_q2t_sb"), 1)
                yield
                for t in range(TILES):
                    w("st", t + 1)
                    pv = prob[:, t].rearrange("p a b c -> p (a b c)")[:, 0:HEADS * WIN]
                    a.activation(pv.rearrange("p (a n) -> p a n", a=2), ps[:, 4 + 2 * t:6 + 2 * t, 0:PAIRS * WIN], ACT.Exp).then_inc(S("a_exp"), 1)
                yield
                w("pv", 1)
                for k in range(2):
                    ins = a.copy(ot[:].rearrange("p s (t w n) -> p t s w n", t=TILES, w=2)[:, :, :, k, :],
                                 ps[:, 2 + k, 0:TILES * 3 * WIN].rearrange("p (t s n) -> p t s n", t=TILES, n=WIN))
                ins.then_inc(S("a_ot"), 1)
                yield
                yield
                w("ontp", 1)
                a.copy(ont[0:C, :], ps[0:C, 5, 0:TOK]).then_inc(S("a_ont"), 1)
                yield
                yield
                w("x2t", 1)
                a.copy(b_xnt[0:C, :], ps[0:C, 2, 0:TOK]).then_inc(S("a_x2t_sb"), 1)
                yield
                w("y1", 1)
                for m in range(MT):
                    ins = a.activation(y1all[:, bass.ds(i - 1, 1), m, :].rearrange("p a n -> p (a n)"),
                                       ps[:, 4 + m // 2, TOK * (m % 2):TOK * (m % 2) + TOK], ACT.Identity, bias=b1[:, m:m + 1])
                ins.then_inc(S("a_y1_sb"), 1)
                yield

            run_pass(act, ORDER_A, front_a, back_a)

            with act.Fori(1, GROUPS + 1) as i:
                w = waits(act, "b_", i)
                k = SHIFT * SIDE
                for u in range(GIMG):
                    h0 = hb[:, u].rearrange("p m n -> p (m n)")
                    w("cl", u + 1)
                    a.activation(h0, h0, ACT.Gelu).then_inc(S("b_h"), 1)
                for u in range(GIMG):
                    img = bass.ds((i - 1) * GIMG + u, 1)
                    w("y2", u + 1)
                    a.activation(y2all[:, img, k:TOK].rearrange("p a n -> p (a n)"), ps[0:C, u, 0:TOK - k], ACT.Identity, bias=b2[:, 0:1])
                    a.activation(y2all[:, img, 0:k].rearrange("p a n -> p (a n)"), ps[0:C, u, TOK - k:TOK], ACT.Identity,
                                 bias=b2[:, 0:1]).then_inc(S("b_y2_sb"), 1)

            def front_c(i):
                w = waits(act, "c_", i)
                yield
                w("xt", 1)
                a.copy(f_xnt[0:C, :], ps[0:C, 1, 0:TOK]).then_inc(S("c_xnt"), 1)
                yield
                w("qc", 1)
                qc = ps[0:C, 0, 0:TOK].rearrange("p (r c) -> p r c", c=SIDE)
                a.copy(qpad[:, 0, 1:1 + SIDE, 1:SIDE], qc[:, :, 0:SIDE - 1])
                a.copy(qpad[:, 1, 1:1 + SIDE, :], qc)
                a.copy(qpad[:, 2, 1:1 + SIDE, 0:SIDE - 1], qc[:, :, 1:SIDE]).then_inc(S("c_qpad"), 1)
                w("split", 0)
                w("q", 1)
                a.copy(qk[:, 0].rearrange("p t h c -> p (t h c)"), ps[:, 1, 0:TILES * C]).then_inc(S("c_q_sb"), 1)
                yield
                w("cn", 1)
                a.activation(tn[:], tn[:], ACT.Gelu).then_inc(S("c_cg"), 1)
                yield
                w("tt", 1)
                a.copy(tnt[:, :], ps[0:C, 1, 0:TOK]).then_inc(S("c_tnt"), 1)
                yield
                w("offs", 1)
                a.activation(th[:].rearrange("p a n -> p (a n)"), ps[0:C, 0, :], ACT.Tanh).then_inc(S("c_tanh"), 1)
                yield
                w("hxt", 1)
                a.copy(hatx[:].rearrange("p t g c -> p (t g c)"), ps[:, 1, 0:2 * C]).then_inc(S("c_hatx"), 1)
                yield
                for _ in range(6):
                    yield
                w("xst", 1)
                a.copy(f_xnt[0:C, :], ps[0:C, 0, 0:TOK]).then_inc(S("c_xst_sb"), 1)
                yield
                w("kv", 1)
                w("pv", 0)
                kv = tiles(1, 2 * C)
                a.copy(qk[:, 1].rearrange("p t h c -> p t (h c)"), kv[:, :, 0:C]).then_inc(S("c_k_sb"), 1)
                a.copy(va[:, :, :, 0:HD], kv[:, :, C:2 * C].rearrange("p t (h c) -> p t h c", c=HD)).then_inc(S("c_v"), 1)
                yield
                w("q2t", 0)
                w("k_sb", 1)
                copies(S("c_copies"))
                yield
                yield
                yield

            def back_c(i):
                w = waits(act, "c_", i)
                for t in range(TILES):
                    turned(w, "qt", t + 1, 0, t, 2 + t).then_inc(S("c_qt_sb"), 1)
                    turned(w, "kt", t + 1, 1, t, 4 + 2 * t).then_inc(S("c_kt_sb"), 1)
                yield
                for u in range(3):
                    yield
                for t in range(TILES):
                    turned(w, "q2t", t + 1, 0, t, 2 + t).then_inc(S("c_q2t_sb"), 1)
                yield
                for u in range(6):
                    w("st", u + 1)
                    if u >= 2:
                        w("pv", u - 1)
                    bk = 4 + 2 * (u % 2)
                    a.activation(prob[:, u % 2].rearrange("p a b n -> p a (b n)"), ps[:, bk:bk + 2, :], ACT.Exp, scale=float(HD) ** -0.5).then_inc(S("c_exp"), 1)
                    if u % 2:
                        yield
                for s in range(3):
                    w("pv", (4, 4, 6)[s])
                    a.copy(ot[:, s, :], ps[:, 2 + s // 2, TOK * (s % 2):TOK * (s % 2) + TOK]).then_inc(S("c_ot"), 1)
                yield
                yield
                w("ontp", 1)
                a.copy(ont[0:C, :], ps[0:C, 6, 0:TOK]).then_inc(S("c_ont"), 1)
                yield
                yield
                yield
                w("x3t", 1)
                a.copy(b_xnt[0:C, :], ps[0:C, 2, 0:TOK]).then_inc(S("c_x3t_sb"), 1)
                w("gsub", 1)
                a.activation(sc[:], sc[:], ACT.Exp).then_inc(S("c_gexp"), 1)
                yield
                for e in range(EXPERTS):
                    w("h1", e + 1)
                    bk = 4 + 2 * (e % 2)
                    a.activation(hb[:, e % 2].rearrange("p m n -> p (m n)"), ps[:, bk:bk + 2, :].rearrange("p a n -> p (a n)")[:, 0:MT * TOK],
                                 ACT.Gelu).then_inc(S("c_h"), 1)
                    if e:
                        yield
                yield

            run_pass(act, ORDER_C, front_c, back_c)

        @block.tensor
        def _(pe):
            m = nc.tensor
            prime(pe, "pe")

            def mm(o, l, r, start=True, stop=True):
                return m.matmul(o, l, r, start=start, stop=stop)

            def turn(bank, x, t):
                for b in range(PAIRS):
                    ins = m.transpose(bank_bf(bank)[:, b, :], stack[:, x, t].rearrange("p h c -> p (h c)")[:, P * b:P * b + P], identb[:])
                return ins

            def cols(t):
                return slice(P * t, P * t + P)

            pe.wait_ge(weights_in, 16 * len(loads))
            pe.wait_ge(setup_pool, 8)
            pe.wait_ge(setup_dve, 6)
            mm(ps[0:C, 0, 0:GROUPS], onesm[0:C, 0:C], wsum[0:C, :]).then_inc(setup_pe, 1)
            pe.wait_ge(setup_dve, 8)
            mm(ps[:, 0, 0:GROUPS], onesm[:, :], wsum[:, :]).then_inc(setup_pe, 1)
            mm(ps[:, 1, 0:REL], cpb_w1[:], table[:]).then_inc(setup_pe, 1)
            pe.wait_ge(setup_act, 1)
            mm(ps[0:HEADS, 2, 0:REL], cpb_w2[:], hid_t[:]).then_inc(setup_pe, 1)
            pe.wait_ge(bt_dma, 16 * 65)
            for b in range(2):
                ins = mm(ps[:, 3 + b, 0:384], flip[:], ebraw[:, 6 * b:6 * b + 6, :].rearrange("p h n -> p (h n)"))
            ins.then_inc(setup_pe, 1)
            pe.wait_ge(setup_act, ASETUP)
            pe.wait_ge(setup_dve, DSETUP)
            pe.wait_ge(setup_pool, 14)
            pe.wait_ge(bias_dma, 48)

            def front_a(i):
                w = waits(pe, "a_", i)
                yield
                w("qk", 0)
                w("v", 0)
                w("xn", 1)
                for t in range(TILES):
                    ins = mm(ps[0:C, 0, cols(t)], f_xn[:, t, :], perm_in[:])
                ins.then_inc(S("a_xt"), 1)
                w("xnt", 1)
                for t in range(TILES):
                    mm(ps[:, t, 0:3 * C], f_xnt[:, cols(t)], wqkv[:]).then_inc(S("a_qkv"), 1)
                yield
                for _ in range(4):
                    yield

            def window(t, k):
                return slice(P * t + WIN * k, P * t + WIN * k + WIN)

            def back_a(i):
                w = waits(pe, "a_", i)
                w("split", 1)
                w("copies", 1)
                w("x2t_sb", 0)
                w("y1_sb", 0)
                for t in range(TILES):
                    turn(2 + t, 0, t).then_inc(S("a_qt"), 1)
                    turn(4 + 2 * t, 1, t).then_inc(S("a_kt"), 1)
                yield
                for t in range(TILES):
                    w("qt_sb", t + 1)
                    w("kt_sb", t + 1)
                    settle(pe, "pe")
                    for h in range(HEADS):
                        b, a = h // 2, h % 2
                        r = slice(SLOT * a, SLOT * a + MAXCOL)
                        for k in range(2):
                            ins = mm(ps[WIN * k:WIN * k + WIN, 4 + 2 * t + a, WIN * b:WIN * b + WIN],
                                     stackt[r, 0, b, window(t, k)], stackt[r, 1, b, window(t, k)])
                    ins.then_inc(S("a_s"), 1)
                yield
                for t in range(TILES):
                    w("nm", t + 1)
                    turn(2 + t, 0, t).then_inc(S("a_q2t"), 1)
                yield
                for t in range(TILES):
                    w("q2t_sb", t + 1)
                    settle(pe, "pe")
                    for h in range(HEADS):
                        b, a = h // 2, h % 2
                        r = slice(SLOT * a, SLOT * a + FULL)
                        for k in range(2):
                            ins = mm(ps[WIN * k:WIN * k + WIN, 4 + 2 * t + a, WIN * b:WIN * b + WIN],
                                     stackt[r, 1, b, window(t, k)], stackt[r, 0, b, window(t, k)])
                    ins.then_inc(S("a_st"), 1)
                yield
                w("va", 1)
                for t in range(TILES):
                    w("prob", t + 1)
                    settle(pe, "pe")
                    pv = prob[:, t].rearrange("p a b c -> p (a b c)")
                    for h in range(HEADS):
                        for k in range(2):
                            at = (h % 2) * PAIRS * WIN + (h // 2) * WIN
                            to = (3 * t + h // 4) * WIN
                            r = slice(WIN * k, WIN * k + WIN)
                            ins = mm(ps[32 * (h % 4):32 * (h % 4) + 32, 2 + k, to:to + WIN], va[r, t, h, :], pv[r, at:at + WIN])
                ins.then_inc(S("a_pv"), 1)
                yield
                w("ot", 1)
                for t in range(TILES):
                    for s in range(3):
                        ins = m.transpose(ps[:, 4 + 2 * t, cols(s)], ot[:, s, cols(t)], ident[:])
                    ins.then_inc(S("a_otr"), 1)
                yield
                w("on", 2)
                for t in range(TILES):
                    ins = mm(ps[0:C, 5, cols(t)], on[:, t, :], perm_out[:])
                ins.then_inc(S("a_ontp"), 1)
                yield
                w("ont", 1)
                for t in range(TILES):
                    ins = mm(tiles(7, C)[:, t, :], ont[:, cols(t)], wproj[:])
                ins.then_inc(S("a_proj"), 1)
                yield
                w("xn2", 1)
                for t in range(TILES):
                    ins = m.transpose(ps[0:C, 2, cols(t)], b_xn[:, t, :], ident[:])
                ins.then_inc(S("a_x2t"), 1)
                yield
                w("x2t_sb", 1)
                for k in range(MT):
                    ins = mm(ps[:, 4 + k // 2, TOK * (k % 2):TOK * (k % 2) + TOK], w1s[:, cols(k)], b_xnt[0:C, :])
                ins.then_inc(S("a_y1"), 1)
                yield

            run_pass(pe, ORDER_A, front_a, back_a)

            with pe.Fori(1, GROUPS + 1) as i:
                w = waits(pe, "b_", i)
                w("y2_sb", 0)
                for u in range(GIMG):
                    w("h", u + 1)
                    for k in range(MT):
                        ins = mm(ps[0:C, u, 0:TOK], w2s[:, k, :], hb[:, u, k, :], k == 0, k == MT - 1)
                    ins.then_inc(S("b_y2"), 1)

            pe.wait_ge(S("b_y2_sb"), (GROUPS + 1) * GIMG)

            def front_c(i):
                w = waits(pe, "c_", i)
                w("mul", 0)
                w("v", 0)
                w("ycl", 1)
                for t in range(TILES):
                    ins = m.transpose(tiles(0, C)[:, t, :], ycl[:, cols(t)], ident[0:C, 0:C])
                ins.then_inc(S("c_yt"), 1)
                yield
                w("xn", 1)
                for t in range(TILES):
                    ins = m.transpose(ps[0:C, 1, cols(t)], f_xn[:, t, :], ident[:])
                ins.then_inc(S("c_xt"), 1)
                yield
                w("xnt", 1)
                mm(ps[0:C, 0, 0:TOK], wq[:], f_xnt[:]).then_inc(S("c_qc"), 1)
                for t in range(TILES):
                    ins = mm(tiles(1, C)[:, t, :], f_xnt[:, cols(t)], wq[:])
                ins.then_inc(S("c_q"), 1)
                yield
                w("qpad", 1)
                for t in range(TILES):
                    o = tiles(0, C)[:, t, :]
                    for k in range(9):
                        r0 = 8 * t + k // 3
                        mm(o, qpad[:, k % 3, r0:r0 + 8, :].rearrange("p r c -> p (r c)"), wconv[:, k, :], k == 0, False)
                    ins = mm(o, onesb[:], bias3[:, EXPERTS * C:EXPERTS * C + C], False, True)
                ins.then_inc(S("c_conv"), 1)
                yield
                w("q_sb", 1)
                w("cg", 1)
                for t in range(TILES):
                    ins = m.transpose(ps[0:C, 1, cols(t)], tn[:, t, :], ident[:])
                ins.then_inc(S("c_tt"), 1)
                yield
                w("tnt", 1)
                for k in range(2):
                    ins = mm(ps[0:C, 0, TOK * k:TOK * k + TOK], woffp[:, k, :], tnt[:])
                ins.then_inc(S("c_offs"), 1)
                yield
                w("hat", 1)
                for t in range(TILES):
                    ins = m.transpose(tiles(1, C)[:, t, :], hat[:, 1, cols(t)], ident[0:C, 0:C])
                ins.then_inc(S("c_hxt"), 1)
                yield
                for k in range(6):
                    t, b = k // 3, k % 3
                    if k == 0:
                        w("rows_in", 16 * DG)
                    if k == 1:
                        w("hatx", 1)
                    if k >= 2:
                        w("mul", k - 1)
                    mm(ps[:, k % 2, :], hat[:, 0, cols(t)],
                       rows[:, 2 * b:2 * b + 2].rearrange("p g c k -> p (g c k)")).then_inc(S("c_t3"), 1)
                    yield
                w("xs", 1)
                for t in range(TILES):
                    ins = m.transpose(ps[0:C, 0, cols(t)], xs[:, t, :], ident[:])
                ins.then_inc(S("c_xst"), 1)
                yield
                w("xst_sb", 1)
                for t in range(TILES):
                    ins = mm(tiles(1, 2 * C)[:, t, :], f_xnt[:, cols(t)], wkv[:])
                ins.then_inc(S("c_kv"), 1)
                yield
                yield
                yield
                yield

            def back_c(i):
                w = waits(pe, "c_", i)
                w("split", 1)
                w("copies", 1)
                w("acc", 0)
                w("v", 1)
                for t in range(TILES):
                    turn(2 + t, 0, t).then_inc(S("c_qt"), 1)
                    turn(4 + 2 * t, 1, t).then_inc(S("c_kt"), 1)
                yield
                w("qt_sb", 2)
                w("kt_sb", 2)
                for u in range(6):
                    t, pq = u // 3, u % 3
                    if u >= 2:
                        w("nm", u - 1)
                    for h in range(4):
                        b, a = 2 * pq + h // 2, h % 2
                        r = slice(SLOT * a, SLOT * a + SPLIT)
                        ins = mm(ps[:, 4 + 2 * (u % 2) + a, TOK * (h // 2):TOK * (h // 2) + TOK],
                                 stackt[r, 0, b, cols(t)], stackt[r, 1, b, :])
                    ins.then_inc(S("c_s"), 1)
                    if u % 2:
                        yield
                w("parts", 1)
                for t in range(TILES):
                    turn(2 + t, 0, t).then_inc(S("c_q2t"), 1)
                yield
                w("q2t_sb", 2)

                def values(u):
                    pq, k = u // 2, u % 2
                    w("exp", u + 1)
                    for h in range(4):
                        ins = mm(ps[32 * h:32 * h + 32, 2 + pq // 2, TOK * (pq % 2):TOK * (pq % 2) + TOK],
                                 va[:, k, 4 * pq + h, :], prob[:, u % 2, h % 2, h // 2, :], k == 0, k == 1)
                    ins.then_inc(S("c_pv"), 1)

                for u in range(6):
                    pq, k = u // 2, u % 2
                    if u >= 2:
                        w("exp", u - 1)
                    for h in range(4):
                        b, a = 2 * pq + h // 2, h % 2
                        r = slice(SLOT * a, SLOT * a + FULL)
                        ins = mm(ps[:, 4 + 2 * (u % 2) + a, TOK * (h // 2):TOK * (h // 2) + TOK],
                                 stackt[r, 1, b, cols(k)], stackt[r, 0, b, :])
                    ins.then_inc(S("c_st"), 1)
                    if u >= 1:
                        values(u - 1)
                    if u % 2:
                        yield
                values(5)
                yield
                w("ot", 3)
                for t in range(TILES):
                    for s in range(3):
                        ins = m.transpose(ps[:, 4 + t, cols(s)], ot[:, s, cols(t)], ident[:])
                    ins.then_inc(S("c_otr"), 1)
                yield
                w("on", 2)
                for t in range(TILES):
                    ins = m.transpose(ps[0:C, 6, cols(t)], on[:, t, :], ident[:])
                ins.then_inc(S("c_ontp"), 1)
                yield
                w("ont", 1)
                for t in range(TILES):
                    ins = mm(tiles(7, C)[:, t, :], ont[:, cols(t)], wo[:])
                ins.then_inc(S("c_proj"), 1)
                yield
                w("xn3", 1)
                for t in range(TILES):
                    ins = m.transpose(ps[0:C, 2, cols(t)], b_xn[:, t, :], ident[:])
                ins.then_inc(S("c_x3t"), 1)
                yield
                w("x3t_sb", 1)
                for t in range(TILES):
                    ins = mm(tiles(3, EXPERTS)[:, t, :], b_xnt[:, cols(t)], wg[:])
                ins.then_inc(S("c_gate"), 1)
                yield

                def up(e):
                    if e >= 2:
                        w("h", e - 1)
                    bk = 4 + 2 * (e % 2)
                    for k in range(MT):
                        ins = mm(ps[:, bk + k // 2, TOK * (k % 2):TOK * (k % 2) + TOK], we1[:, e, cols(k)], b_xnt[:])
                    ins.then_inc(S("c_h1"), 1)

                up(0)
                up(1)
                w("gsub", 1)
                for t in range(TILES):
                    mm(ps[:, 2 + t, 0:EXPERTS * C], onesb[:], bias3[:, 0:EXPERTS * C], True, False)
                for e in range(EXPERTS):
                    w("h", e + 1)
                    for t in range(TILES):
                        for k in range(MT):
                            ins = mm(ps[:, 2 + t, C * e:C * e + C], hb[:, e % 2, k, cols(t)], we2[:, e, k, :],
                                     False, k == MT - 1 and e == EXPERTS - 1)
                    if e == EXPERTS - 1:
                        ins.then_inc(S("c_y"), 1)
                    if e + 2 < EXPERTS:
                        up(e + 2)
                    if e < 3:
                        yield
                yield

            run_pass(pe, ORDER_C, front_c, back_c)


def _constants():
    import numpy as np

    c = {}
    c["ident"] = np.eye(P, dtype=np.float32)
    perm = np.zeros((P, P), np.float32)
    for w in range(2):
        for r in range(8):
            for q in range(8):
                perm[r * SIDE + (SHIFT + 8 * w + q) % SIDE, w * WIN + r * 8 + q] = 1
    c["perm_in"] = perm
    c["perm_out"] = np.ascontiguousarray(perm.T)
    flip = np.zeros((WIN, P), np.float32)
    for j in range(WIN):
        flip[WIN - 1 - j, j] = flip[WIN - 1 - j, WIN + j] = 1
    c["flip"] = flip
    mq = np.zeros((P, TILES, MASKROWS), np.float32)
    mk = np.zeros((P, TILES, MASKROWS), np.float32)
    for t in range(TILES):
        for w in range(2):
            for r in range(8):
                for q in range(8):
                    p = w * WIN + r * 8 + q
                    cl = 2 * (t == 1 and r >= 4) + (w == 1 and q >= 4)
                    mq[p, t, 0], mk[p, t, 0] = 1, -100
                    mq[p, t, 1 + cl], mk[p, t, 1 + cl] = 1, 100
    c["mask_q"], c["mask_k"] = mq, mk
    d = np.arange(-7, 8, dtype=np.float32)
    tb = np.stack(np.meshgrid(d, d, indexing="ij"), axis=-1) / np.float32(7) * np.float32(8)
    tb = np.sign(tb) * np.log2(np.abs(tb) + np.float32(1)) / np.float32(3)
    c["table"] = np.ascontiguousarray(tb.reshape(REL, 2).T.astype(np.float32))
    q = np.arange(TOK)
    r = np.arange(SIDE)
    y = (q % SIDE)[None, :] - r[:, None]
    x = (q // SIDE)[None, :] - r[:, None]
    c["posc"] = np.ascontiguousarray(np.tile(np.stack([y, x], 1), (DG, 1, 1)).astype(np.float32))
    c["tri"] = np.ascontiguousarray(np.broadcast_to(np.tril(np.ones((EXPERTS, EXPERTS), np.float32), -1), (P, EXPERTS, EXPERTS)))
    return c


def _layout(a):
    import numpy as np

    row = lambda v: np.asarray(v).reshape(1, -1)
    cat = lambda *v: np.ascontiguousarray(np.concatenate(v, 0))
    T = lambda v: np.ascontiguousarray(np.asarray(v).T)
    L = {"x": np.ascontiguousarray(a["x"]).reshape(IMAGES * TOK, C)}
    L["cpb_w1"] = T(a["L0_conv_cpb_w1"])
    L["cpb_b1"] = np.ascontiguousarray(a["L0_conv_cpb_b1"]).reshape(P, 1)
    L["cpb_w2"] = T(a["L0_conv_cpb_w2"])
    L["lscale"] = np.ascontiguousarray(np.broadcast_to(row(a["L0_conv_logit_scale"]), (P, HEADS)))
    qb = np.array(a["L0_conv_qkv_b"]).reshape(1, -1)
    qb[:, C:2 * C] = 0
    L["wqkv"] = cat(T(a["L0_conv_qkv_w"]), qb)
    L["wproj"] = cat(T(a["L0_conv_proj_w"]), row(a["L0_conv_proj_b"]))
    L["w1"] = T(a["L0_ffn_W1"])
    L["b1"] = T(np.asarray(a["L0_ffn_b1"]).reshape(MT, P))
    L["w2"] = np.ascontiguousarray(np.asarray(a["L0_ffn_W2"]).T.reshape(MT, P, C).transpose(1, 0, 2))
    L["b2"] = np.ascontiguousarray(a["L0_ffn_b2"]).reshape(C, 1)
    L["wq"] = cat(a["L1_conv_w_q"], row(a["L1_conv_b_q"]))
    w0 = np.asarray(a["L1_conv_w_off0"]).reshape(9, GC, C)
    wc = np.zeros((C, 9, C), w0.dtype)
    wp = np.asarray(a["L1_conv_w_offp"])
    wf = np.zeros((C, 2, C), wp.dtype)
    for g in range(DG):
        s = slice(GC * g, GC * g + GC)
        wc[s, :, s] = w0[:, :, s].transpose(1, 0, 2)
        wf[s, 0, s] = np.broadcast_to(wp[:, 0:1], (GC, SIDE))
        wf[s, 1, s] = np.broadcast_to(wp[:, 1:2], (GC, SIDE))
    L["wconv"], L["woffp"] = wc, wf
    L["lng"] = np.ascontiguousarray(np.broadcast_to(row(a["L1_conv_ln_g"]), (P, C)))
    L["lnb"] = np.ascontiguousarray(np.broadcast_to(row(a["L1_conv_ln_b"]), (P, C)))
    L["wkv"] = cat(np.concatenate([a["L1_conv_w_k"], a["L1_conv_w_v"]], 1),
                   np.concatenate([row(a["L1_conv_b_k"]), row(a["L1_conv_b_v"])], 1))
    L["wo"] = cat(a["L1_conv_w_o"], row(a["L1_conv_b_o"]))
    L["wg"] = cat(a["L1_ffn_gate_w"], row(a["L1_ffn_gate_b"]))
    w1 = np.asarray(a["L1_ffn_w1"]).transpose(1, 0, 2)
    L["we1"] = cat(w1, np.asarray(a["L1_ffn_b1"]).reshape(1, EXPERTS, HID))
    L["we2"] = np.ascontiguousarray(np.asarray(a["L1_ffn_w2"]).reshape(EXPERTS, MT, P, C).transpose(2, 0, 1, 3))
    L["be2"] = np.ascontiguousarray(np.concatenate([row(a["L1_ffn_b2"]), row(a["L1_conv_b_off0"])], 1))
    return L


def kernel(**inputs):
    import numpy as _np
    import concourse.bacc as _bacc
    from concourse import mybir as _mybir
    from concourse.bass_utils import run_bass_kernel_spmd as _run

    nc = _bacc.Bacc("TRN2", target_bir_lowering=False, num_devices=1)
    given = {**_layout(inputs), **_constants()}
    arrays, aps = {}, {}
    for name, a in given.items():
        a = _np.ascontiguousarray(a)
        arrays[f"in_{name}"] = a
        aps[name] = nc.dram_tensor(f"in_{name}", a.shape, _mybir.dt.from_np(a.dtype), kind="ExternalInput").ap()
    out = nc.dram_tensor("out_0", (IMAGES * TOK, C), _mybir.dt.float32, kind="ExternalOutput").ap()
    build_program(nc, aps, out)
    r = _run(nc, [arrays], core_ids=[0])
    return _np.asarray(r.results[0]["out_0"]).reshape(IMAGES, SIDE, SIDE, C)
```

```python
from contextlib import ExitStack

import concourse.bass as bass
from concourse import mybir

F32 = mybir.dt.float32
BF16 = mybir.dt.bfloat16
ALU = mybir.AluOpType
ACT = mybir.ActivationFunctionType
AX = mybir.AxisListType
RMAX = bass.bass_isa.ReduceOp.max

P = 128
IMAGES = 16
SIDE = 16
TOK = SIDE * SIDE
TILES = TOK // P
C = 96
HEADS = 12
HD = C // HEADS
PAIRS = HEADS // 2
SLOT = 64
SPLIT = 6 * HD
MASKROWS = 5
MAXCOL = SPLIT + MASKROWS
FULL = MAXCOL + 3
WIN = 64
HID = 4 * C
MT = HID // P
HAT_PARTS = (0, 0, 1, 1, 0, 2)
ROW_PARTS = (0, 1, 0, 1, 2, 0)
GROUPS = 5
GIMG = IMAGES // GROUPS
QIMG = GROUPS * GIMG
EPSQ = 1e-5
QB = 128.0
LIM = QB - EPSQ
DG = 6
GC = C // DG
EXPERTS = 4
REL = 15 * 15
SHIFT = 4


ORDER_A = "afafpfaafprfrarpp"
ORDER_C = "eeeoeeosaeaasaseeeoaaeeeaooseoeaokokkeaeassaasooaaoasoao"
BEHIND_A = dict(p=0, r=1, a=2, f=3)
BEHIND_C = dict(o=0, s=1, k=2, a=3, e=4)


def build_program(nc, A, out):
    ctx = ExitStack()
    with ctx:
        def sb(name, shape, dt=F32):
            return ctx.enter_context(nc.sbuf_tensor(name, shape, dt))

        ident = sb("ident", [P, P])
        identb = sb("identb", [P, P], BF16)
        perm_in = sb("perm_in", [P, P])
        perm_out = sb("perm_out", [P, P])
        flip = sb("flip", [WIN, P])
        mask_q = sb("mask_q", [P, TILES, MASKROWS])
        mask_k = sb("mask_k", [P, TILES, MASKROWS])
        table = sb("table", [2, REL])
        cpb_w1 = sb("cpb_w1", [2, P])
        cpb_b1 = sb("cpb_b1", [P, 1])
        cpb_w2 = sb("cpb_w2", [P, HEADS])
        lscale = sb("lscale", [P, HEADS])
        wqkv = sb("wqkv", [C + 1, 3 * C])
        wproj = sb("wproj", [C + 1, C])
        w1 = sb("w1", [C, HID])
        w1s = sb("w1s", [C, HID])
        b1 = sb("b1", [P, MT])
        w2 = sb("w2", [P, MT, C])
        w2s = sb("w2s", [P, MT, C])
        b2 = sb("b2", [C, 1])
        wq = sb("wq", [C + 1, C])
        wconv = sb("wconv", [C, 9, C])
        lng = sb("lng", [P, C])
        lnb = sb("lnb", [P, C])
        woffp = sb("woffp", [C, 2, C])
        posc = sb("posc", [C, 2, TOK])
        wkv = sb("wkv", [C + 1, 2 * C])
        wo = sb("wo", [C + 1, C])
        wg = sb("wg", [C + 1, EXPERTS])
        we1 = sb("we1", [C + 1, EXPERTS, HID])
        we2 = sb("we2", [P, EXPERTS, MT, C])
        be2 = sb("be2", [1, EXPERTS * C + C])
        bres = sb("bres", [1, EXPERTS * C + C])
        bpart = sb("bpart", [1, 3, EXPERTS * C + C], BF16)
        bias3 = sb("bias3", [3, 2, TILES, 2 * C], BF16)
        cbias3 = sb("cbias3", [3, C], BF16)
        onesb = sb("onesb", [3, P], BF16)
        tri = sb("tri", [P, EXPERTS, EXPERTS])
        loads = [(ident, "ident"), (perm_in, "perm_in"), (perm_out, "perm_out"), (flip, "flip"),
                 (mask_q, "mask_q"), (mask_k, "mask_k"), (table, "table"), (cpb_w1, "cpb_w1"),
                 (cpb_b1, "cpb_b1"), (cpb_w2, "cpb_w2"), (lscale, "lscale"), (wqkv, "wqkv"),
                 (wproj, "wproj"), (w1, "w1"), (b1, "b1"), (w2, "w2"), (b2, "b2"), (wq, "wq"),
                 (wconv, "wconv"), (lng, "lng"), (lnb, "lnb"), (woffp, "woffp"),
                 (posc, "posc"), (wkv, "wkv"), (wo, "wo"), (wg, "wg"), (we1, "we1"), (we2, "we2"),
                 (be2, "be2"), (tri, "tri")]
        onesm = sb("onesm", [P, P])
        neghalf = sb("neghalf", [P, 2 * TILES * HEADS])
        hid_t = sb("hid_t", [P, REL])
        bt_sb = sb("bt_sb", [HEADS, REL])
        ebraw = sb("ebraw", [WIN, HEADS, 8 * 15])
        ebz = sb("ebz", [P, HEADS, WIN])
        expbias = sb("expbias", [P, 2, PAIRS, WIN])
        wsum = sb("wsum", [P, GROUPS])
        wmean = sb("wmean", [P, 2, GROUPS])
        y1all = sb("y1all", [P, IMAGES, MT, TOK])
        y2all = sb("y2all", [C, IMAGES, TOK])
        gm1 = sb("gm1", [P, IMAGES])
        gm2 = sb("gm2", [P, IMAGES])
        gg = sb("gg", [P, 2, GROUPS])
        ggall = sb("ggall", [P, 2, GROUPS])
        gs = sb("gs", [P, 2, GROUPS])
        qs1 = sb("qs1", [P, IMAGES])
        qs2 = sb("qs2", [P, IMAGES])
        xraw = sb("xraw", [P, TILES, C])
        xin = sb("xin", [P, TILES, C])
        xres = sb("xres", [P, TILES, C])
        norms = {h: dict(stats=sb(h + "stats", [P, TILES, 6]), mv=sb(h + "mv", [P, TILES, 2]),
                         veps=sb(h + "veps", [P, TILES]), rstd=sb(h + "rstd", [P, TILES])) for h in "ps"}
        f_xn = sb("f_xn", [P, TILES, C])
        b_xn = sb("b_xn", [P, TILES, C])
        f_xnt = sb("f_xnt", [C + 1, TOK])
        b_xnt = sb("b_xnt", [C + 1, TOK])
        xst = sb("xst", [C + 1, TOK])
        sq = sb("sq", [P, TILES, 2, HEADS, HD])
        ss = sb("ss", [P, TILES, 2 * HEADS])
        rn = sb("rn", [P, TILES, 2, HEADS])
        qk = sb("qk", [P, 2, TILES, HEADS, HD])
        res = sb("res", [P, 2, TILES, HEADS, HD])
        stack = sb("stack", [P, 2, TILES, HEADS, SLOT], BF16)
        stackt = sb("stackt", [P, 2, PAIRS, TOK], BF16)
        qkv_sb = sb("qkv_sb", [P, TILES, 3 * C])
        v_new = sb("v_new", [P, TILES, HEADS, HD])
        va = sb("va", [P, TILES, HEADS, 32])
        nm = sb("nm", [P, TILES, 2, PAIRS])
        nmr = sb("nmr", [P, TILES, 2, PAIRS])
        prob = sb("prob", [P, 4, 2, TOK])
        ot = sb("ot", [P, 3, TOK])
        rec = sb("rec", [P, TILES, HEADS])
        on = sb("on", [P, TILES, C])
        ont = sb("ont", [C + 1, TOK])
        hb = sb("hb", [P, 3, MT, TOK])
        ycl = sb("ycl", [C, TOK])
        qpad = sb("qpad", [C, 3, SIDE + 2, SIDE])
        tn = sb("tn", [P, TILES, C])
        tnt = sb("tnt", [C, TOK])
        th = sb("th", [C, 2, TOK])
        hat = sb("hat", [C, 2, TOK])
        hatx = sb("hatx", [P, TILES, DG, SIDE])
        xnr = sb("xnr", [P, TILES, C])
        xnp = sb("xnp", [P, 3, TILES, C], BF16)
        hatr = sb("hatr", [C, TOK])
        hatp = sb("hatp", [C, 3, TOK], BF16)
        rows = sb("rows", [6 * SIDE, SIDE, C], BF16)
        hatst = sb("hatst", [6 * SIDE, DG, TOK], BF16)
        samp = sb("samp", [P, 2, 2 * SIDE, GC])
        xs = sb("xs", [P, TILES, C])
        sc = sb("sc", [P, TILES, EXPERTS])
        scm = sb("scm", [P, TILES])
        scs = sb("scs", [P, TILES])
        gt = sb("gt", [P, TILES, EXPERTS, EXPERTS])
        eq = sb("eq", [P, TILES, EXPERTS, EXPERTS])
        acc = sb("acc", [P, TILES, C])

        ps = ctx.enter_context(nc.psum_tensor("ps", [P, 8, 512], F32))

        def bank_bf(b):
            return ps[:, b, 0:384].bitcast(BF16).rearrange("p (a c) -> p a c", c=P)

        def tile_probs(t):
            return prob[:, 2 * t:2 * t + 2].rearrange("p a b c -> p (a b c)")[:, 0:HEADS * WIN]

        def tiles(b, n):
            return ps[:, b, 0:TILES * n].rearrange("p (t c) -> p t c", c=n)

        x1_dram = nc.dram_tensor("x1_scratch", [IMAGES * TOK, C], F32).ap()
        xn_dram = nc.dram_tensor("xn_scratch", [3, TOK, C], BF16).ap()
        hat_dram = nc.dram_tensor("hat_scratch", [C, 3, TOK], BF16).ap()
        bt_dram = nc.dram_tensor("bt_scratch", [HEADS, REL], F32).ap()

        class Signal:

            def __init__(self, name, n):
                self.sem = ctx.enter_context(nc.semaphore(name))
                self.n = n

            def at(self, i, k):
                return i * self.n + k

        made = {}

        def signals(prefix, owner, **counts):
            for k, n in counts.items():
                made[prefix + k] = (Signal(prefix + k, n), owner)

        def plain_sem(name):
            return ctx.enter_context(nc.semaphore(name))

        weights_in = plain_sem("weights_in")
        bt_dma = plain_sem("bt_dma")
        bias_dma = plain_sem("bias_dma")
        setup_dve = plain_sem("setup_dve")
        setup_pool = plain_sem("setup_pool")
        setup_pe = plain_sem("setup_pe")
        setup_act = plain_sem("setup_act")
        gam = [plain_sem(f"gamma{n}") for n in range(2)]
        gam_all = [plain_sem(f"gamma_all{n}") for n in range(2)]
        gam_ready = [plain_sem(f"gamma_ready{n}") for n in range(2)]
        own_sems = {k: plain_sem(k) for k in ("dve_first", "dve_mid", "dve_last", "dve_sample", "pool_split", "pool_parts")}

        signals("a_", "sp", x_in=48, x1_out=48)
        signals("a_", "dve", var=1, xn=1, ss=1, qk=2, nm=2, prob=2, on=2, x1=1, var2=1, xn2=1, gm=1)
        signals("a_", "pool", rstd=1, rn=2, va=1, split=1, rstd2=1)
        signals("a_", "act", xnt=1, sq=2, qkv_sb=2, v=1, copies=1, qt_sb=2, kt_sb=2, q2t_sb=2, exp=2, ot=1, ont=1,
                x2t_sb=1, y1_sb=1)
        signals("a_", "pe", xt=1, qkv=2, qt=2, kt=2, s=2, q2t=2, st=2, pv=1, otr=2, ontp=1, proj=1,
                x2t=1, y1=1)
        signals("b_", "dve", cl=GIMG, gm=GIMG)
        signals("b_", "act", h=GIMG, y2_sb=GIMG)
        signals("b_", "pe", y2=GIMG)
        signals("c_", "sp", x_in=16, xn_out=48, rows_in=96, hat_out=16, hat_in=96, out=16)
        signals("c_", "dve", ycl=1, xadd=1, var=1, xn=1, cvar=1, cn=1, hat=1, mul=6, xs=1, nm=12, parts=1,
                on=2, x3=1, var3=1, xn3=1, gsub=1, acc=2)
        signals("c_", "pool", rstd=1, xnp=1, crstd=1, hatp=1, va=1, split=1, rstd3=1)
        signals("c_", "act", xnt=1, qpad=1, q_new=1, cg=1, tnt=1, tanh=1, hatx=1, xst_sb=1, k_sb=1, v=1,
                copies=1, qt_sb=2, kt_sb=2, q2t_sb=2, exp=12, ot=3, ont=1, x3t_sb=1, gexp=1, h=8)
        signals("c_", "pe", yt=1, xt=1, qc=1, q=1, conv=1, tt=1, offs=1, hxt=1, t3=6, xst=1, kv=1,
                qt=2, kt=2, s=12, q2t=2, st=12, pv=12, otr=2, ontp=1, proj=1, x3t=1, gate=1, h1=8, y=2)

        def S(name):
            return made[name][0].sem

        def waits(eng, prefix, i):
            def w(name, k):
                sig = made[prefix + name][0]
                eng.wait_ge(sig.sem, sig.at(i, k))
            return w

        def prime(eng, who):
            for s, owner in made.values():
                if owner == who:
                    eng.sem_inc(s.sem, s.n)

        settled = {k: plain_sem("settled_" + k) for k in ("sp", "pool", "pe")}

        def settle(eng, who):
            eng.sem_inc(settled[who], 1)

        def turn_of(order, parts):
            for c in order:
                if c in parts:
                    next(parts[c])
            for rest in parts.values():
                assert next(rest, "end") == "end", "stages left over"

        def run_pass(eng, order, behind, **parts):
            last = max(behind.values())

            def turn(j, there):
                turn_of(order, {c: p(j - behind[c]) for c, p in parts.items() if there(behind[c])})

            for j in range(1, last + 1):
                turn(j, lambda n: n < j)
            with eng.Fori(last + 1, IMAGES + 1) as j:
                turn(j, lambda n: True)
            for j in range(IMAGES + 1, IMAGES + last + 1):
                turn(j, lambda n: j - n <= IMAGES)

        def kept(i, k=0):
            return slots(i)[:, TILES * C * k:TILES * C * (k + 1)].rearrange("p (t c) -> p t c", c=C)

        def queries_keys(i):
            return slots(i)[:, TILES * C:3 * TILES * C].rearrange("p (n c) -> p n c", c=HD)

        def slots(i):
            return y1all[:, bass.ds(i - 1, 1)].rearrange("p a m n -> p (a m n)")

        class Own:

            def __init__(self, eng, sem):
                self.eng, self.sem, self.n = eng, own_sems[sem], 0
                eng.sem_clear(self.sem)

            def mark(self, ins):
                ins.then_inc(self.sem, 1)
                self.n += 1
                return self.n

            def wait(self, n):
                self.eng.wait_ge(self.sem, n)

            def link(self, ins):
                self.wait(self.mark(ins))

        block = ctx.enter_context(nc.Block())
        ASETUP = 8
        DSETUP = 28

        @block.sync
        def _(sp):
            prime(sp, "sp")
            for t, name in loads:
                sp.dma_start(t[:], A[name]).then_inc(weights_in, 16)
            sp.wait_ge(setup_act, 2)
            sp.dma_start(bt_dram, bt_sb[:, :]).then_inc(bt_dma, 16)
            sp.wait_ge(bt_dma, 16)
            for rj in range(8):
                src = bass.AP(bt_dram.tensor, bt_dram.offset + rj * 15, [[1, 8], [REL, HEADS], [1, 7 * 15 + 8]])
                sp.dma_start(ebraw[rj * 8:rj * 8 + 8, :, 0:7 * 15 + 8], src).then_inc(bt_dma, 16)
            sp.wait_ge(setup_dve, DSETUP)
            for k in range(3):
                for t in range(TILES):
                    sp.dma_start(bias3[k:k + 1, :, t, :], bpart[:, k, 0:EXPERTS * C].rearrange("p (h n) -> p h n", h=2)).then_inc(bias_dma, 16)
                sp.dma_start(cbias3[k:k + 1, :], bpart[:, k, EXPERTS * C:]).then_inc(bias_dma, 16)
            cut = TOK - SHIFT * SIDE - P

            def shifted(i):
                base = (i - 1) * TOK
                return ((bass.ds(base + SHIFT * SIDE, P), 0, slice(0, P)),
                        (bass.ds(base + SHIFT * SIDE + P, cut), 1, slice(0, cut)),
                        (bass.ds(base, P - cut), 1, slice(cut, P)))

            def project_a(i):
                w = waits(sp, "a_", i)
                w("xn", 0)
                settle(sp, "sp")
                for rows_, t, part in shifted(i):
                    sp.dma_start(xin[part, t, :], A["x"][rows_, :]).then_inc(S("a_x_in"), 16)
                for _ in range(ORDER_A.count("p")):
                    yield

            def split_a(i):
                for _ in range(3):
                    yield

            def attend_a(i):
                for _ in range(ORDER_A.count("a")):
                    yield

            def finish_a(i):
                w = waits(sp, "a_", i)
                yield
                yield
                w("x1", 1)
                settle(sp, "sp")
                for rows_, t, part in shifted(i):
                    sp.dma_start(x1_dram[rows_, :], xres[part, t, :]).then_inc(S("a_x1_out"), 16)
                for _ in range(ORDER_A.count("f") - 2):
                    yield

            run_pass(sp, ORDER_A, BEHIND_A, p=project_a, r=split_a, a=attend_a, f=finish_a)
            sp.wait_ge(S("a_x1_out"), (IMAGES + 1) * 48)
            sp.wait_ge(gam_ready[1], 1)

            def offsets_c(i):
                w = waits(sp, "c_", i)
                base = (i - 1) * TOK
                w("xadd", 0)
                settle(sp, "sp")
                sp.dma_start(xraw[:, :, :], x1_dram[bass.ds(base, TOK), :].rearrange("(t p) c -> p t c", p=P)).then_inc(S("c_x_in"), 16)
                yield
                yield
                w("rows_in", 0)
                settle(sp, "sp")
                w("xnp", 1)
                settle(sp, "sp")
                for k in range(3):
                    sp.dma_start(xn_dram[k].rearrange("(t p) c -> p t c", p=P), xnp[:, k, :, :]).then_inc(S("c_xn_out"), 16)
                for _ in range(ORDER_C.count("o") - 3):
                    yield
                w("t3", 0)
                settle(sp, "sp")
                w("xn_out", 48)
                settle(sp, "sp")
                for slot in range(6):
                    src = xn_dram[ROW_PARTS[slot]].rearrange("(r c) k -> r c k", c=SIDE)
                    sp.dma_start(rows[SIDE * slot:SIDE * slot + SIDE, :, :], src).then_inc(S("c_rows_in"), 16)
                w("hatp", 1)
                settle(sp, "sp")
                sp.dma_start(hat_dram, hatp[:, :, :]).then_inc(S("c_hat_out"), 16)
                w("hat_out", 16)
                settle(sp, "sp")
                for slot in range(6):
                    src = hat_dram[:, HAT_PARTS[slot], :].rearrange("(g r) q -> r g q", r=SIDE)
                    sp.dma_start(hatst[SIDE * slot:SIDE * slot + SIDE, :, :], src).then_inc(S("c_hat_in"), 16)
                yield

            def sample_c(i):
                for _ in range(ORDER_C.count("s")):
                    yield

            def split_c(i):
                for _ in range(3):
                    yield

            def attend_c(i):
                for _ in range(ORDER_C.count("a")):
                    yield

            def experts_c(i):
                w = waits(sp, "c_", i)
                base = (i - 1) * TOK
                for _ in range(ORDER_C.count("e") - 1):
                    yield
                w("acc", 2)
                settle(sp, "sp")
                sp.dma_start(out[bass.ds(base, TOK), :].rearrange("(t p) c -> p t c", p=P), acc[:, :, :]).then_inc(S("c_out"), 16)
                yield

            run_pass(sp, ORDER_C, BEHIND_C, o=offsets_c, s=sample_c, k=split_c, a=attend_c, e=experts_c)
            sp.wait_ge(S("c_out"), (IMAGES + 1) * 16)

        @block.gpsimd
        def _(pool):
            g = nc.gpsimd
            prime(pool, "pool")

            def setup(ins):
                ins.then_inc(setup_pool, 1)

            setup(g.memset(onesm[:], 1.0))
            setup(g.memset(neghalf[:], -0.5))
            setup(g.memset(stack[:], 0.0))
            setup(g.memset(va[:], 0.0))
            setup(g.memset(qpad[:], 0.0))
            setup(g.memset(y2all[:], 0.0))
            setup(g.memset(onesb[:], 1.0))
            pool.wait_ge(weights_in, 16 * len(loads))
            pool.wait_ge(setup_pool, 7)
            for t in range(TILES):
                for a, m in ((0, mask_q), (1, mask_k)):
                    setup(g.tensor_copy(stack[:, a, t, :, SPLIT:MAXCOL],
                                        m[:, t:t + 1, :].to_broadcast([P, HEADS, MASKROWS])))
            setup(g.memset(stack[:, 1, :, :, MAXCOL:FULL].rearrange("p t h c -> p (t h) c"), 1.0))
            setup(g.memset(va[:, :, :, HD:HD + 1], 1.0))
            pool.wait_ge(setup_pool, 13)

            def power(half, ready):
                n = norms[half]
                g.tensor_tensor(n["rstd"][:], n["veps"][:], neghalf[:, 0:TILES], ALU.pow).then_inc(S(ready), 1)

            def values_in(w, values, ready):
                w("pv", 0)
                w("v", 1)
                settle(pool, "pool")
                g.tensor_copy(va[:, :, :, 0:HD], values).then_inc(ready, 1)

            def split(own, src, ready):
                st = stack[:].rearrange("p a t h c -> p (a t h) c")
                rs = res[:].rearrange("p a t h c -> p (a t h) c")
                half = (slice(0, TILES * HEADS), slice(TILES * HEADS, 2 * TILES * HEADS))
                own.link(g.tensor_copy(st[:, :, 0:HD], src))
                own.link(g.tensor_tensor(rs, src, st[:, :, 0:HD], ALU.subtract))
                own.link(g.tensor_copy(st[:, :, HD:2 * HD], rs))
                yield
                for x, k in ((0, 2), (1, 5)):
                    own.mark(g.tensor_tensor(st[:, half[x], HD * k:HD * k + HD], rs[:, half[x]], st[:, half[x], HD:2 * HD], ALU.subtract))
                yield
                own.mark(g.tensor_copy(st[:, half[0], HD * 4:HD * 5], rs[:, half[0]]))
                own.wait(own.n)
                g.tensor_copy(st[:, half[1], HD * 3:HD * 4], rs[:, half[1]]).then_inc(ready, 1)

            def project_a(i):
                w = waits(pool, "a_", i)
                w("var", 1)
                power("p", "a_rstd")
                yield
                yield
                w("qk", 0)
                w("ss", 1)
                for t in range(TILES):
                    g.tensor_tensor(rn[:, t].rearrange("p a h -> p (a h)"), ss[:, t, :], neghalf[:, 0:2 * HEADS],
                                    ALU.pow).then_inc(S("a_rn"), 1)
                    yield

            def split_a(i):
                w = waits(pool, "a_", i)
                own = Own(pool, "pool_split")
                w("qk", 2)
                w("q2t", 0)
                settle(pool, "pool")
                yield from split(own, qk[:].rearrange("p a t h c -> p (a t h) c"), S("a_split"))
                yield

            def attend_a(i):
                values_in(waits(pool, "a_", i), v_new[:], S("a_va"))
                for _ in range(5):
                    yield

            def finish_a(i):
                w = waits(pool, "a_", i)
                for _ in range(2):
                    yield
                w("var2", 1)
                power("s", "a_rstd2")
                for _ in range(3):
                    yield

            run_pass(pool, ORDER_A, BEHIND_A, p=project_a, r=split_a, a=attend_a, f=finish_a)

            pool.wait_ge(gam[0], 1)
            g.partition_all_reduce(ggall[:, 0], gg[:, 0], P, RMAX).then_inc(gam_all[0], 1)
            pool.wait_ge(gam[1], 1)
            g.partition_all_reduce(ggall[:, 1], gg[:, 1], P, RMAX).then_inc(gam_all[1], 1)
            g.memset(stack[:, :, :, :, SPLIT:MAXCOL], 0.0).then_inc(setup_pool, 1)
            pool.wait_ge(setup_pool, 14)

            def parts(own, src, left, part, ready):
                own.link(g.tensor_copy(part(0), src))
                own.link(g.tensor_tensor(left, src, part(0), ALU.subtract))
                yield
                own.link(g.tensor_copy(part(1), left))
                g.tensor_tensor(part(2), left, part(1), ALU.subtract).then_inc(ready, 1)

            def offsets_c(i):
                w = waits(pool, "c_", i)
                own = Own(pool, "pool_parts")
                yield
                w("var", 1)
                power("p", "c_rstd")
                yield
                yield
                w("xn_out", 0)
                w("xn", 1)
                settle(pool, "pool")
                yield from parts(own, f_xn[:], xnr[:], lambda k: xnp[:, k], S("c_xnp"))
                yield
                yield
                w("cvar", 1)
                power("p", "c_crstd")
                for _ in range(5):
                    yield
                w("hat_out", 0)
                w("hat", 1)
                settle(pool, "pool")
                yield from parts(own, hat[:, 0, :], hatr[:], lambda k: hatp[:, k, :], S("c_hatp"))
                yield

            def sample_c(i):
                for _ in range(8):
                    yield

            def split_c(i):
                w = waits(pool, "c_", i)
                own = Own(pool, "pool_split")
                w("k_sb", 1)
                w("q_new", 1)
                w("q2t", 0)
                settle(pool, "pool")
                yield from split(own, queries_keys(i), S("c_split"))
                yield

            def attend_c(i):
                values_in(waits(pool, "c_", i), kept(i, 3).rearrange("p t (h c) -> p t h c", c=HD), S("c_va"))
                for _ in range(16):
                    yield

            def experts_c(i):
                w = waits(pool, "c_", i)
                yield
                w("var3", 1)
                power("s", "c_rstd3")
                for _ in range(15):
                    yield

            run_pass(pool, ORDER_C, BEHIND_C, o=offsets_c, s=sample_c, k=split_c, a=attend_c, e=experts_c)

        @block.vector
        def _(dve):
            import math
            v = nc.vector
            prime(dve, "dve")
            dve.wait_ge(weights_in, 16 * len(loads))
            dve.wait_ge(setup_pool, 7)
            n = [0]

            def setup(ins):
                ins.then_inc(setup_dve, 1)
                n[0] += 1
                dve.wait_ge(setup_dve, n[0])

            setup(v.tensor_copy(identb[:], ident[:]))
            setup(v.memset(f_xnt[C:C + 1, :], 1.0))
            setup(v.memset(b_xnt[C:C + 1, :], 1.0))
            setup(v.memset(ont[C:C + 1, :], 1.0))
            setup(v.memset(gm2[:], 0.0))
            setup(v.tensor_reduce(wsum[0:C, :], w1[:, 0:GROUPS * (HID // GROUPS)].rearrange("p (g n) -> p g n", g=GROUPS), AX.X, ALU.add))
            dve.wait_ge(setup_pe, 1)
            setup(v.tensor_scalar(wmean[0:C, 0, :], ps[0:C, 0, 0:GROUPS], 1.0 / (HID // GROUPS * C), None, ALU.mult))
            gw = C // GROUPS
            w2g = w2[:, :, 0:GROUPS * gw].rearrange("p m (g n) -> p g m n", g=GROUPS)
            setup(v.tensor_reduce(wsum[:, :], w2g, AX.XY, ALU.add))
            dve.wait_ge(setup_pe, 2)
            setup(v.tensor_scalar(wmean[:, 1, :], ps[:, 0, 0:GROUPS], 1.0 / (gw * HID), None, ALU.mult))
            setup(v.memset(w1s[:], 0.0))
            setup(v.memset(w2s[:], 0.0))
            g1 = HID // GROUPS
            for g in range(GROUPS):
                v.tensor_scalar(w1s[:, g1 * g:g1 * (g + 1)], w1[:, g1 * g:g1 * (g + 1)], wmean[0:C, 0, g:g + 1], None, ALU.subtract).then_inc(setup_dve, 1)
                v.tensor_scalar(w2s[:, :, gw * g:gw * (g + 1)], w2[:, :, gw * g:gw * (g + 1)], wmean[:, 1, g:g + 1], None, ALU.subtract).then_inc(setup_dve, 1)
            n[0] += 2 * GROUPS
            setup(v.tensor_copy(bpart[:, 0, :], be2[:]))
            setup(v.tensor_tensor(bres[:], be2[:], bpart[:, 0, :], ALU.subtract))
            setup(v.tensor_copy(bpart[:, 1, :], bres[:]))
            setup(v.tensor_tensor(bpart[:, 2, :], bres[:], bpart[:, 1, :], ALU.subtract))
            dve.wait_ge(setup_act, 4)
            setup(v.tensor_scalar(ebz[:], ebz[:], 8.0, 8.0, ALU.mult, ALU.add))
            setup(v.tensor_scalar(lscale[:], lscale[:], math.log(100.0), None, ALU.min))
            setup(v.memset(xst[C:C + 1, :], 1.0))
            assert n[0] == DSETUP

            def norm(half, own, srcs, eps, ready):
                n = norms[half]
                for t in range(TILES):
                    own.mark(v.bn_stats(n["stats"][:, t, :], srcs[t]))
                own.wait(own.n)
                for t in range(TILES):
                    own.mark(v.bn_aggr(n["mv"][:, t, :], n["stats"][:, t, :]))
                own.wait(own.n)
                v.tensor_scalar(n["veps"][:], n["mv"][:, :, 1], eps, None, ALU.add).then_inc(S(ready), 1)

            def normed(half, dst, srcs):
                n = norms[half]
                for t in range(TILES):
                    ins = v.tensor_scalar(dst[:, t, :], srcs[t], n["mv"][:, t, 0:1], n["rstd"][:, t:t + 1], ALU.subtract, ALU.mult)
                return ins

            def both(v_):
                return [v_[:, t, :] for t in range(TILES)]

            def negmax_parts(own, ts):
                part = lambda k: stack[:, 0, ts, :, MAXCOL + k].rearrange("p t (b a) -> p t a b", a=2)
                own.link(v.tensor_copy(part(0), nm[:, ts]))
                own.link(v.tensor_tensor(nmr[:, ts], nm[:, ts], part(0), ALU.subtract))
                own.link(v.tensor_copy(part(1), nmr[:, ts]))
                return v.tensor_tensor(part(2), nmr[:, ts], part(1), ALU.subtract)

            def divide(own, t, bank):
                o = ps[:, bank, 0:384].rearrange("p (h c) -> p h c", c=32)
                own.link(v.reciprocal(rec[:, t, :], o[:, :, HD]))
                return v.tensor_tensor(on[:, t].rearrange("p (h c) -> p h c", c=HD), o[:, :, 0:HD],
                                       rec[:, t, :].to_broadcast([P, HEADS, HD]), ALU.mult)

            dve.wait_ge(setup_act, ASETUP)

            def project_a(i):
                w = waits(dve, "a_", i)
                own = Own(dve, "dve_first")
                w("x_in", 48)
                v.tensor_copy(kept(i), xin[:])
                norm("p", own, both(xin), 1e-6, "a_var")
                yield
                w("rstd", 1)
                normed("p", f_xn, both(xin)).then_inc(S("a_xn"), 1)
                yield
                w("sq", 2)
                own.link(v.tensor_reduce(ss[:], sq[:].rearrange("p t a h c -> p t (a h) c"), AX.X, ALU.add))
                v.tensor_scalar(ss[:], ss[:], 1e-24, None, ALU.max).then_inc(S("a_ss"), 1)
                yield
                yield

            def split_a(i):
                w = waits(dve, "a_", i)
                own = Own(dve, "dve_sample")
                w("qkv_sb", 2)
                for t in range(TILES):
                    w("rn", t + 1)
                    own.link(v.tensor_tensor(rn[:, t, 0, :], rn[:, t, 0, :], lscale[:], ALU.mult))
                w("split", 0)
                w("copies", 0)
                for t in range(TILES):
                    v.tensor_tensor(qk[:, :, t], qkv_sb[:, t, 0:2 * C].rearrange("p (a h c) -> p a h c", a=2, c=HD),
                                    rn[:, t].to_broadcast([P, 2, HEADS, HD]), ALU.mult).then_inc(S("a_qk"), 1)
                for _ in range(3):
                    yield

            def attend_a(i):
                w = waits(dve, "a_", i)
                own = Own(dve, "dve_mid")
                yield
                for t in range(TILES):
                    w("s", t + 1)
                    own.link(v.tensor_reduce(nm[:, t], ps[:, 2 + 2 * t:4 + 2 * t, 0:PAIRS * WIN].rearrange("p a (b n) -> p a b n", n=WIN),
                                             AX.X, ALU.max, negate=True))
                    negmax_parts(own, slice(t, t + 1)).then_inc(S("a_nm"), 1)
                yield
                yield
                for t in range(TILES):
                    w("exp", t + 1)
                    v.tensor_tensor(tile_probs(t), tile_probs(t), expbias[:].rearrange("p a b c -> p (a b c)"),
                                    ALU.mult).then_inc(S("a_prob"), 1)
                yield
                yield

            def finish_a(i):
                w = waits(dve, "a_", i)
                own = Own(dve, "dve_last")
                for t in range(TILES):
                    w("otr", t + 1)
                    divide(own, t, 6 + t).then_inc(S("a_on"), 1)
                yield
                yield
                w("x1_out", 0)
                w("proj", 1)
                v.tensor_tensor(xres[:], kept(i), tiles(7, C), ALU.add).then_inc(S("a_x1"), 1)
                w("x1", 1)
                norm("s", own, both(xres), 1e-5, "a_var2")
                yield
                w("rstd2", 1)
                normed("s", b_xn, both(xres)).then_inc(S("a_xn2"), 1)
                yield
                w("y1_sb", 1)
                v.tensor_reduce(gm1[:, bass.ds(i - 1, 1)], y1all[:, bass.ds(i - 1, 1)].rearrange("p a m n -> p (a m n)"),
                                AX.X, ALU.max, apply_absolute_value=True).then_inc(S("a_gm"), 1)
                yield

            run_pass(dve, ORDER_A, BEHIND_A, p=project_a, r=split_a, a=attend_a, f=finish_a)

            def gammas(n, gm, qs):
                v.tensor_reduce(gg[:, n], gm[:, 0:QIMG].rearrange("p (g n) -> p g n", n=GIMG), AX.X, ALU.max).then_inc(gam[n], 1)
                own = Own(dve, "dve_first")
                dve.wait_ge(gam_all[n], 1)
                own.link(v.tensor_scalar(gs[:, n], ggall[:, n], EPSQ, None, ALU.add))
                own.link(v.reciprocal(gs[:, n], gs[:, n]))
                own.link(v.tensor_scalar(gs[:, n], gs[:, n], QB, None, ALU.mult))
                own.link(v.memset(qs[:], 0.0))
                v.tensor_copy(qs[:, 0:QIMG].rearrange("p (g n) -> p g n", n=GIMG),
                              gs[:, n].to_broadcast([P, GROUPS, GIMG])).then_inc(gam_ready[n], 1)
                dve.wait_ge(gam_ready[n], 1)

            dve.wait_ge(S("a_gm"), IMAGES + 1)
            gammas(0, gm1, qs1)
            with dve.Fori(1, GROUPS + 1) as i:
                own = Own(dve, "dve_first")
                w = waits(dve, "b_", i)
                for u in range(GIMG):
                    img = bass.ds((i - 1) * GIMG + u, 1)
                    h0 = hb[:, u].rearrange("p m n -> p (m n)")
                    if u == 0:
                        w("y2", 0)
                    own.link(v.tensor_scalar(h0, y1all[:, img].rearrange("p a m n -> p (a m n)"), qs1[:, img], LIM, ALU.mult, ALU.min))
                    v.tensor_scalar(h0, h0, -LIM, None, ALU.max).then_inc(S("b_cl"), 1)
                for u in range(GIMG):
                    img = bass.ds((i - 1) * GIMG + u, 1)
                    w("y2_sb", u + 1)
                    v.tensor_reduce(gm2[0:C, img], y2all[:, img, :].rearrange("p a n -> p (a n)"),
                                    AX.X, ALU.max, apply_absolute_value=True).then_inc(S("b_gm"), 1)
            dve.wait_ge(S("b_gm"), (GROUPS + 1) * GIMG)
            gammas(1, gm2, qs2)

            def offsets_c(i):
                w = waits(dve, "c_", i)
                own = Own(dve, "dve_first")
                own.link(v.tensor_scalar(ycl[:], y2all[:, bass.ds(i - 1, 1), :].rearrange("p a n -> p (a n)"),
                                         qs2[0:C, bass.ds(i - 1, 1)], LIM, ALU.mult, ALU.min))
                v.tensor_scalar(ycl[:], ycl[:], -LIM, None, ALU.max).then_inc(S("c_ycl"), 1)
                yield
                w("x_in", 16)
                w("yt", 1)
                v.tensor_tensor(xin[:], xraw[:], tiles(0, C), ALU.add).then_inc(S("c_xadd"), 1)
                w("xadd", 1)
                v.tensor_copy(kept(i), xin[:])
                norm("p", own, both(xin), 1e-6, "c_var")
                yield
                w("rstd", 1)
                w("xnp", 0)
                normed("p", f_xn, both(xin)).then_inc(S("c_xn"), 1)
                yield
                yield
                yield
                yield
                w("conv", 1)
                norm("p", own, both(tiles(0, C)), 1e-3, "c_cvar")
                yield
                w("crstd", 1)
                own.link(normed("p", tn, both(tiles(0, C))))
                row = lambda x: x[:, :].rearrange("p (a c) -> p a c", a=1).to_broadcast([P, TILES, C])
                own.link(v.tensor_tensor(tn[:], tn[:], row(lng), ALU.mult))
                v.tensor_tensor(tn[:], tn[:], row(lnb), ALU.add).then_inc(S("c_cn"), 1)
                yield
                yield
                yield
                w("hatp", 0)
                w("hxt", 0)
                w("tanh", 1)
                flat = lambda x: x[:].rearrange("p a n -> p (a n)")
                own.link(v.scalar_tensor_tensor(flat(th), flat(th), SIDE / 2.0, flat(posc), ALU.mult, ALU.add))
                own.link(v.scalar_tensor_tensor(flat(hat), flat(th), -1.0, flat(th), ALU.mult, ALU.min))
                v.tensor_scalar(flat(hat), flat(hat), 1.0, 0.0, ALU.add, ALU.max).then_inc(S("c_hat"), 1)
                yield
                yield
                yield

            def sample_c(i):
                w = waits(dve, "c_", i)
                own = Own(dve, "dve_sample")
                for k in range(6):
                    t, b = k // 3, k % 3
                    if k == 0:
                        w("hatx", 1)
                    w("t3", k + 1)
                    hx = hatx[:, t, 2 * b:2 * b + 2, :].rearrange("p g c -> p (g c)")
                    v.tensor_tensor(samp[:, k % 2], ps[:, 1, :].rearrange("p (a c) -> p a c", c=GC),
                                    hx.to_broadcast([P, 2 * SIDE, GC]), ALU.mult).then_inc(S("c_mul"), 1)
                    w("mul", k + 1)
                    ins = v.tensor_reduce(xs[:, t, 2 * GC * b:2 * GC * (b + 1)].rearrange("p (g k) -> p g k", g=2),
                                          samp[:, k % 2].rearrange("p (g c) k -> p g k c", g=2), AX.X, ALU.add)
                    if k == 5:
                        ins.then_inc(S("c_xs"), 1)
                    else:
                        own.link(ins)
                    yield
                yield
                yield

            def split_c(i):
                for _ in range(3):
                    yield

            def attend_c(i):
                w = waits(dve, "c_", i)
                own = Own(dve, "dve_mid")
                yield
                for u in range(12):
                    t, pq, a = u // 6, u // 2 % 3, u % 2
                    w("s", u + 1)
                    v.tensor_reduce(nm[:, t, a, 2 * pq:2 * pq + 2], ps[:, 4 + a, :].rearrange("p (b n) -> p b n", n=TOK),
                                    AX.X, ALU.max, negate=True).then_inc(S("c_nm"), 1)
                    if a:
                        yield
                w("nm", 12)
                negmax_parts(own, slice(0, TILES)).then_inc(S("c_parts"), 1)
                yield
                for u in range(6):
                    yield
                yield
                w("ontp", 0)
                for t in range(TILES):
                    w("otr", t + 1)
                    divide(own, t, 4 + t).then_inc(S("c_on"), 1)
                yield

            def experts_c(i):
                w = waits(dve, "c_", i)
                own = Own(dve, "dve_last")
                yield
                w("proj", 1)
                w("acc", 0)
                v.tensor_tensor(xres[:], kept(i), tiles(7, C), ALU.add).then_inc(S("c_x3"), 1)
                w("x3", 1)
                norm("s", own, both(xres), 1e-5, "c_var3")
                yield
                w("rstd3", 1)
                normed("s", b_xn, both(xres)).then_inc(S("c_xn3"), 1)
                yield
                w("gate", 1)
                own.link(v.tensor_copy(sc[:], tiles(7, EXPERTS)))
                own.link(v.tensor_reduce(scm[:], sc[:], AX.X, ALU.max))
                v.tensor_tensor(sc[:], sc[:], scm[:].to_broadcast([P, TILES, EXPERTS]), ALU.subtract).then_inc(S("c_gsub"), 1)
                yield
                w("gexp", 1)
                own.link(v.tensor_reduce(scs[:], sc[:], AX.X, ALU.add))
                own.link(v.reciprocal(scs[:], scs[:]))
                own.link(v.tensor_tensor(sc[:], sc[:], scs[:].to_broadcast([P, TILES, EXPERTS]), ALU.mult))
                yield
                for t in range(TILES):
                    other = sc[:, t:t + 1, :].to_broadcast([P, EXPERTS, EXPERTS])
                    mine = sc[:, t, :].to_broadcast([P, EXPERTS, EXPERTS])
                    own.mark(v.tensor_tensor(gt[:, t], other, mine, ALU.is_gt))
                    own.mark(v.tensor_tensor(eq[:, t], other, mine, ALU.is_equal))
                own.wait(own.n)
                for t in range(TILES):
                    own.mark(v.tensor_tensor(eq[:, t], eq[:, t], tri[:], ALU.mult))
                own.wait(own.n)
                own.link(v.tensor_tensor(gt[:], gt[:], eq[:], ALU.add))
                yield
                own.link(v.tensor_reduce(eq[:, :, :, 0], gt[:], AX.X, ALU.add))
                own.link(v.tensor_scalar(eq[:, :, :, 0], eq[:, :, :, 0], 1.5, None, ALU.is_lt))
                own.link(v.tensor_tensor(sc[:], sc[:], eq[:, :, :, 0], ALU.mult))
                yield
                own.link(v.tensor_reduce(scs[:], sc[:], AX.X, ALU.add))
                own.link(v.tensor_scalar(scs[:], scs[:], 1e-9, None, ALU.add))
                own.link(v.reciprocal(scs[:], scs[:]))
                own.link(v.tensor_tensor(sc[:], sc[:], scs[:].to_broadcast([P, TILES, EXPERTS]), ALU.mult))
                for _ in range(3):
                    yield
                for half in range(2):
                    if half == 0:
                        w("out", 0)
                    w("y", half + 1)
                    for e in range(2):
                        src = acc if half or e else xres
                        for t in range(TILES):
                            ins = v.scalar_tensor_tensor(acc[:, t, :], tiles(7, 2 * C)[:, t, C * e:C * e + C],
                                                         sc[:, t, 2 * half + e:2 * half + e + 1], src[:, t, :], ALU.mult, ALU.add)
                            if e == 0:
                                own.mark(ins)
                        if e == 0:
                            own.wait(own.n)
                    ins.then_inc(S("c_acc"), 1)
                    if half == 0:
                        w("acc", 1)
                        for _ in range(5):
                            yield
                yield

            run_pass(dve, ORDER_C, BEHIND_C, o=offsets_c, s=sample_c, k=split_c, a=attend_c, e=experts_c)

        @block.scalar
        def _(act):
            a = nc.scalar
            prime(act, "act")
            n = [0]

            def setup(ins):
                ins.then_inc(setup_act, 1)
                n[0] += 1
                act.wait_ge(setup_act, n[0])

            act.wait_ge(setup_pe, 3)
            setup(a.activation(hid_t[:], ps[:, 1, 0:REL], ACT.Relu, bias=cpb_b1[:, 0:1]))
            act.wait_ge(setup_pe, 4)
            setup(a.copy(bt_sb[:], ps[0:HEADS, 2, 0:REL]))
            act.wait_ge(setup_pe, 5)
            setup(a.activation(ebz[:, 0:6], ps[:, 3, 0:384].rearrange("p (h n) -> p h n", n=WIN), ACT.Tanh, scale=0.5))
            setup(a.activation(ebz[:, 6:12], ps[:, 4, 0:384].rearrange("p (h n) -> p h n", n=WIN), ACT.Tanh, scale=0.5))
            act.wait_ge(setup_dve, DSETUP)
            setup(a.activation(expbias[:], ebz[:].rearrange("p (b a) n -> p a b n", a=2), ACT.Exp))
            setup(a.activation(lscale[:], lscale[:], ACT.Exp))
            setup(a.activation(w1s[:], w1s[:], ACT.Sign))
            setup(a.activation(w2s[:], w2s[:], ACT.Sign))

            act.wait_ge(setup_pool, 13)

            def copies(src, ready):
                for x, b in ((0, 3), (1, 2)):
                    d = stack[:, x].rearrange("p t h c -> p (t h) c")
                    one = src[:, TILES * HEADS * x:TILES * HEADS * (x + 1)]
                    a.copy(d[:, :, HD * b:HD * b + HD], one)
                    ins = a.copy(d[:, :, HD * (b + 2):HD * (b + 2) + HD], one)
                ins.then_inc(ready, 1)

            def turned(w, sig, k, x, t, bank):
                w(sig, k)
                return a.copy(stackt[:, x, :, P * t:P * t + P], bank_bf(bank))

            def project_a(i):
                w = waits(act, "a_", i)
                yield
                w("xt", 1)
                a.copy(f_xnt[0:C, :], ps[0:C, 0, 0:TOK]).then_inc(S("a_xnt"), 1)
                yield
                w("qk", 0)
                w("v", 0)
                for t in range(TILES):
                    w("qkv", t + 1)
                    a.activation(sq[:, t].rearrange("p a h c -> p (a h c)"), ps[:, t, 0:2 * C], ACT.Square).then_inc(S("a_sq"), 1)
                    a.copy(qkv_sb[:, t, :], ps[:, t, 0:3 * C]).then_inc(S("a_qkv_sb"), 1)
                yield
                yield

            def split_a(i):
                w = waits(act, "a_", i)
                w("va", 0)
                w("qkv_sb", 2)
                a.copy(v_new[:].rearrange("p t h c -> p t (h c)"), qkv_sb[:, :, 2 * C:3 * C]).then_inc(S("a_v"), 1)
                w("q2t", 0)
                w("qk", 2)
                copies(qk[:].rearrange("p a t h c -> p (a t h) c"), S("a_copies"))
                for _ in range(3):
                    yield

            def attend_a(i):
                w = waits(act, "a_", i)
                for t in range(TILES):
                    turned(w, "qt", t + 1, 0, t, 2 + 2 * t).then_inc(S("a_qt_sb"), 1)
                    turned(w, "kt", t + 1, 1, t, 3 + 2 * t).then_inc(S("a_kt_sb"), 1)
                yield
                yield
                for t in range(TILES):
                    turned(w, "q2t", t + 1, 0, t, 2 + 2 * t).then_inc(S("a_q2t_sb"), 1)
                yield
                for t in range(TILES):
                    w("st", t + 1)
                    a.activation(tile_probs(t).rearrange("p (a n) -> p a n", a=2), ps[:, 2 + 2 * t:4 + 2 * t, 0:PAIRS * WIN],
                                 ACT.Exp).then_inc(S("a_exp"), 1)
                yield
                w("pv", 1)
                w("otr", 0)
                for k in range(2):
                    ins = a.copy(ot[:].rearrange("p s (t w n) -> p t s w n", t=TILES, w=2)[:, :, :, k, :],
                                 ps[:, 2 + k, 0:TILES * 3 * WIN].rearrange("p (t s n) -> p t s n", t=TILES, n=WIN))
                ins.then_inc(S("a_ot"), 1)
                yield

            def finish_a(i):
                w = waits(act, "a_", i)
                yield
                w("ontp", 1)
                a.copy(ont[0:C, :], ps[0:C, 6, 0:TOK]).then_inc(S("a_ont"), 1)
                yield
                yield
                w("x2t", 1)
                a.copy(b_xnt[0:C, :], ps[0:C, 6, 0:TOK]).then_inc(S("a_x2t_sb"), 1)
                yield
                w("y1", 1)
                for m in range(MT):
                    ins = a.activation(y1all[:, bass.ds(i - 1, 1), m, :].rearrange("p a n -> p (a n)"),
                                       ps[:, 6 + m // 2, TOK * (m % 2):TOK * (m % 2) + TOK], ACT.Identity, bias=b1[:, m:m + 1])
                ins.then_inc(S("a_y1_sb"), 1)
                yield

            run_pass(act, ORDER_A, BEHIND_A, p=project_a, r=split_a, a=attend_a, f=finish_a)

            with act.Fori(1, GROUPS + 1) as i:
                w = waits(act, "b_", i)
                k = SHIFT * SIDE
                for u in range(GIMG):
                    h0 = hb[:, u].rearrange("p m n -> p (m n)")
                    w("cl", u + 1)
                    a.activation(h0, h0, ACT.Gelu).then_inc(S("b_h"), 1)
                for u in range(GIMG):
                    img = bass.ds((i - 1) * GIMG + u, 1)
                    w("y2", u + 1)
                    a.activation(y2all[:, img, k:TOK].rearrange("p a n -> p (a n)"), ps[0:C, u, 0:TOK - k], ACT.Identity, bias=b2[:, 0:1])
                    a.activation(y2all[:, img, 0:k].rearrange("p a n -> p (a n)"), ps[0:C, u, TOK - k:TOK], ACT.Identity,
                                 bias=b2[:, 0:1]).then_inc(S("b_y2_sb"), 1)

            def offsets_c(i):
                w = waits(act, "c_", i)
                yield
                yield
                w("xt", 1)
                a.copy(f_xnt[0:C, :], ps[0:C, 0, 0:TOK]).then_inc(S("c_xnt"), 1)
                yield
                w("qc", 1)
                w("q", 1)
                qc = ps[0:C, 0, 0:TOK].rearrange("p (r c) -> p r c", c=SIDE)
                a.copy(qpad[:, 0, 1:1 + SIDE, 1:SIDE], qc[:, :, 0:SIDE - 1])
                a.copy(qpad[:, 1, 1:1 + SIDE, :], qc)
                a.copy(qpad[:, 2, 1:1 + SIDE, 0:SIDE - 1], qc[:, :, 1:SIDE]).then_inc(S("c_qpad"), 1)
                a.copy(kept(i, 1), ps[:, 0, TOK:TOK + TILES * C].rearrange("p (t c) -> p t c", c=C)).then_inc(S("c_q_new"), 1)
                yield
                yield
                yield
                yield
                w("cn", 1)
                a.activation(tn[:], tn[:], ACT.Gelu).then_inc(S("c_cg"), 1)
                yield
                w("tt", 1)
                a.copy(tnt[:, :], ps[0:C, 0, 0:TOK]).then_inc(S("c_tnt"), 1)
                yield
                w("offs", 1)
                a.activation(th[:].rearrange("p a n -> p (a n)"), ps[0:C, 0, :], ACT.Tanh).then_inc(S("c_tanh"), 1)
                yield
                w("mul", 0)
                w("hxt", 1)
                a.copy(hatx[:].rearrange("p t g c -> p (t g c)"), ps[:, 0, 0:2 * C]).then_inc(S("c_hatx"), 1)
                yield
                yield
                yield

            def sample_c(i):
                w = waits(act, "c_", i)
                for _ in range(6):
                    yield
                w("xst", 1)
                a.copy(xst[0:C, :], ps[0:C, 1, 0:TOK]).then_inc(S("c_xst_sb"), 1)
                yield
                w("kv", 1)
                kv = tiles(1, 2 * C)
                a.copy(kept(i, 2), kv[:, :, 0:C]).then_inc(S("c_k_sb"), 1)
                a.copy(kept(i, 3), kv[:, :, C:2 * C]).then_inc(S("c_v"), 1)
                yield

            def split_c(i):
                w = waits(act, "c_", i)
                w("q2t", 0)
                w("q_new", 1)
                w("k_sb", 1)
                copies(queries_keys(i), S("c_copies"))
                for _ in range(3):
                    yield

            def attend_c(i):
                w = waits(act, "c_", i)
                for t in range(TILES):
                    turned(w, "qt", t + 1, 0, t, 2 + 2 * t).then_inc(S("c_qt_sb"), 1)
                    turned(w, "kt", t + 1, 1, t, 3 + 2 * t).then_inc(S("c_kt_sb"), 1)
                yield
                for u in range(6):
                    yield
                for t in range(TILES):
                    turned(w, "q2t", t + 1, 0, t, 2 + t).then_inc(S("c_q2t_sb"), 1)
                yield
                for u in range(12):
                    w("st", u + 1)
                    if u >= 4:
                        w("pv", u - 3)
                    a.activation(prob[:, u % 4].rearrange("p b n -> p (b n)"), ps[:, 4 + u % 2, :], ACT.Exp,
                                 scale=float(HD) ** -0.5).then_inc(S("c_exp"), 1)
                    if u % 2:
                        yield
                for s in range(3):
                    w("pv", (8, 8, 12)[s])
                    a.copy(ot[:, s, :], ps[:, 2 + s // 2, TOK * (s % 2):TOK * (s % 2) + TOK]).then_inc(S("c_ot"), 1)
                yield
                yield

            def experts_c(i):
                w = waits(act, "c_", i)
                w("ontp", 1)
                a.copy(ont[0:C, :], ps[0:C, 6, 0:TOK]).then_inc(S("c_ont"), 1)
                yield
                yield
                yield
                w("x3t", 1)
                a.copy(b_xnt[0:C, :], ps[0:C, 6, 0:TOK]).then_inc(S("c_x3t_sb"), 1)
                w("gsub", 1)
                a.activation(sc[:], sc[:], ACT.Exp).then_inc(S("c_gexp"), 1)
                yield
                for e in range(EXPERTS):
                    for k in range(2):
                        n_ = (2, 1)[k] * TOK
                        w("h1", 2 * e + k + 1)
                        a.activation(hb[:, e % 2].rearrange("p m n -> p (m n)")[:, 2 * TOK * k:2 * TOK * k + n_], ps[:, 6, 0:n_],
                                     ACT.Gelu).then_inc(S("c_h"), 1)
                        yield
                        if e and k == 0:
                            yield
                yield

            run_pass(act, ORDER_C, BEHIND_C, o=offsets_c, s=sample_c, k=split_c, a=attend_c, e=experts_c)

        @block.tensor
        def _(pe):
            m = nc.tensor
            prime(pe, "pe")

            def mm(o, l, r, start=True, stop=True):
                return m.matmul(o, l, r, start=start, stop=stop)

            def turn(bank, x, t):
                for b in range(PAIRS):
                    ins = m.transpose(bank_bf(bank)[:, b, :], stack[:, x, t].rearrange("p h c -> p (h c)")[:, P * b:P * b + P], identb[:])
                return ins

            def cols(t):
                return slice(P * t, P * t + P)

            pe.wait_ge(weights_in, 16 * len(loads))
            pe.wait_ge(setup_pool, 7)
            pe.wait_ge(setup_dve, 6)
            mm(ps[0:C, 0, 0:GROUPS], onesm[0:C, 0:C], wsum[0:C, :]).then_inc(setup_pe, 1)
            pe.wait_ge(setup_dve, 8)
            mm(ps[:, 0, 0:GROUPS], onesm[:, :], wsum[:, :]).then_inc(setup_pe, 1)
            mm(ps[:, 1, 0:REL], cpb_w1[:], table[:]).then_inc(setup_pe, 1)
            pe.wait_ge(setup_act, 1)
            mm(ps[0:HEADS, 2, 0:REL], cpb_w2[:], hid_t[:]).then_inc(setup_pe, 1)
            pe.wait_ge(bt_dma, 16 * 9)
            for b in range(2):
                ins = mm(ps[:, 3 + b, 0:384], flip[:], ebraw[:, 6 * b:6 * b + 6, :].rearrange("p h (r c) -> p h r c", c=15)[:, :, :, 0:8])
            ins.then_inc(setup_pe, 1)
            pe.wait_ge(setup_act, ASETUP)
            pe.wait_ge(setup_dve, DSETUP)
            pe.wait_ge(setup_pool, 13)
            pe.wait_ge(bias_dma, 144)

            def window(t, k):
                return slice(P * t + WIN * k, P * t + WIN * k + WIN)

            def project_a(i):
                w = waits(pe, "a_", i)
                yield
                w("qkv_sb", 0)
                w("xn", 1)
                for t in range(TILES):
                    ins = mm(ps[0:C, 0, cols(t)], f_xn[:, t, :], perm_in[:])
                ins.then_inc(S("a_xt"), 1)
                yield
                w("xnt", 1)
                for t in range(TILES):
                    mm(ps[:, t, 0:3 * C], f_xnt[:, cols(t)], wqkv[:]).then_inc(S("a_qkv"), 1)
                yield
                yield

            def split_a(i):
                for _ in range(3):
                    yield

            def attend_a(i):
                w = waits(pe, "a_", i)
                w("split", 1)
                w("copies", 1)
                w("ot", 0)
                for t in range(TILES):
                    turn(2 + 2 * t, 0, t).then_inc(S("a_qt"), 1)
                    turn(3 + 2 * t, 1, t).then_inc(S("a_kt"), 1)
                yield
                for t in range(TILES):
                    w("qt_sb", t + 1)
                    w("kt_sb", t + 1)
                    settle(pe, "pe")
                    for h in range(HEADS):
                        b, a = h // 2, h % 2
                        r = slice(SLOT * a, SLOT * a + MAXCOL)
                        for k in range(2):
                            ins = mm(ps[WIN * k:WIN * k + WIN, 2 + 2 * t + a, WIN * b:WIN * b + WIN],
                                     stackt[r, 0, b, window(t, k)], stackt[r, 1, b, window(t, k)])
                    ins.then_inc(S("a_s"), 1)
                yield
                for t in range(TILES):
                    w("nm", t + 1)
                    turn(2 + 2 * t, 0, t).then_inc(S("a_q2t"), 1)
                yield
                for t in range(TILES):
                    w("q2t_sb", t + 1)
                    settle(pe, "pe")
                    for h in range(HEADS):
                        b, a = h // 2, h % 2
                        r = slice(SLOT * a, SLOT * a + FULL)
                        for k in range(2):
                            ins = mm(ps[WIN * k:WIN * k + WIN, 2 + 2 * t + a, WIN * b:WIN * b + WIN],
                                     stackt[r, 1, b, window(t, k)], stackt[r, 0, b, window(t, k)])
                    ins.then_inc(S("a_st"), 1)
                yield
                w("va", 1)
                for t in range(TILES):
                    w("prob", t + 1)
                    settle(pe, "pe")
                    for h in range(HEADS):
                        for k in range(2):
                            at = (h % 2) * PAIRS * WIN + (h // 2) * WIN
                            to = (3 * t + h // 4) * WIN
                            r = slice(WIN * k, WIN * k + WIN)
                            ins = mm(ps[32 * (h % 4):32 * (h % 4) + 32, 2 + k, to:to + WIN], va[r, t, h, :], tile_probs(t)[r, at:at + WIN])
                ins.then_inc(S("a_pv"), 1)
                yield

            def finish_a(i):
                w = waits(pe, "a_", i)
                w("y1_sb", 0)
                w("ot", 1)
                for t in range(TILES):
                    for s in range(3):
                        ins = m.transpose(ps[:, 6 + t, cols(s)], ot[:, s, cols(t)], ident[:])
                    ins.then_inc(S("a_otr"), 1)
                yield
                w("on", 2)
                for t in range(TILES):
                    ins = mm(ps[0:C, 6, cols(t)], on[:, t, :], perm_out[:])
                ins.then_inc(S("a_ontp"), 1)
                yield
                w("ont", 1)
                for t in range(TILES):
                    ins = mm(tiles(7, C)[:, t, :], ont[:, cols(t)], wproj[:])
                ins.then_inc(S("a_proj"), 1)
                yield
                w("xn2", 1)
                for t in range(TILES):
                    ins = m.transpose(ps[0:C, 6, cols(t)], b_xn[:, t, :], ident[:])
                ins.then_inc(S("a_x2t"), 1)
                yield
                w("x2t_sb", 1)
                for k in range(MT):
                    ins = mm(ps[:, 6 + k // 2, TOK * (k % 2):TOK * (k % 2) + TOK], w1s[:, cols(k)], b_xnt[0:C, :])
                ins.then_inc(S("a_y1"), 1)
                yield

            run_pass(pe, ORDER_A, BEHIND_A, p=project_a, r=split_a, a=attend_a, f=finish_a)

            with pe.Fori(1, GROUPS + 1) as i:
                w = waits(pe, "b_", i)
                w("y2_sb", 0)
                for u in range(GIMG):
                    w("h", u + 1)
                    for k in range(MT):
                        ins = mm(ps[0:C, u, 0:TOK], w2s[:, k, :], hb[:, u, k, :], k == 0, k == MT - 1)
                    ins.then_inc(S("b_y2"), 1)

            pe.wait_ge(S("b_y2_sb"), (GROUPS + 1) * GIMG)

            def offsets_c(i):
                w = waits(pe, "c_", i)
                w("hatx", 0)
                w("ycl", 1)
                for t in range(TILES):
                    ins = m.transpose(tiles(0, C)[:, t, :], ycl[:, cols(t)], ident[0:C, 0:C])
                ins.then_inc(S("c_yt"), 1)
                yield
                yield
                w("xn", 1)
                for t in range(TILES):
                    ins = m.transpose(ps[0:C, 0, cols(t)], f_xn[:, t, :], ident[:])
                ins.then_inc(S("c_xt"), 1)
                yield
                w("xnt", 1)
                mm(ps[0:C, 0, 0:TOK], wq[:], f_xnt[:]).then_inc(S("c_qc"), 1)
                for t in range(TILES):
                    ins = mm(ps[:, 0, TOK + C * t:TOK + C * t + C], f_xnt[:, cols(t)], wq[:])
                ins.then_inc(S("c_q"), 1)
                yield
                w("qpad", 1)
                w("q_new", 1)
                for t in range(TILES):
                    o = tiles(0, C)[:, t, :]
                    for k in range(9):
                        r0 = 8 * t + k // 3
                        mm(o, qpad[:, k % 3, r0:r0 + 8, :].rearrange("p r c -> p (r c)"), wconv[:, k, :], k == 0, False)
                    ins = mm(o, onesb[:], cbias3[:], False, True)
                    if t == 0:
                        yield
                ins.then_inc(S("c_conv"), 1)
                yield
                yield
                yield
                w("cg", 1)
                for t in range(TILES):
                    ins = m.transpose(ps[0:C, 0, cols(t)], tn[:, t, :], ident[:])
                ins.then_inc(S("c_tt"), 1)
                yield
                w("tnt", 1)
                for k in range(2):
                    ins = mm(ps[0:C, 0, TOK * k:TOK * k + TOK], woffp[:, k, :], tnt[:])
                ins.then_inc(S("c_offs"), 1)
                yield
                w("hat", 1)
                for t in range(TILES):
                    ins = m.transpose(tiles(0, C)[:, t, :], hat[:, 1, cols(t)], ident[0:C, 0:C])
                ins.then_inc(S("c_hxt"), 1)
                yield
                yield
                yield

            def sample_c(i):
                w = waits(pe, "c_", i)
                w("v", 0)
                w("rows_in", 96)
                w("hat_in", 96)
                for k in range(6):
                    t, b = k // 3, k % 3
                    if k >= 1:
                        w("mul", k)
                    for g in (2 * b, 2 * b + 1):
                        ins = mm(ps[:, 1, TOK * (g % 2):TOK * (g % 2) + TOK], hatst[:, g, cols(t)], rows[:, :, GC * g:GC * g + GC])
                    ins.then_inc(S("c_t3"), 1)
                    yield
                w("xs", 1)
                for t in range(TILES):
                    ins = m.transpose(ps[0:C, 1, cols(t)], xs[:, t, :], ident[:])
                ins.then_inc(S("c_xst"), 1)
                yield
                w("xst_sb", 1)
                for t in range(TILES):
                    ins = mm(tiles(1, 2 * C)[:, t, :], xst[:, cols(t)], wkv[:])
                ins.then_inc(S("c_kv"), 1)
                yield

            def split_c(i):
                for _ in range(3):
                    yield

            def attend_c(i):
                w = waits(pe, "c_", i)
                w("split", 1)
                w("copies", 1)
                w("ot", 0)
                w("on", 0)
                for t in range(TILES):
                    turn(2 + 2 * t, 0, t).then_inc(S("c_qt"), 1)
                    turn(3 + 2 * t, 1, t).then_inc(S("c_kt"), 1)
                yield
                w("qt_sb", 2)
                w("kt_sb", 2)
                for u in range(12):
                    t, pq, a = u // 6, u // 2 % 3, u % 2
                    if u >= 2:
                        w("nm", u - 1)
                    r = slice(SLOT * a, SLOT * a + SPLIT)
                    for b in range(2):
                        ins = mm(ps[:, 4 + a, TOK * b:TOK * b + TOK],
                                 stackt[r, 0, 2 * pq + b, cols(t)], stackt[r, 1, 2 * pq + b, :])
                    ins.then_inc(S("c_s"), 1)
                    if a:
                        yield
                w("parts", 1)
                for t in range(TILES):
                    turn(2 + t, 0, t).then_inc(S("c_q2t"), 1)
                yield
                w("q2t_sb", 2)
                w("va", 1)

                def values(u):
                    pq, k, a = u // 4, u // 2 % 2, u % 2
                    w("exp", u + 1)
                    for b in range(2):
                        h = 2 * b + a
                        ins = mm(ps[32 * h:32 * h + 32, 2 + pq // 2, TOK * (pq % 2):TOK * (pq % 2) + TOK],
                                 va[:, k, 4 * pq + h, :], prob[:, u % 4, b, :], k == 0, k == 1)
                    ins.then_inc(S("c_pv"), 1)

                for u in range(12):
                    pq, k, a = u // 4, u // 2 % 2, u % 2
                    if u >= 2:
                        w("exp", u - 1)
                    r = slice(SLOT * a, SLOT * a + FULL)
                    for b in range(2):
                        ins = mm(ps[:, 4 + a, TOK * b:TOK * b + TOK],
                                 stackt[r, 1, 2 * pq + b, cols(k)], stackt[r, 0, 2 * pq + b, :])
                    ins.then_inc(S("c_st"), 1)
                    if u >= 2:
                        values(u - 2)
                    if a:
                        yield
                values(10)
                values(11)
                yield
                w("ot", 3)
                for t in range(TILES):
                    for s in range(3):
                        ins = m.transpose(ps[:, 4 + t, cols(s)], ot[:, s, cols(t)], ident[:])
                    ins.then_inc(S("c_otr"), 1)
                yield

            def experts_c(i):
                w = waits(pe, "c_", i)
                w("acc", 0)
                w("on", 2)
                for t in range(TILES):
                    ins = m.transpose(ps[0:C, 6, cols(t)], on[:, t, :], ident[:])
                ins.then_inc(S("c_ontp"), 1)
                yield
                w("ont", 1)
                for t in range(TILES):
                    ins = mm(tiles(7, C)[:, t, :], ont[:, cols(t)], wo[:])
                ins.then_inc(S("c_proj"), 1)
                yield
                w("xn3", 1)
                for t in range(TILES):
                    ins = m.transpose(ps[0:C, 6, cols(t)], b_xn[:, t, :], ident[:])
                ins.then_inc(S("c_x3t"), 1)
                yield
                w("x3t_sb", 1)
                for t in range(TILES):
                    ins = mm(tiles(7, EXPERTS)[:, t, :], b_xnt[:, cols(t)], wg[:])
                ins.then_inc(S("c_gate"), 1)
                yield

                def up(e, k):
                    if e or k:
                        w("h", 2 * e + k)
                    for m_ in (0, 1) if k == 0 else (2,):
                        ins = mm(ps[:, 6, TOK * (m_ % 2):TOK * (m_ % 2) + TOK], we1[:, e, cols(m_)], b_xnt[:])
                    ins.then_inc(S("c_h1"), 1)

                def down(e):
                    if e % 2 == 0:
                        w(*(("gsub", 1), ("acc", 1))[e // 2])
                        mm(ps[:, 7, 0:TILES * 2 * C], onesb[:], bias3[:, e // 2].rearrange("p t n -> p (t n)"), True, False)
                    w("h", 2 * e + 2)
                    for t in range(TILES):
                        for k in range(MT):
                            ins = mm(tiles(7, 2 * C)[:, t, C * (e % 2):C * (e % 2) + C], hb[:, e % 2, k, cols(t)], we2[:, e, k, :],
                                     False, t == TILES - 1 and k == MT - 1 and e % 2 == 1)
                    if e % 2:
                        ins.then_inc(S("c_y"), 1)

                up(0, 0)
                yield
                up(0, 1)
                yield
                for e in range(1, EXPERTS):
                    up(e, 0)
                    yield
                    down(e - 1)
                    yield
                    up(e, 1)
                    yield
                down(EXPERTS - 1)
                yield

            run_pass(pe, ORDER_C, BEHIND_C, o=offsets_c, s=sample_c, k=split_c, a=attend_c, e=experts_c)


def _constants():
    import numpy as np

    c = {}
    c["ident"] = np.eye(P, dtype=np.float32)
    perm = np.zeros((P, P), np.float32)
    for w in range(2):
        for r in range(8):
            for q in range(8):
                perm[r * SIDE + (SHIFT + 8 * w + q) % SIDE, w * WIN + r * 8 + q] = 1
    c["perm_in"] = perm
    c["perm_out"] = np.ascontiguousarray(perm.T)
    flip = np.zeros((WIN, P), np.float32)
    for j in range(WIN):
        flip[WIN - 1 - j, j] = flip[WIN - 1 - j, WIN + j] = 1
    c["flip"] = flip
    mq = np.zeros((P, TILES, MASKROWS), np.float32)
    mk = np.zeros((P, TILES, MASKROWS), np.float32)
    for t in range(TILES):
        for w in range(2):
            for r in range(8):
                for q in range(8):
                    p = w * WIN + r * 8 + q
                    cl = 2 * (t == 1 and r >= 4) + (w == 1 and q >= 4)
                    mq[p, t, 0], mk[p, t, 0] = 1, -100
                    mq[p, t, 1 + cl], mk[p, t, 1 + cl] = 1, 100
    c["mask_q"], c["mask_k"] = mq, mk
    d = np.arange(-7, 8, dtype=np.float32)
    tb = np.stack(np.meshgrid(d, d, indexing="ij"), axis=-1) / np.float32(7) * np.float32(8)
    tb = np.sign(tb) * np.log2(np.abs(tb) + np.float32(1)) / np.float32(3)
    c["table"] = np.ascontiguousarray(tb.reshape(REL, 2).T.astype(np.float32))
    q = np.arange(TOK)
    r = np.arange(SIDE)
    y = (q % SIDE)[None, :] - r[:, None]
    x = (q // SIDE)[None, :] - r[:, None]
    c["posc"] = np.ascontiguousarray(np.tile(np.stack([y, x], 1), (DG, 1, 1)).astype(np.float32))
    c["tri"] = np.ascontiguousarray(np.broadcast_to(np.tril(np.ones((EXPERTS, EXPERTS), np.float32), -1), (P, EXPERTS, EXPERTS)))
    return c


def _layout(a):
    import numpy as np

    row = lambda v: np.asarray(v).reshape(1, -1)
    cat = lambda *v: np.ascontiguousarray(np.concatenate(v, 0))
    T = lambda v: np.ascontiguousarray(np.asarray(v).T)
    L = {"x": np.ascontiguousarray(a["x"]).reshape(IMAGES * TOK, C)}
    L["cpb_w1"] = T(a["L0_conv_cpb_w1"])
    L["cpb_b1"] = np.ascontiguousarray(a["L0_conv_cpb_b1"]).reshape(P, 1)
    L["cpb_w2"] = T(a["L0_conv_cpb_w2"])
    L["lscale"] = np.ascontiguousarray(np.broadcast_to(row(a["L0_conv_logit_scale"]), (P, HEADS)))
    qb = np.array(a["L0_conv_qkv_b"]).reshape(1, -1)
    qb[:, C:2 * C] = 0
    L["wqkv"] = cat(T(a["L0_conv_qkv_w"]), qb)
    L["wproj"] = cat(T(a["L0_conv_proj_w"]), row(a["L0_conv_proj_b"]))
    L["w1"] = T(a["L0_ffn_W1"])
    L["b1"] = T(np.asarray(a["L0_ffn_b1"]).reshape(MT, P))
    L["w2"] = np.ascontiguousarray(np.asarray(a["L0_ffn_W2"]).T.reshape(MT, P, C).transpose(1, 0, 2))
    L["b2"] = np.ascontiguousarray(a["L0_ffn_b2"]).reshape(C, 1)
    L["wq"] = cat(a["L1_conv_w_q"], row(a["L1_conv_b_q"]))
    w0 = np.asarray(a["L1_conv_w_off0"]).reshape(9, GC, C)
    wc = np.zeros((C, 9, C), w0.dtype)
    wp = np.asarray(a["L1_conv_w_offp"])
    wf = np.zeros((C, 2, C), wp.dtype)
    for g in range(DG):
        s = slice(GC * g, GC * g + GC)
        wc[s, :, s] = w0[:, :, s].transpose(1, 0, 2)
        wf[s, 0, s] = np.broadcast_to(wp[:, 0:1], (GC, SIDE))
        wf[s, 1, s] = np.broadcast_to(wp[:, 1:2], (GC, SIDE))
    L["wconv"], L["woffp"] = wc, wf
    L["lng"] = np.ascontiguousarray(np.broadcast_to(row(a["L1_conv_ln_g"]), (P, C)))
    L["lnb"] = np.ascontiguousarray(np.broadcast_to(row(a["L1_conv_ln_b"]), (P, C)))
    L["wkv"] = cat(np.concatenate([a["L1_conv_w_k"], a["L1_conv_w_v"]], 1),
                   np.concatenate([row(a["L1_conv_b_k"]), row(a["L1_conv_b_v"])], 1))
    L["wo"] = cat(a["L1_conv_w_o"], row(a["L1_conv_b_o"]))
    L["wg"] = cat(a["L1_ffn_gate_w"], row(a["L1_ffn_gate_b"]))
    w1 = np.asarray(a["L1_ffn_w1"]).transpose(1, 0, 2)
    L["we1"] = cat(w1, np.asarray(a["L1_ffn_b1"]).reshape(1, EXPERTS, HID))
    L["we2"] = np.ascontiguousarray(np.asarray(a["L1_ffn_w2"]).reshape(EXPERTS, MT, P, C).transpose(2, 0, 1, 3))
    L["be2"] = np.ascontiguousarray(np.concatenate([row(a["L1_ffn_b2"]), row(a["L1_conv_b_off0"])], 1))
    return L


def kernel(**inputs):
    import numpy as _np
    import concourse.bacc as _bacc
    from concourse import mybir as _mybir
    from concourse.bass_utils import run_bass_kernel_spmd as _run

    nc = _bacc.Bacc("TRN2", target_bir_lowering=False, num_devices=1)
    given = {**_layout(inputs), **_constants()}
    arrays, aps = {}, {}
    for name, a in given.items():
        a = _np.ascontiguousarray(a)
        arrays[f"in_{name}"] = a
        aps[name] = nc.dram_tensor(f"in_{name}", a.shape, _mybir.dt.from_np(a.dtype), kind="ExternalInput").ap()
    out = nc.dram_tensor("out_0", (IMAGES * TOK, C), _mybir.dt.float32, kind="ExternalOutput").ap()
    build_program(nc, aps, out)
    r = _run(nc, [arrays], core_ids=[0])
    return _np.asarray(r.results[0]["out_0"]).reshape(IMAGES, SIDE, SIDE, C)
```
